# Optimizing a Trainium2 kernel written in Bass

```python
import numpy as np
import jax
import jax.numpy as jnp

def _softmax(x, axis=-1):
    return jax.nn.softmax(x, axis=axis)

def _gelu(x):
    return jax.nn.gelu(x, approximate=True)

def _silu(x):
    return jax.nn.silu(x)

def _sigmoid(x):
    return jax.nn.sigmoid(x)

def _layernorm(x, axis=-1, eps=1e-05):
    m = jnp.mean(x, axis=axis, keepdims=True)
    v = jnp.var(x, axis=axis, keepdims=True)
    return (x - m) / jnp.sqrt(v + eps)

def _scatter_add(tgt, idx, src, axis=0):
    return tgt.at[idx].add(src)

def _segment_sum(src, seg, n):
    return jax.ops.segment_sum(src, seg, n)
kernel_name = 'mk_decoder_postln_d2_seqx_r8_4a923c'

def setup_inputs(seed: int=0):
    np.random.seed(seed)
    _w = jnp.asarray

    def _rec_inputs():
        import jax
        import jax.numpy as jnp
        _rk = jax.random.key(seed)
        x = 7.22e-05 + 1 * jax.random.normal(jax.random.fold_in(_rk, 1), (16, 128, 128), jnp.float32)
        _lenS = 128 - jax.random.randint(jax.random.fold_in(_rk, 7), (16,), 0, max(1, 128 // 4) + 1, jnp.int32)
        _lenS2 = 77 - jax.random.randint(jax.random.fold_in(_rk, 8), (16,), 0, max(1, 77 // 4) + 1, jnp.int32)
        _ctx_1024P = jax.random.normal(jax.random.fold_in(_rk, 11), (16, 16, 128), jnp.float32)
        _ctx_1024c = jax.random.dirichlet(jax.random.fold_in(_rk, 511), 0.3 * jnp.ones((16,), jnp.float32), (16, 77))
        _ctx_1024t = jnp.einsum('bsk,bkd->bsd', _ctx_1024c, _ctx_1024P)
        _ctx_1024t = _ctx_1024t * jax.lax.rsqrt(jnp.mean(jnp.square(_ctx_1024t)) + 1e-12) * 0.953939
        ctx_1024 = -0.000514642 + 1.00011 * (_ctx_1024t + 0.3 * jax.random.normal(jax.random.fold_in(_rk, 611), (16, 77, 128), jnp.float32))
        _validS = jnp.arange(128)[None, :] < _lenS[:, None]
        _validS2 = jnp.arange(77)[None, :] < _lenS2[:, None]
        _causal = jnp.tril(jnp.ones((128, 128), dtype=bool))
        mask_1x1xSxS2_bk1 = jnp.broadcast_to(_validS2[0:1, None, None, :], (1, 1, 128, 77))
        return (x, ctx_1024, mask_1x1xSxS2_bk1)
    x, ctx_1024, mask_1x1xSxS2_bk1 = _rec_inputs()

    def _L0_attn_setup():
        import jax, jax.numpy as jnp
        import numpy as np
        DIM = 128
        D_STATE = 16
        D_CONV = 4
        D_INNER = 2 * DIM
        DT_RANK = (DIM + 15) // 16
        E = 8
        K = 2
        HID = 4 * DIM
        B, L = (1, 256)

        def _rmsnorm(x):
            n = jnp.sqrt(jnp.sum(x * x, axis=-1, keepdims=True))
            return x * DIM ** 0.5 / jnp.maximum(n, 1e-12)

        def _selective_scan(u, A_log, D, x_proj_w, dt_proj_w, dt_proj_b):
            A = -jnp.exp(A_log)
            x_dbl = u @ x_proj_w.T
            dt, Bm, Cm = jnp.split(x_dbl, [DT_RANK, DT_RANK + D_STATE], axis=-1)
            delta = jax.nn.softplus(dt @ dt_proj_w.T + dt_proj_b)
            dA = jnp.exp(delta[..., None] * A)
            dBu = delta[..., None] * Bm[:, :, None, :] * u[..., None]

            def step(h, inp):
                dA_t, dBu_t, C_t = inp
                h = dA_t * h + dBu_t
                y = jnp.einsum('bdn,bn->bd', h, C_t)
                return (h, y)
            h0 = jnp.zeros((u.shape[0], D_INNER, D_STATE), u.dtype)
            _, ys = jax.lax.scan(step, h0, (dA.swapaxes(0, 1), dBu.swapaxes(0, 1), Cm.swapaxes(0, 1)))
            y = ys.swapaxes(0, 1)
            return y + u * D

        def _mamba(xn, in_proj_w, conv_w, conv_b, x_proj_w, dt_proj_w, dt_proj_b, A_log, D, out_proj_w):
            xr = xn @ in_proj_w.T
            xm, res = jnp.split(xr, 2, axis=-1)
            xc = jax.lax.conv_general_dilated(xm.swapaxes(1, 2), conv_w, (1,), [(D_CONV - 1, 0)], feature_group_count=D_INNER) + conv_b[:, None]
            xc = jax.nn.silu(xc.swapaxes(1, 2))
            y = _selective_scan(xc, A_log, D, x_proj_w, dt_proj_w, dt_proj_b)
            y = y * jax.nn.silu(res)
            return y @ out_proj_w.T

        def _moe(x, gate_w, w1, w2):
            gates = jax.nn.softmax(x @ gate_w.T, axis=-1)
            vals, idx = jax.lax.top_k(gates, K)
            vals = vals / jnp.sum(vals, axis=-1, keepdims=True)
            sparse = jnp.sum(jax.nn.one_hot(idx, E, dtype=x.dtype) * vals[..., None], axis=-2)
            h = jax.nn.gelu(jnp.einsum('bld,ehd->bleh', x, w1), approximate=False)
            y = jnp.einsum('bleh,edh->bled', h, w2)
            return jnp.einsum('bled,ble->bld', y, sparse)
        key = jax.random.key(seed)
        ks = jax.random.split(key, 12)
        g = lambda k, shape, s: jax.random.normal(k, shape, jnp.float32) * s
        A_log = jnp.log(jnp.tile(jnp.arange(1, D_STATE + 1, dtype=jnp.float32), (D_INNER, 1)))
        return {'x': g(ks[0], (B, L, DIM), 1.0), 'in_proj_w': g(ks[1], (2 * D_INNER, DIM), 0.02), 'conv_w': g(ks[2], (D_INNER, 1, D_CONV), 0.1), 'conv_b': jnp.zeros((D_INNER,), jnp.float32), 'x_proj_w': g(ks[3], (DT_RANK + 2 * D_STATE, D_INNER), 0.02), 'dt_proj_w': g(ks[4], (D_INNER, DT_RANK), 0.02), 'dt_proj_b': g(ks[5], (D_INNER,), 0.1), 'A_log': A_log, 'D': jnp.ones((D_INNER,), jnp.float32), 'out_proj_w': g(ks[6], (DIM, D_INNER), 0.02), 'gate_w': g(ks[7], (E, DIM), 0.02), 'w1': g(ks[8], (E, HID, DIM), 0.02), 'w2': g(ks[9], (E, DIM, HID), 0.02)}
    _L0_attn_all = _L0_attn_setup()
    _L0_attn_in = {k: v for k, v in _L0_attn_all.items() if k in ('in_proj_w', 'conv_w', 'conv_b', 'x_proj_w', 'dt_proj_w', 'dt_proj_b', 'A_log', 'D', 'out_proj_w', 'gate_w', 'w1', 'w2')}
    del _L0_attn_all

    def _L0_xattn_setup():
        import jax, jax.numpy as jnp
        import numpy as np
        import math
        H = 16

        def _split_heads(x):
            b, n, hd = x.shape
            return x.reshape(b, n, H, hd // H).transpose(0, 2, 1, 3)
        key = jax.random.key(seed)
        ks = jax.random.split(key, 5)
        D = 128
        s = 1.0 / math.sqrt(D)
        return {'hidden_states': jax.random.normal(ks[0], (8, 128, D), dtype=jnp.float32), 'context_states': jax.random.normal(ks[1], (8, 32, D), dtype=jnp.float32), 'Wq': jax.random.normal(ks[2], (D, D), dtype=jnp.float32) * s, 'bq': jnp.zeros((D,), dtype=jnp.float32), 'Wk': jax.random.normal(ks[3], (D, D), dtype=jnp.float32) * s, 'bk': jnp.zeros((D,), dtype=jnp.float32), 'Wv': jax.random.normal(ks[4], (D, D), dtype=jnp.float32) * s, 'bv': jnp.zeros((D,), dtype=jnp.float32)}
    _L0_xattn_all = _L0_xattn_setup()
    _L0_xattn_in = {k: v for k, v in _L0_xattn_all.items() if k in ('Wq', 'bq', 'Wk', 'bk', 'Wv', 'bv')}
    del _L0_xattn_all

    def _L0_ffn_setup():
        import jax, jax.numpy as jnp
        import numpy as np
        import math
        DIM = 128
        NUM_HEADS = 16
        SHARED_HEADS = 1
        ROUTED_HEADS = 3
        HEAD_DIM = DIM // NUM_HEADS
        B, N = (2, 256)
        key = jax.random.key(seed)
        ks = jax.random.split(key, 16)
        s = 1.0 / math.sqrt(DIM)
        inp = {'x': jax.random.normal(ks[0], (B, N, DIM), dtype=jnp.float32), 'Wq': jax.random.uniform(ks[1], (DIM, DIM), minval=-s, maxval=s), 'bq': jax.random.uniform(ks[2], (DIM,), minval=-s, maxval=s), 'Wk': jax.random.uniform(ks[3], (DIM, DIM), minval=-s, maxval=s), 'bk': jax.random.uniform(ks[4], (DIM,), minval=-s, maxval=s), 'Wv': jax.random.uniform(ks[5], (DIM, DIM), minval=-s, maxval=s), 'bv': jax.random.uniform(ks[6], (DIM,), minval=-s, maxval=s), 'Wp': jax.random.uniform(ks[7], (DIM, DIM), minval=-s, maxval=s), 'bp': jax.random.uniform(ks[8], (DIM,), minval=-s, maxval=s), 'Wr': jax.random.uniform(ks[9], (NUM_HEADS - SHARED_HEADS, DIM), minval=-s, maxval=s), 'br': jax.random.uniform(ks[10], (NUM_HEADS - SHARED_HEADS,), minval=-s, maxval=s), 'Ws': jax.random.uniform(ks[11], (2, DIM), minval=-s, maxval=s), 'bs': jax.random.uniform(ks[12], (2,), minval=-s, maxval=s), 'temperature': jnp.full((NUM_HEADS, 1, 1), float(np.log(np.expm1(1.0 / 0.24))), dtype=jnp.float32), 'query_embedding': 0.02 * jax.random.normal(ks[13], (NUM_HEADS, 1, HEAD_DIM), dtype=jnp.float32)}
        return inp
    _L0_ffn_all = _L0_ffn_setup()
    _L0_ffn_in = {k: v for k, v in _L0_ffn_all.items() if k in ('Wq', 'bq', 'Wk', 'bk', 'Wv', 'bv', 'Wp', 'bp', 'Wr', 'br', 'Ws', 'bs', 'temperature', 'query_embedding')}
    del _L0_ffn_all

    def _L1_attn_setup():
        import jax, jax.numpy as jnp
        import numpy as np
        B, L, D_MODEL = (2, 256, 128)
        D_STATE, EXPAND, D_CONV = (16, 2, 4)
        D_INNER = EXPAND * D_MODEL
        DT_RANK = D_MODEL // 16
        key = jax.random.key(seed)
        ks = jax.random.split(key, 8)
        s = lambda k, sh, sc: jax.random.normal(k, sh, dtype=jnp.float32) * sc
        return {'hidden_states': s(ks[0], (B, L, D_MODEL), 1.0), 'W_in': s(ks[1], (D_MODEL, 2 * D_INNER), D_MODEL ** (-0.5)), 'conv_w': s(ks[2], (D_CONV, D_INNER), 0.2), 'conv_b': jnp.zeros((D_INNER,), jnp.float32), 'W_x': s(ks[3], (D_INNER, DT_RANK + 2 * D_STATE), D_INNER ** (-0.5)), 'W_dt': s(ks[4], (DT_RANK, D_INNER), DT_RANK ** (-0.5)), 'b_dt': jnp.full((D_INNER,), -4.0) + s(ks[5], (D_INNER,), 0.1), 'A_log': jnp.log(jnp.broadcast_to(jnp.arange(1, D_STATE + 1, dtype=jnp.float32), (D_INNER, D_STATE))), 'D': jnp.ones((D_INNER,), jnp.float32), 'W_out': s(ks[6], (D_INNER, D_MODEL), D_INNER ** (-0.5))}
    _L1_attn_all = _L1_attn_setup()
    _L1_attn_in = {k: v for k, v in _L1_attn_all.items() if k in ('W_in', 'conv_w', 'conv_b', 'W_x', 'W_dt', 'b_dt', 'A_log', 'D', 'W_out')}
    del _L1_attn_all

    def _L1_xattn_setup():
        import jax, jax.numpy as jnp
        import numpy as np
        B, S, D, H = (2, 256, 128, 16)
        DH = D // H

        def _rope(x):
            s, dh = (x.shape[2], x.shape[3])
            inv = jnp.exp(jnp.arange(0, dh, 2, dtype=jnp.float32) * (-(4.0 * jnp.log(jnp.float32(10.0))) / dh))
            pos = jnp.arange(s, dtype=jnp.float32)[:, None]
            sin = jnp.sin(pos * inv)
            cos = jnp.cos(pos * inv)
            x1 = x[..., 0::2]
            x2 = x[..., 1::2]
            out = jnp.stack([x1 * sin - x2 * cos, -x1 * cos - x2 * sin], axis=-1)
            return out.reshape(x.shape)
        key = jax.random.key(seed)
        ks = jax.random.split(key, 12)
        f = lambda k, sh: jax.random.normal(k, sh, dtype=jnp.float32)
        inp = {'q': f(ks[0], (B, S, D)), 'k': f(ks[1], (B, S, D)), 'v': f(ks[2], (B, S, D))}
        scale = 1.0 / np.sqrt(D)
        names = ['q', 'k', 'v', 'o']
        for i, n in enumerate(names):
            inp['W' + n] = f(ks[3 + i], (D, D)) * scale
            inp['b' + n] = f(ks[7 + i], (D,)) * scale
        inp['mask'] = jnp.triu(jnp.ones((S, S), dtype=bool), k=1)[None, None]
        return inp
    _L1_xattn_all = _L1_xattn_setup()
    _L1_xattn_in = {k: v for k, v in _L1_xattn_all.items() if k in ('Wq', 'bq', 'Wk', 'bk', 'Wv', 'bv', 'Wo', 'bo')}
    del _L1_xattn_all

    def _L1_ffn_setup():
        import jax, jax.numpy as jnp
        import numpy as np
        import math
        N_EXP = 8
        TOP_K = 2
        CAPACITY_FACTOR = 1.25

        def _capacity(num_tokens):
            cap = math.floor(TOP_K * CAPACITY_FACTOR * num_tokens / N_EXP)
            cap += cap % 2
            return int(cap)
        key = jax.random.key(seed)
        k1, k2, k3, k4 = jax.random.split(key, 4)
        B, C, d = (4, 128, 128)
        x = jax.random.normal(k1, (B, C, d), dtype=jnp.float32)
        w_g = jax.random.normal(k2, (d, N_EXP), dtype=jnp.float32) * 0.02
        c_fc = jax.random.normal(k3, (N_EXP, d, 4 * d), dtype=jnp.float32) * 0.02
        c_proj = jax.random.normal(k4, (N_EXP, 4 * d, d), dtype=jnp.float32) * 0.02
        return {'x': x, 'w_g': w_g, 'c_fc': c_fc, 'c_proj': c_proj}
    _L1_ffn_all = _L1_ffn_setup()
    _L1_ffn_in = {k: v for k, v in _L1_ffn_all.items() if k in ('w_g', 'c_fc', 'c_proj')}
    del _L1_ffn_all
    return {'x': x, 'ctx_1024': ctx_1024, 'mask_1x1xSxS2_bk1': mask_1x1xSxS2_bk1, 'L0_attn_in_proj_w': _L0_attn_in['in_proj_w'], 'L0_attn_conv_w': _L0_attn_in['conv_w'], 'L0_attn_conv_b': _L0_attn_in['conv_b'], 'L0_attn_x_proj_w': _L0_attn_in['x_proj_w'], 'L0_attn_dt_proj_w': _L0_attn_in['dt_proj_w'], 'L0_attn_dt_proj_b': _L0_attn_in['dt_proj_b'], 'L0_attn_A_log': _L0_attn_in['A_log'], 'L0_attn_D': _L0_attn_in['D'], 'L0_attn_out_proj_w': _L0_attn_in['out_proj_w'], 'L0_attn_gate_w': _L0_attn_in['gate_w'], 'L0_attn_w1': _L0_attn_in['w1'], 'L0_attn_w2': _L0_attn_in['w2'], 'L0_xattn_Wq': _L0_xattn_in['Wq'], 'L0_xattn_bq': _L0_xattn_in['bq'], 'L0_xattn_Wk': _L0_xattn_in['Wk'], 'L0_xattn_bk': _L0_xattn_in['bk'], 'L0_xattn_Wv': _L0_xattn_in['Wv'], 'L0_xattn_bv': _L0_xattn_in['bv'], 'L0_ffn_Wq': _L0_ffn_in['Wq'], 'L0_ffn_bq': _L0_ffn_in['bq'], 'L0_ffn_Wk': _L0_ffn_in['Wk'], 'L0_ffn_bk': _L0_ffn_in['bk'], 'L0_ffn_Wv': _L0_ffn_in['Wv'], 'L0_ffn_bv': _L0_ffn_in['bv'], 'L0_ffn_Wp': _L0_ffn_in['Wp'], 'L0_ffn_bp': _L0_ffn_in['bp'], 'L0_ffn_Wr': _L0_ffn_in['Wr'], 'L0_ffn_br': _L0_ffn_in['br'], 'L0_ffn_Ws': _L0_ffn_in['Ws'], 'L0_ffn_bs': _L0_ffn_in['bs'], 'L0_ffn_temperature': _L0_ffn_in['temperature'], 'L0_ffn_query_embedding': _L0_ffn_in['query_embedding'], 'L1_attn_W_in': _L1_attn_in['W_in'], 'L1_attn_conv_w': _L1_attn_in['conv_w'], 'L1_attn_conv_b': _L1_attn_in['conv_b'], 'L1_attn_W_x': _L1_attn_in['W_x'], 'L1_attn_W_dt': _L1_attn_in['W_dt'], 'L1_attn_b_dt': _L1_attn_in['b_dt'], 'L1_attn_A_log': _L1_attn_in['A_log'], 'L1_attn_D': _L1_attn_in['D'], 'L1_attn_W_out': _L1_attn_in['W_out'], 'L1_xattn_Wq': _L1_xattn_in['Wq'], 'L1_xattn_bq': _L1_xattn_in['bq'], 'L1_xattn_Wk': _L1_xattn_in['Wk'], 'L1_xattn_bk': _L1_xattn_in['bk'], 'L1_xattn_Wv': _L1_xattn_in['Wv'], 'L1_xattn_bv': _L1_xattn_in['bv'], 'L1_xattn_Wo': _L1_xattn_in['Wo'], 'L1_xattn_bo': _L1_xattn_in['bo'], 'L1_ffn_w_g': _L1_ffn_in['w_g'], 'L1_ffn_c_fc': _L1_ffn_in['c_fc'], 'L1_ffn_c_proj': _L1_ffn_in['c_proj']}

def reference(x, ctx_1024, mask_1x1xSxS2_bk1, L0_attn_in_proj_w, L0_attn_conv_w, L0_attn_conv_b, L0_attn_x_proj_w, L0_attn_dt_proj_w, L0_attn_dt_proj_b, L0_attn_A_log, L0_attn_D, L0_attn_out_proj_w, L0_attn_gate_w, L0_attn_w1, L0_attn_w2, L0_xattn_Wq, L0_xattn_bq, L0_xattn_Wk, L0_xattn_bk, L0_xattn_Wv, L0_xattn_bv, L0_ffn_Wq, L0_ffn_bq, L0_ffn_Wk, L0_ffn_bk, L0_ffn_Wv, L0_ffn_bv, L0_ffn_Wp, L0_ffn_bp, L0_ffn_Wr, L0_ffn_br, L0_ffn_Ws, L0_ffn_bs, L0_ffn_temperature, L0_ffn_query_embedding, L1_attn_W_in, L1_attn_conv_w, L1_attn_conv_b, L1_attn_W_x, L1_attn_W_dt, L1_attn_b_dt, L1_attn_A_log, L1_attn_D, L1_attn_W_out, L1_xattn_Wq, L1_xattn_bq, L1_xattn_Wk, L1_xattn_bk, L1_xattn_Wv, L1_xattn_bv, L1_xattn_Wo, L1_xattn_bo, L1_ffn_w_g, L1_ffn_c_fc, L1_ffn_c_proj):
    import jax
    import jax.numpy as jnp

    def _L0_attn_ref(x, in_proj_w, conv_w, conv_b, x_proj_w, dt_proj_w, dt_proj_b, A_log, D, out_proj_w, gate_w, w1, w2):
        import jax, jax.numpy as jnp
        import numpy as np
        DIM = 128
        D_STATE = 16
        D_CONV = 4
        D_INNER = 2 * DIM
        DT_RANK = (DIM + 15) // 16
        E = 8
        K = 2
        HID = 4 * DIM
        B, L = (1, 256)

        def _rmsnorm(x):
            n = jnp.sqrt(jnp.sum(x * x, axis=-1, keepdims=True))
            return x * DIM ** 0.5 / jnp.maximum(n, 1e-12)

        def _selective_scan(u, A_log, D, x_proj_w, dt_proj_w, dt_proj_b):
            A = -jnp.exp(A_log)
            x_dbl = u @ x_proj_w.T
            dt, Bm, Cm = jnp.split(x_dbl, [DT_RANK, DT_RANK + D_STATE], axis=-1)
            delta = jax.nn.softplus(dt @ dt_proj_w.T + dt_proj_b)
            dA = jnp.exp(delta[..., None] * A)
            dBu = delta[..., None] * Bm[:, :, None, :] * u[..., None]

            def step(h, inp):
                dA_t, dBu_t, C_t = inp
                h = dA_t * h + dBu_t
                y = jnp.einsum('bdn,bn->bd', h, C_t)
                return (h, y)
            h0 = jnp.zeros((u.shape[0], D_INNER, D_STATE), u.dtype)
            _, ys = jax.lax.scan(step, h0, (dA.swapaxes(0, 1), dBu.swapaxes(0, 1), Cm.swapaxes(0, 1)))
            y = ys.swapaxes(0, 1)
            return y + u * D

        def _mamba(xn, in_proj_w, conv_w, conv_b, x_proj_w, dt_proj_w, dt_proj_b, A_log, D, out_proj_w):
            xr = xn @ in_proj_w.T
            xm, res = jnp.split(xr, 2, axis=-1)
            xc = jax.lax.conv_general_dilated(xm.swapaxes(1, 2), conv_w, (1,), [(D_CONV - 1, 0)], feature_group_count=D_INNER) + conv_b[:, None]
            xc = jax.nn.silu(xc.swapaxes(1, 2))
            y = _selective_scan(xc, A_log, D, x_proj_w, dt_proj_w, dt_proj_b)
            y = y * jax.nn.silu(res)
            return y @ out_proj_w.T

        def _moe(x, gate_w, w1, w2):
            gates = jax.nn.softmax(x @ gate_w.T, axis=-1)
            vals, idx = jax.lax.top_k(gates, K)
            vals = vals / jnp.sum(vals, axis=-1, keepdims=True)
            sparse = jnp.sum(jax.nn.one_hot(idx, E, dtype=x.dtype) * vals[..., None], axis=-2)
            h = jax.nn.gelu(jnp.einsum('bld,ehd->bleh', x, w1), approximate=False)
            y = jnp.einsum('bleh,edh->bled', h, w2)
            return jnp.einsum('bled,ble->bld', y, sparse)
        skip = x
        xn = _rmsnorm(x)
        xm = _mamba(xn, in_proj_w, conv_w, conv_b, x_proj_w, dt_proj_w, dt_proj_b, A_log, D, out_proj_w) + xn
        xm = _rmsnorm(xm)
        return _moe(xm, gate_w, w1, w2) + skip

    def _L0_xattn_ref(hidden_states, context_states, Wq, bq, Wk, bk, Wv, bv):
        import jax, jax.numpy as jnp
        import numpy as np
        import math
        H = 16

        def _split_heads(x):
            b, n, hd = x.shape
            return x.reshape(b, n, H, hd // H).transpose(0, 2, 1, 3)
        q = _split_heads(hidden_states @ Wq.T + bq)
        ctx = jnp.concatenate((hidden_states, context_states), axis=-2)
        k = _split_heads(ctx @ Wk.T + bk)
        v = _split_heads(ctx @ Wv.T + bv)
        d = q.shape[-1]
        scores = jnp.einsum('bhqd,bhkd->bhqk', q, k) / math.sqrt(d)
        probs = jax.nn.softmax(scores, axis=-1)
        out = jnp.einsum('bhqk,bhkd->bhqd', probs, v)
        b, h, n, dd = out.shape
        return out.transpose(0, 2, 1, 3).reshape(b, n, h * dd)

    def _L0_ffn_ref(x, Wq, bq, Wk, bk, Wv, bv, Wp, bp, Wr, br, Ws, bs, temperature, query_embedding):
        import jax, jax.numpy as jnp
        import numpy as np
        import math
        DIM = 128
        NUM_HEADS = 16
        SHARED_HEADS = 1
        ROUTED_HEADS = 3
        HEAD_DIM = DIM // NUM_HEADS
        B, N = (2, 256)
        Bsz, Nn, C = x.shape
        H, hd = (NUM_HEADS, HEAD_DIM)

        def heads(W, b):
            y = x @ W.T + b
            return y.reshape(Bsz, Nn, H, hd).transpose(0, 2, 1, 3)
        q = heads(Wq, bq)
        k = heads(Wk, bk)
        v = heads(Wv, bv)
        q_norm = q / jnp.linalg.norm(q, axis=-1, keepdims=True)
        q_scaled = (q_norm + query_embedding[None]) * jax.nn.softplus(temperature)[None]
        attn = jnp.einsum('bhqd,bhkd->bhqk', q_scaled, k) / math.sqrt(hd)
        attn = jax.nn.softmax(attn, axis=-1)
        h = jnp.einsum('bhqk,bhkd->bhqd', attn, v)
        h = h.transpose(0, 2, 1, 3).reshape(Bsz, Nn, C)
        gates = jax.nn.softmax(h @ Wr.T + br, axis=-1)
        _, idx = jax.lax.top_k(gates, ROUTED_HEADS)
        mask = jax.nn.one_hot(idx, H - SHARED_HEADS, dtype=gates.dtype).sum(axis=-2)
        routed_gates = gates * mask * ROUTED_HEADS
        sw = jax.nn.softmax(h @ Ws.T + bs, axis=-1)
        shared_gates = sw * SHARED_HEADS
        weight_0 = sw * 2.0
        shared_gates = weight_0[..., 0:1] * shared_gates
        routed_gates = weight_0[..., 1:2] * routed_gates
        masked_gates = jnp.concatenate([shared_gates, routed_gates], axis=-1)
        out = h * masked_gates.sum(axis=-1, keepdims=True)
        return out @ Wp.T + bp

    def _L1_attn_ref(hidden_states, W_in, conv_w, conv_b, W_x, W_dt, b_dt, A_log, D, W_out):
        import jax, jax.numpy as jnp
        import numpy as np
        B, L, D_MODEL = (2, 256, 128)
        D_STATE, EXPAND, D_CONV = (16, 2, 4)
        D_INNER = EXPAND * D_MODEL
        DT_RANK = D_MODEL // 16
        silu = jax.nn.silu
        xz = hidden_states @ W_in
        x, z = jnp.split(xz, 2, axis=-1)
        x = jax.lax.conv_general_dilated(x, conv_w[:, None, :], (1,), [(D_CONV - 1, 0)], dimension_numbers=('NWC', 'WIO', 'NWC'), feature_group_count=D_INNER)
        x = silu(x + conv_b)
        proj = x @ W_x
        dt_low = proj[..., :DT_RANK]
        Bm = proj[..., DT_RANK:DT_RANK + D_STATE]
        Cm = proj[..., DT_RANK + D_STATE:]
        dt = jax.nn.softplus(dt_low @ W_dt + b_dt)
        A = -jnp.exp(A_log)

        def step(h, inputs):
            dt_t, x_t, B_t, C_t = inputs
            h = jnp.exp(dt_t[..., None] * A) * h + (dt_t * x_t)[..., None] * B_t[:, None, :]
            y = jnp.einsum('bds,bs->bd', h, C_t)
            return (h, y)
        h0 = jnp.zeros((hidden_states.shape[0], D_INNER, D_STATE), x.dtype)
        xs = (jnp.swapaxes(dt, 0, 1), jnp.swapaxes(x, 0, 1), jnp.swapaxes(Bm, 0, 1), jnp.swapaxes(Cm, 0, 1))
        _, ys = jax.lax.scan(step, h0, xs)
        y = jnp.swapaxes(ys, 0, 1) + x * D
        y = y * silu(z)
        return y @ W_out

    def _L1_xattn_ref(q, k, v, Wq, bq, Wk, bk, Wv, bv, Wo, bo, mask):
        import jax, jax.numpy as jnp
        import numpy as np
        B, S, D, H = (2, 256, 128, 16)
        DH = D // H

        def _rope(x):
            s, dh = (x.shape[2], x.shape[3])
            inv = jnp.exp(jnp.arange(0, dh, 2, dtype=jnp.float32) * (-(4.0 * jnp.log(jnp.float32(10.0))) / dh))
            pos = jnp.arange(s, dtype=jnp.float32)[:, None]
            sin = jnp.sin(pos * inv)
            cos = jnp.cos(pos * inv)
            x1 = x[..., 0::2]
            x2 = x[..., 1::2]
            out = jnp.stack([x1 * sin - x2 * cos, -x1 * cos - x2 * sin], axis=-1)
            return out.reshape(x.shape)
        b, s, d = q.shape
        h, dh = (H, DH)

        def proj(x, W, bias):
            return (x @ W.T + bias).reshape(b, -1, h, dh).transpose(0, 2, 1, 3)
        Q = proj(q, Wq, bq)
        K = proj(k, Wk, bk)
        V = proj(v, Wv, bv)
        PQ = _rope(Q)
        PK = _rope(K)
        scores = jnp.einsum('bhqd,bhkd->bhqk', PQ, PK)
        neg = jnp.finfo(scores.dtype).min
        scores = jnp.where(mask, neg, scores)
        p = jax.nn.softmax(scores, axis=-1)
        p = jnp.where(mask, jnp.float32(0.0), p)
        out = jnp.einsum('bhqk,bhkd->bhqd', p, V)
        out = out.transpose(0, 2, 1, 3).reshape(b, s, d)
        return out @ Wo.T + bo

    def _L1_ffn_ref(x, w_g, c_fc, c_proj):
        import jax, jax.numpy as jnp
        import numpy as np
        import math
        N_EXP = 8
        TOP_K = 2
        CAPACITY_FACTOR = 1.25

        def _capacity(num_tokens):
            cap = math.floor(TOP_K * CAPACITY_FACTOR * num_tokens / N_EXP)
            cap += cap % 2
            return int(cap)
        B, C, d = x.shape
        T = B * C
        cap = _capacity(T)
        xt = x.reshape(T, d)
        logits = xt @ w_g
        top_v, top_i = jax.lax.top_k(logits, TOP_K)
        full = jnp.full_like(logits, -jnp.inf)
        full = full.at[jnp.arange(T)[:, None], top_i].set(top_v)
        probs = jax.nn.softmax(full, axis=-1)
        exp_mask = jax.nn.one_hot(top_i, N_EXP, dtype=jnp.int32)
        exp_mask = jnp.transpose(exp_mask, (1, 0, 2))
        exp_rank = jnp.cumsum(exp_mask.reshape(TOP_K * T, N_EXP), axis=0) - 1
        exp_rank = exp_rank.reshape(TOP_K, T, N_EXP)
        exp_mask = exp_mask * (exp_rank < cap).astype(jnp.int32)
        exp_rank = jnp.sum(exp_mask * exp_rank, axis=-1)
        exp_weights = exp_mask.astype(x.dtype) * probs[None]
        rank_oh = jax.nn.one_hot(exp_rank, cap, dtype=x.dtype)
        cb_weight = jnp.einsum('kte,ktc->tec', exp_weights, rank_oh)
        sec_mask = (cb_weight != 0).astype(x.dtype)
        exp_batches = jnp.einsum('tec,td->ecd', sec_mask, xt)
        h = jax.nn.gelu(jnp.einsum('ecd,edf->ecf', exp_batches, c_fc), approximate=False)
        exp_out = jnp.einsum('ecf,efd->ecd', h, c_proj)
        out = cb_weight.reshape(T, N_EXP * cap) @ exp_out.reshape(N_EXP * cap, d)
        return out.reshape(B, C, d)
    x = _layernorm(x + _L0_attn_ref(x, L0_attn_in_proj_w, L0_attn_conv_w, L0_attn_conv_b, L0_attn_x_proj_w, L0_attn_dt_proj_w, L0_attn_dt_proj_b, L0_attn_A_log, L0_attn_D, L0_attn_out_proj_w, L0_attn_gate_w, L0_attn_w1, L0_attn_w2), axis=-1)
    x = _layernorm(x + _L0_xattn_ref(x, ctx_1024, L0_xattn_Wq, L0_xattn_bq, L0_xattn_Wk, L0_xattn_bk, L0_xattn_Wv, L0_xattn_bv), axis=-1)
    x = _layernorm(x + _L0_ffn_ref(x, L0_ffn_Wq, L0_ffn_bq, L0_ffn_Wk, L0_ffn_bk, L0_ffn_Wv, L0_ffn_bv, L0_ffn_Wp, L0_ffn_bp, L0_ffn_Wr, L0_ffn_br, L0_ffn_Ws, L0_ffn_bs, L0_ffn_temperature, L0_ffn_query_embedding), axis=-1)
    x = _layernorm(x + _L1_attn_ref(x, L1_attn_W_in, L1_attn_conv_w, L1_attn_conv_b, L1_attn_W_x, L1_attn_W_dt, L1_attn_b_dt, L1_attn_A_log, L1_attn_D, L1_attn_W_out), axis=-1)
    x = _layernorm(x + _L1_xattn_ref(x, ctx_1024, ctx_1024, L1_xattn_Wq, L1_xattn_bq, L1_xattn_Wk, L1_xattn_bk, L1_xattn_Wv, L1_xattn_bv, L1_xattn_Wo, L1_xattn_bo, mask_1x1xSxS2_bk1), axis=-1)
    x = _layernorm(x + _L1_ffn_ref(x, L1_ffn_w_g, L1_ffn_c_fc, L1_ffn_c_proj), axis=-1)
    return x

_drawn_inputs = setup_inputs


def setup_inputs(seed=0):
    import zlib

    import numpy as np

    out = dict(_drawn_inputs(seed))
    spreads = {'L0_attn_conv_b': (0.0, 0.8),
     'L0_attn_D': (1.0, 0.6),
     'L0_xattn_bq': (0.0, 0.417),
     'L0_xattn_bk': (0.0, 0.8),
     'L0_xattn_bv': (0.0, 0.1),
     'L0_ffn_temperature': (4.151041507720947, 0.6),
     'L1_attn_conv_b': (0.0, 0.281),
     'L1_attn_D': (1.0, 0.6)}
    factors = {'L0_attn_in_proj_w': 8.0,
     'L0_attn_conv_w': 8.0,
     'L0_attn_x_proj_w': 8.0,
     'L0_attn_dt_proj_w': 8.0,
     'L0_attn_dt_proj_b': 8.0,
     'L0_attn_A_log': 8.0,
     'L0_attn_out_proj_w': 8.0,
     'L0_attn_gate_w': 3.694,
     'L0_attn_w1': 3.252,
     'L0_attn_w2': 3.21,
     'L0_ffn_bq': 8.0,
     'L0_ffn_bk': 8.0,
     'L0_ffn_Wr': 8.0,
     'L0_ffn_br': 8.0,
     'L0_ffn_Ws': 8.0,
     'L0_ffn_bs': 8.0,
     'L0_ffn_query_embedding': 8.0,
     'L1_attn_W_x': 8.0,
     'L1_attn_W_dt': 8.0,
     'L1_attn_b_dt': 8.0,
     'L1_attn_A_log': 8.0,
     'L1_xattn_bk': 2.797}
    for name, (base, spread) in spreads.items():
        noise = np.random.default_rng([zlib.crc32(name.encode()), seed]).standard_normal(out[name].shape)
        drawn = base * np.exp(spread * noise) if base else spread * noise
        out[name] = jnp.asarray(drawn.astype(out[name].dtype))
    for name, factor in factors.items():
        out[name] = (out[name] * factor).astype(out[name].dtype)
    return out
```

```python
from contextlib import ExitStack

import numpy as np

import concourse.bass as bass
from concourse import mybir

F32 = mybir.dt.float32
BF16 = mybir.dt.bfloat16
U32 = mybir.dt.uint32
U8 = mybir.dt.uint8
ALU = mybir.AluOpType
ACT = mybir.ActivationFunctionType
AX = mybir.AxisListType

B, L, D = 16, 128, 128
CTX = 77
SEQ = 4
TOK = SEQ * L
GROUPS = B // SEQ
DI, NS, RANK, CONV = 256, 16, 8, 4
HALF = DI // 128
HEADS, DH = 16, 8
EXPERTS, HID = 8, 512
SLICES = HID // 128
CAPACITY = 640
TILES = B
ROUTED, SHARED = 15, 2
NEG = float(np.finfo(np.float32).min)

PARAMS = [
    ("in_w0", 2 * DI), ("in_w1", 2 * DI), ("x_w0", HALF * 40), ("x_w1", HALF * 40),
    ("dt_w0", DI), ("dt_w1", DI), ("out_w0", HALF * D), ("out_w1", HALF * D),
    ("conv_w0", HALF * CONV), ("conv_w1", HALF * CONV), ("conv_b0", HALF), ("conv_b1", HALF),
    ("dt_b0", HALF), ("dt_b1", HALF), ("a_log0", HALF * NS), ("a_log1", HALF * NS),
    ("d0", HALF), ("d1", HALF), ("gate0", EXPERTS), ("gate1", EXPERTS),
    ("xq", D), ("xk", D), ("xv", D), ("xbq", 1), ("xbk", 1), ("xbv", D),
    ("fq", D), ("fk", D), ("fv", D), ("fp", D), ("fbq", 1), ("fbk", 1), ("fbv", D), ("fbp", 1),
    ("frs", ROUTED + SHARED), ("fbrs", ROUTED + SHARED), ("temp", 1), ("qe", 1),
    ("rq", D), ("rqs", D), ("rk", D), ("rks", D), ("rv", D), ("ro", D),
    ("rbq", 1), ("rbqs", 1), ("rbk", 1), ("rbks", 1), ("rbv", D), ("rbo", 1),
    ("ident", 128), ("mean", 128), ("center", 128), ("head_ones", 128), ("before", 128), ("ones", 128),
    ("head_mask", 4), ("iota", EXPERTS), ("rope_sin", L), ("rope_cos", L), ("scan_keep", EXPERTS * 2 * TILES),
]
COLUMN = {}
WIDTH = 0
for _name, _cols in PARAMS:
    COLUMN[_name] = (WIDTH, WIDTH + _cols)
    WIDTH += _cols


class Chain:

    def __init__(self, engine, semaphore, base=0):
        self.engine, self.semaphore, self.base, self.n = engine, semaphore, base, 0

    def mark(self, instruction):
        instruction.then_inc(self.semaphore, 1)
        self.n += 1
        return self.n

    def wait(self, n):
        self.engine.wait_ge(self.semaphore, self.base + n)

    def link(self, instruction):
        self.wait(self.mark(instruction))


DVE_LINKS = 113
DVE_LINKS_2 = 7


def decoder_kernel(nc, x_t, ctx_t, params, selectors, w_in, w_out, mask, out):
    with ExitStack() as ctx:
        def sb(name, shape, dt=F32):
            return ctx.enter_context(nc.sbuf_tensor(name, shape, dt))

        semaphores = {}

        def S(name):
            if name not in semaphores:
                semaphores[name] = ctx.enter_context(nc.semaphore(name))
            return semaphores[name]

        ps = ctx.enter_context(nc.psum_tensor("ps", [128, 8, 512], F32))
        pw = sb("pw", [128, WIDTH])
        sel = sb("sel", [96, 2 * NS, 128], BF16)
        moe_in = sb("moe_in", [128, 2, EXPERTS, HID])
        moe_out = sb("moe_out", [128, 2, EXPERTS, SLICES, D])
        x_in = sb("x_in", [128, TOK])
        ctx_in = sb("ctx_in", [128, SEQ * CTX])
        xn = sb("xn", [128, TOK])
        x1 = sb("x1", [128, TOK])
        x2 = sb("x2", [128, TOK])
        x3 = sb("x3", [128, TOK])
        x4 = sb("x4", [128, TOK])
        xm = x4
        x5 = sb("x5", [128, B * L])
        res = sb("res", [128, TOK])
        sq = sb("sq", [128, TOK])
        rs = sb("rs", [128, TOK])
        xp = sb("xp", [128, HALF, SEQ, CONV - 1 + L])
        shared = sb("shared", [128, 6 * HALF * TOK])
        sz, cv, u, dl, dtu, yacc = (
            shared[:, i * HALF * TOK:(i + 1) * HALF * TOK].rearrange("p (h t) -> p h t", h=HALF) for i in range(6))
        dtl = sb("dtl", [RANK, TOK])
        bcs = sb("bcs", [96, TOK], BF16)
        bc_hi = sb("bc_hi", [32, TOK], BF16)
        bc_r = sb("bc_r", [32, TOK])
        a_neg = sb("a_neg", [128, 2, HALF, NS])
        dA = sb("dA", [128, 2, HALF, SEQ, L])
        arena = sb("arena", [128, 8192])

        def part(a, n):
            return arena[:, a:a + n]

        ab = part(0, 1024).rearrange("p (h t) -> p h t", h=HALF)
        u1 = part(1024, 1024).rearrange("p (h t) -> p h t", h=HALF)
        lb = part(2048, 1024).rearrange("p (h t) -> p h t", h=HALF)
        rb = part(3072, 1024).rearrange("p (h t) -> p h t", h=HALF)
        hs = part(4096, 2048).rearrange("p (s n) -> p s n", s=2)
        hc = part(6144, 2048).rearrange("p (s h t) -> p s h t", s=2, h=HALF)
        gelu = part(0, 2048).rearrange("p (s t) -> p s t", s=4)
        gate_sb = part(2048, 1024).rearrange("p (s t) -> p s t", s=2)
        weighted = part(3072, 512)
        sc = part(0, 4096).rearrange("p (s n) -> p s n", s=2)
        pr = part(4096, 4096).rearrange("p (s n) -> p s n", s=2)
        qm = shared[:, 0:4 * TOK].rearrange("p (i t) -> p i t", i=4)
        pt = shared[:, 2048:3584].rearrange("p (s a b) -> p s a b", s=3, a=4)
        qf, qt, hT = shared[:, 3584:4096], shared[:, 4096:4608], shared[:, 4608:5120]
        kt = shared[:, 5120:5120 + SEQ * (L + CTX)].rearrange("p (s t) -> p s t", s=SEQ)
        va = sb("va", [128, SEQ, HEADS, DH + 1])
        vb = sb("vb", [CTX, SEQ, HEADS, DH + 1])
        mx = sb("mx", [128, HEADS])
        rec = sb("rec", [128, HEADS])
        ot = sb("ot", [128, SEQ, D])
        bqm = sb("bqm", [128, 4])
        spm = sb("spm", [128, 4])
        tmp = sb("tmp", [128, 4])
        mask8 = sb("mask8", [128, CTX], U8)
        mneg = sb("mneg", [128, CTX])
        keep = sb("keep", [128, 1])
        rl = sb("rl", [128, TILES, ROUTED + SHARED])
        r1 = sb("r1", [128, TILES])
        r2 = sb("r2", [128, TILES])
        v8 = sb("v8", [128, TILES, 8])
        i8 = sb("i8", [128, TILES, 8], U32)
        f8 = sb("f8", [128, TILES, 8])
        t8 = sb("t8", [128, TILES, 8])
        gt = sb("gt", [128, SEQ, EXPERTS])
        gt_all = sb("gt_all", [128, TILES, EXPERTS])
        oh = part(5120, 256).rearrange("p (e k t) -> p e k t", e=EXPERTS, k=2)
        tot = part(5376, 256).rearrange("p (e k t) -> p e k t", e=EXPERTS, k=2)
        rank = part(5632, 256).rearrange("p (e k t) -> p e k t", e=EXPERTS, k=2)
        x5g, yout = x1, x2

        def W(name):
            a, b = COLUMN[name]
            return pw[:, a:b]

        def seqs(ap, width=L):
            return ap.rearrange("p (s t) -> p s t", s=SEQ)

        ident = W("ident")
        idle = sb("idle", [128, 1])
        LN_EPS = sb("ln_eps", [128, 1])

        block = ctx.enter_context(nc.Block())

        DBU = (slice(2, 4), slice(6, 8))
        NORMS = 7

        @block.sync
        def _(sp):
            sp.dma_start(pw[:, :], params).then_inc(S("params_in"), 16)
            sp.dma_start(sel[:, :, :], selectors).then_inc(S("sel_in"), 16)
            sp.dma_start(mask8[:, :], mask).then_inc(S("mask_in"), 16)
            sp.dma_start(x_in[:, :], x_t[:, 0:TOK]).then_inc(S("x_in"), 16)
            sp.dma_start(ctx_in[:, :], ctx_t[:, 0:SEQ * CTX]).then_inc(S("ctx_in"), 16)
            with sp.Fori(1, GROUPS) as g:
                sp.wait_ge(S("x_used"), g)
                sp.dma_start(x_in[:, :], x_t[:, bass.ts(g, TOK)]).then_inc(S("x_in"), 16)
                sp.wait_ge(S("ctx_used"), g)
                sp.dma_start(ctx_in[:, :], ctx_t[:, bass.ts(g, SEQ * CTX)]).then_inc(S("ctx_in"), 16)
            sp.sem_inc(S("out_free"), 1)
            with sp.Fori(0, GROUPS) as g:
                sp.wait_ge(S("out_ready"), g + 1)
                sp.dma_start(out[:, bass.ts(g, TOK)], yout[:, :]).then_inc(S("stored"), 16)
                sp.wait_ge(S("stored"), g * 16 + 16)
                sp.sem_inc(S("out_free"), 1)

        @block.gpsimd
        def _(pool):
            for l in range(2):
                pool.dma_start(moe_in[:, l, :, :], w_in[:, l, :, :]).then_inc(S(f"moe_in{l}"), 16)
                pool.dma_start(moe_out[:, l, :, :, :], w_out[:, l, :, :, :]).then_inc(S(f"moe_in{l}"), 16)
            with pool.Fori(0, GROUPS) as g:
                for l in range(2):
                    turn = g * 2 + l
                    pool.wait_ge(S("seeded"), turn + 1)
                    for n in range(NS):
                        pool.wait_ge(S("hc"), turn * NS + n + 1)
                        if n:
                            pool.wait_ge(S("summed"), turn * NS + n)
                        pool.tensor_tensor(yacc[:, :, :], yacc[:, :, :], hc[:, n % 2, :, :],
                                           ALU.add).then_inc(S("summed"), 1)

        @block.tensor
        def _(pe):
            def norm(i, g, src, gate):
                if i < NORMS:
                    nth, cth = g * NORMS + i, g * (NORMS - 2) + i - 2
                else:
                    nth, cth = g + GROUPS * NORMS, g + GROUPS * (NORMS - 2)
                if i >= 2:
                    gate()
                    pe.matmul(ps[:, 0, :], W("center"), src, start=True, stop=True).then_inc(S("centred"), 1)
                pe.wait_ge(S("squared"), nth + 1)
                pe.matmul(ps[:, 1, :], W("mean"), sq[:, :], start=True, stop=True).then_inc(S("var"), 1)

            def mamba(l, g, src):
                turn = g * 2 + l
                for m in range(4):
                    pe.matmul(ps[:, m, :], W(f"in_w{l}")[:, m * 128:(m + 1) * 128], src,
                              start=True, stop=True).then_inc(S("proj"), 1)
                pe.wait_ge(S("u_ready"), turn * HALF + HALF)
                for bank, a, n in ((4, 0, RANK), (5, RANK, 2 * NS)):
                    for h in range(HALF):
                        mm = pe.matmul(ps[0:n, bank, :], W(f"x_w{l}")[:, h * 40 + a:h * 40 + a + n], u[:, h, :],
                                       start=(h == 0), stop=(h == HALF - 1))
                    mm.then_inc(S("xdbl"), 1)
                pe.wait_ge(S("dtl"), turn + 1)
                for h in range(HALF):
                    pe.matmul(ps[:, 6 + h, :], W(f"dt_w{l}")[0:RANK, h * 128:(h + 1) * 128], dtl[:, :],
                              start=True, stop=True).then_inc(S("dt_mm"), 1)
                pe.wait_ge(S("bc_split"), turn + 1)
                pe.wait_ge(S("z_silu"), turn * HALF + HALF)
                for n in range(NS):
                    if n:
                        pe.wait_ge(S("dbu"), turn * NS + n)
                    pe.matmul(ps[:, 0, :], sel[:, n, :], bcs[:, :], start=True, stop=True).then_inc(S("b_row"), 1)
                    if n:
                        pe.wait_ge(S("hc"), turn * NS + n)
                    pe.matmul(ps[:, 1, :], sel[:, NS + n, :], bcs[:, :], start=True, stop=True).then_inc(S("c_row"), 1)
                pe.wait_ge(S("gated"), turn + 1)
                for h in range(HALF):
                    mm = pe.matmul(ps[:, 4, :], W(f"out_w{l}")[:, h * D:(h + 1) * D], yacc[:, h, :],
                                   start=(h == 0), stop=(h == HALF - 1))
                mm.then_inc(S("mamba_out"), 1)

            def experts(l, g, src, gates_ready):
                def down(i):
                    e, f = divmod(i, SLICES)
                    pe.wait_ge(S(f"gelu{l}"), g * 32 + i + 1)
                    if f == 0 and e >= 2:
                        pe.wait_ge(S(f"weighted{l}"), g * EXPERTS + e - 1)
                    mm = pe.matmul(ps[:, 2 + e % 2, :], moe_out[:, l, e, f, :], gelu[:, i % 4, :],
                                   start=(f == 0), stop=(f == SLICES - 1))
                    mm.then_inc(S(f"down{l}"), 1)

                def spread(e):
                    if e == 0:
                        gates_ready()
                    if e >= 2:
                        pe.wait_ge(S(f"gate_copied{l}"), g * EXPERTS + e - 1)
                    for j in range(SEQ):
                        mm = pe.matmul(ps[:, 4 + e % 2, j * L:(j + 1) * L],
                                       gt[:, j, e:e + 1].to_broadcast([128, 128]), ident, start=True, stop=True)
                    mm.then_inc(S(f"gate_spread{l}"), 1)

                for i in range(EXPERTS * SLICES):
                    e, f = divmod(i, SLICES)
                    if i >= 2:
                        pe.wait_ge(S(f"gelu{l}"), g * 32 + i - 1)
                    pe.matmul(ps[:, i % 2, :], moe_in[:, l, e, f * 128:(f + 1) * 128], src,
                              start=True, stop=True).then_inc(S(f"up{l}"), 1)
                    if i:
                        down(i - 1)
                    if f == 2:
                        spread(e)
                down(EXPERTS * SLICES - 1)

            def values(src, n, bank, w, rows):
                for j in range(SEQ):
                    mm = pe.matmul(ps[0:rows, bank, j * D:(j + 1) * D], src[:, j * rows:(j + 1) * rows], w,
                                   start=True, stop=True)
                mm.then_inc(S(n), 1)

            def attend(a, g, keys, halves):
                steps = SEQ * halves
                per = 4 // halves
                width = 512 // per

                def scores(k):
                    j, half = divmod(k, halves)
                    if k:
                        pe.wait_ge(S("scores_readr" if a == "r" else f"shifted{a}"), g * steps + k)
                    for i in range(per):
                        for quad in range(4):
                            p = slice(32 * quad, 32 * quad + 32)
                            mm = pe.matmul(ps[:, quad, i * width:i * width + keys],
                                           qm[p, half * per + i, j * L:(j + 1) * L], kt[p, j, 0:keys],
                                           start=True, stop=True)
                    mm.then_inc(S(f"scores{a}"), 1)

                parts = [("a", 0, min(keys, 128))] + ([("b", 128, keys - 128)] if keys > 128 else [])
                if a == "r":
                    parts = [("b", 0, CTX)]
                blocks = per * len(parts)
                turn = 0

                scores(0)
                for k in range(steps):
                    j, half = divmod(k, halves)
                    if k + 1 < steps:
                        scores(k + 1)
                    pe.wait_ge(S(f"probs{a}"), g * steps + k + 1)
                    made = []
                    for q in range(per):
                        for name, at, rows in parts:
                            if turn >= 3:
                                pe.wait_ge(S(f"turned{a}"), g * steps * blocks + turn - 2)
                            for quad in range(4):
                                c = (quad * per + q) * keys + at
                                mm = pe.transpose(ps[0:rows, 4 + turn % 3, quad * 128:(quad + 1) * 128],
                                                  pr[:, k % 2, c:c + rows], ident)
                            mm.then_inc(S(f"turn{a}"), 1)
                            made.append((q, name, rows, turn))
                            turn += 1
                        if q:
                            product(a, g, j, half, per, parts, made, q - 1, steps, blocks, k)
                    product(a, g, j, half, per, parts, made, per - 1, steps, blocks, k)
                    if half == halves - 1:
                        pe.wait_ge(S(f"normed{a}"), g * SEQ + j + 1)
                        pe.transpose(ps[:, 7, 256:256 + L], ot[:, j, :], ident).then_inc(S(f"head_out{a}"), 1)

            def product(a, g, j, half, per, parts, made, q, steps, blocks, k):
                mine = [m for m in made if m[0] == q]
                pe.wait_ge(S(f"turned{a}"), g * steps * blocks + mine[-1][3] + 1)
                if q == 0 and half == 0 and j:
                    pe.wait_ge(S({"x": "res3", "f": "h_ready", "r": "r_ready"}[a]), g * SEQ + j)
                for quad in range(4):
                    head = 4 * quad + half * per + q
                    for n, (_, name, rows, t) in enumerate(mine):
                        v = va if name == "a" else vb
                        mm = pe.matmul(ps[:, 7, head * (DH + 1):(head + 1) * (DH + 1)],
                                       pt[0:rows, t % 3, quad, :], v[0:rows, j, head, :],
                                       start=(n == 0), stop=(n == len(mine) - 1))
                mm.then_inc(S(f"product{a}"), 1)

            pe.wait_ge(S("params_in"), 16)
            pe.wait_ge(S("sel_in"), 16)
            with pe.Fori(0, GROUPS) as g:
                norm(0, g, None, None)
                pe.wait_ge(S("n0"), g + 1)
                mamba(0, g, xn[:, :])
                norm(1, g, None, None)
                pe.wait_ge(S("n1"), g + 1)
                for j in range(SEQ):
                    mm = pe.matmul(ps[:, 6, j * EXPERTS:(j + 1) * EXPERTS], xm[:, j * L:(j + 1) * L], W("gate0"),
                                   start=True, stop=True)
                mm.then_inc(S("logits0"), 1)
                pe.wait_ge(S("moe_in0"), 32)
                experts(0, g, xm[:, :], lambda: pe.wait_ge(S("gates0"), g + 1))
                norm(2, g, res[:, :], lambda: pe.wait_ge(S("res2"), g + 1))
                pe.wait_ge(S("n2"), g + 1)
                pe.matmul(ps[:, 0, :], W("xq"), x1[:, :], start=True, stop=True).then_inc(S("q_mm_x"), 1)
                pe.matmul(ps[:, 1, :], W("xk"), x1[:, :], start=True, stop=True).then_inc(S("k_mm_x"), 1)
                pe.wait_ge(S("ctx_in"), g * 16 + 16)
                pe.matmul(ps[:, 2, 0:SEQ * CTX], W("xk"), ctx_in[:, :], start=True, stop=True).then_inc(S("k_mm_x"), 1)
                values(x1[:, :], "v_mm_x", 3, W("xv"), L)
                values(ctx_in[:, :], "v_mm_x", 4, W("xv"), CTX)
                pe.wait_ge(S("qkv_x"), g + 1)
                pe.wait_ge(S("q_masked_x"), g * 4 + 4)
                attend("x", g, L + CTX, 2)
                norm(3, g, res[:, :], lambda: pe.wait_ge(S("res3"), g * SEQ + SEQ))
                pe.wait_ge(S("n3"), g + 1)
                pe.matmul(ps[:, 0, :], W("fq"), x2[:, :], start=True, stop=True).then_inc(S("q_mm_f"), 1)
                pe.matmul(ps[:, 1, :], W("fk"), x2[:, :], start=True, stop=True).then_inc(S("k_mm_f"), 1)
                values(x2[:, :], "v_mm_f", 3, W("fv"), L)
                pe.wait_ge(S("q_squared"), g + 1)
                pe.matmul(ps[:, 2, :], W("head_ones"), sq[:, :], start=True, stop=True).then_inc(S("q_norm"), 1)
                pe.wait_ge(S("qkv_f"), g + 1)
                attend("f", g, L, 1)
                pe.wait_ge(S("h_ready"), g * SEQ + SEQ)
                for j in range(SEQ):
                    mm = pe.matmul(ps[:, 6, j * 17:(j + 1) * 17], hT[:, j * L:(j + 1) * L], W("frs"),
                                   start=True, stop=True)
                mm.then_inc(S("logits_f"), 1)
                pe.wait_ge(S("scaled_f"), g + 1)
                for j in range(SEQ):
                    mm = pe.transpose(ps[:, 5, j * L:(j + 1) * L], qm[:, j, 0:L], ident)
                mm.then_inc(S("scaled_turned"), 1)
                pe.wait_ge(S("scaled_copied"), g + 1)
                pe.matmul(ps[:, 4, :], W("fp"), hT[:, :], start=True, stop=True).then_inc(S("proj_f"), 1)
                norm(4, g, res[:, :], lambda: pe.wait_ge(S("res4"), g + 1))
                pe.wait_ge(S("n4"), g + 1)
                mamba(1, g, x3[:, :])
                norm(5, g, res[:, :], lambda: pe.wait_ge(S("res5"), g + 1))
                pe.wait_ge(S("n5"), g + 1)
                pe.matmul(ps[:, 0, :], W("rq"), x4[:, :], start=True, stop=True)
                pe.matmul(ps[:, 1, :], W("rqs"), x4[:, :], start=True, stop=True).then_inc(S("q_mm_r"), 1)
                pe.matmul(ps[:, 2, 0:SEQ * CTX], W("rk"), ctx_in[:, :], start=True, stop=True)
                pe.matmul(ps[:, 3, 0:SEQ * CTX], W("rks"), ctx_in[:, :], start=True, stop=True).then_inc(S("k_mm_r"), 1)
                values(ctx_in[:, :], "ctx_used", 4, W("rv"), CTX)
                pe.wait_ge(S("qkv_r"), g + 1)
                attend("r", g, CTX, 1)
                pe.wait_ge(S("r_ready"), g * SEQ + SEQ)
                pe.matmul(ps[:, 4, :], W("ro"), hT[:, :], start=True, stop=True).then_inc(S("proj_r"), 1)
                norm(6, g, res[:, :], lambda: pe.wait_ge(S("res6"), g + 1))
            pe.wait_ge(S("n6"), GROUPS)
            for t in range(TILES):
                mm = pe.matmul(ps[:, 6, t * EXPERTS:(t + 1) * EXPERTS], x5[:, t * L:(t + 1) * L], W("gate1"),
                               start=True, stop=True)
            mm.then_inc(S("logits1"), 1)
            pe.wait_ge(S("picked"), 1)
            picks = oh[:, :, :, :].rearrange("p e k t -> p (e k t)")
            pe.matmul(ps[:, 4, 0:256], W("before"), picks, start=True, stop=True)
            pe.matmul(ps[:, 5, 0:256], W("ones"), picks, start=True, stop=True).then_inc(S("counted"), 1)
            pe.wait_ge(S("moe_in1"), 32)
            pe.wait_ge(S("ranked"), 1)
            with pe.Fori(0, GROUPS) as g:
                pe.wait_ge(S("x5_group"), g + 1)
                experts(1, g, x5g[:, :], lambda: pe.wait_ge(S("gates1"), g + 1))
                norm(7, g, res[:, :], lambda: pe.wait_ge(S("res7"), g + 1))

        @block.scalar
        def _(act):
            def norm(i, g, src, wait):
                if i < NORMS:
                    nth, cth = g * NORMS + i, g * (NORMS - 2) + i - 2
                else:
                    nth, cth = g + GROUPS * NORMS, g + GROUPS * (NORMS - 2)
                if i >= 2:
                    act.wait_ge(S("centred"), cth + 1)
                    src = ps[:, 0, :]
                else:
                    wait()
                act.activation(sq[:, :], src, ACT.Square).then_inc(S("squared"), 1)
                if i >= 2:
                    act.wait_ge(S("var"), nth + 1)
                    act.activation(rs[:, :], ps[:, 1, :], ACT.Ln, bias=LN_EPS[:, 0:1]).then_inc(S("log"), 1)
                else:
                    act.wait_ge(S("guarded"), g * 2 + i + 1)
                    act.activation(rs[:, :], rs[:, :], ACT.Ln).then_inc(S("log"), 1)
                act.wait_ge(S("log"), nth + 1)
                act.activation(rs[:, :], rs[:, :], ACT.Exp, scale=-0.5).then_inc(S("rsqrt"), 1)

            def mamba(l, g):
                turn = g * 2 + l
                for m in range(HALF):
                    act.wait_ge(S("proj"), turn * 4 + m + 1)
                    act.activation(xp[:, m, :, CONV - 1:], seqs(ps[:, m, :]), ACT.Copy).then_inc(S("x_padded"), 1)
                for m in range(HALF):
                    act.wait_ge(S("proj"), turn * 4 + HALF + m + 1)
                    act.activation(sz[:, m, :], ps[:, HALF + m, :], ACT.Silu).then_inc(S("z_silu"), 1)
                for m in range(HALF):
                    act.wait_ge(S("conv"), turn * HALF + m + 1)
                    act.activation(u[:, m, :], cv[:, m, :], ACT.Silu,
                                   bias=W(f"conv_b{l}")[:, m:m + 1]).then_inc(S("u_ready"), 1)
                act.wait_ge(S("xdbl"), turn * 2 + 1)
                act.activation(dtl[:, :], ps[0:RANK, 4, :], ACT.Copy).then_inc(S("dtl"), 1)
                act.wait_ge(S("u_ready"), turn * HALF + HALF)
                for m in range(HALF):
                    ins = act.activation(yacc[:, m, :], u[:, m, :], ACT.Copy, scale=W(f"d{l}")[:, m:m + 1])
                ins.then_inc(S("seeded"), 1)
                for m in range(HALF):
                    act.wait_ge(S("dt_mm"), turn * HALF + m + 1)
                    ins = act.activation(ab[:, m, :], ps[:, 6 + m, :], ACT.Abs, bias=W(f"dt_b{l}")[:, m:m + 1])
                ins.then_inc(S("abs_z"), 1)
                act.wait_ge(S("abs_z"), turn + 1)
                act.activation(ab, ab, ACT.Exp, scale=-1.0).then_inc(S("exp_z"), 1)
                act.wait_ge(S("one_plus"), turn + 1)
                act.activation(lb, u1, ACT.Ln).then_inc(S("ln_z"), 1)
                act.wait_ge(S("delta"), turn + 1)
                for n in range(NS):
                    if n >= 2:
                        act.wait_ge(S("scan"), turn * NS + n - 1)
                    for m in range(HALF):
                        ins = act.activation(dA[:, n % 2, m, :, 1:], seqs(dl[:, m, :])[:, :, 1:], ACT.Exp,
                                             scale=a_neg[:, l, m, n:n + 1])
                    ins.then_inc(S("decay"), 1)

            def experts(l, g):
                for i in range(EXPERTS * SLICES):
                    e, f = divmod(i, SLICES)
                    act.wait_ge(S(f"up{l}"), g * 32 + i + 1)
                    if i >= 4:
                        act.wait_ge(S(f"down{l}"), g * 32 + i - 3)
                    act.activation(gelu[:, i % 4, :], ps[:, i % 2, :], ACT.Gelu).then_inc(S(f"gelu{l}"), 1)
                    if f == 3:
                        act.wait_ge(S(f"gate_spread{l}"), g * EXPERTS + e + 1)
                        if e >= 2:
                            act.wait_ge(S(f"weighted{l}"), g * EXPERTS + e - 1)
                        act.activation(gate_sb[:, e % 2, :], ps[:, 4 + e % 2, :],
                                       ACT.Copy).then_inc(S(f"gate_copied{l}"), 1)

            def attend(a, g, keys, halves, scale):
                steps = SEQ * halves
                per = 4 // halves
                parts = 2 if keys > 128 else 1
                blocks = per * parts
                turn = 0
                for k in range(steps):
                    act.wait_ge(S(f"shifted{a}"), g * steps + k + 1)
                    if k >= 2:
                        act.wait_ge(S(f"turn{a}"), g * steps * blocks + (k - 1) * blocks)
                    act.activation(pr[:, k % 2, 0:4 * per * keys], sc[:, k % 2, 0:4 * per * keys], ACT.Exp,
                                   scale=scale).then_inc(S(f"probs{a}"), 1)
                    for q in range(per):
                        for p in range(parts):
                            rows = (128 if p == 0 else keys - 128) if keys >= 128 else keys
                            act.wait_ge(S(f"turn{a}"), g * steps * blocks + turn + 1)
                            if turn >= 3:
                                act.wait_ge(S(f"product{a}"), g * steps * per + (turn - 3) // parts + 1)
                            act.activation(pt[0:rows, turn % 3, :, :],
                                           ps[0:rows, 4 + turn % 3, :].rearrange("p (a b) -> p a b", a=4),
                                           ACT.Copy).then_inc(S(f"turned{a}"), 1)
                            turn += 1

            act.wait_ge(S("params_in"), 16)
            for l in range(2):
                act.activation(a_neg[:, l, :, :].rearrange("p h n -> p (h n)"), W(f"a_log{l}"), ACT.Exp).then_inc(S("a_exp"), 1)
            act.activation(tmp[:, 0:1], W("temp"), ACT.Abs).then_inc(S("temp"), 1)
            act.wait_ge(S("temp"), 1)
            act.activation(tmp[:, 1:2], tmp[:, 0:1], ACT.Exp, scale=-1.0).then_inc(S("temp"), 1)
            act.wait_ge(S("temp"), 2)
            act.activation(tmp[:, 2:3], tmp[:, 1:2], ACT.Ln, bias=W("ones")[:, 0:1]).then_inc(S("temp"), 1)
            act.wait_ge(S("vector_setup"), 1)
            with act.Fori(0, GROUPS) as g:
                act.wait_ge(S("x_in"), g * 16 + 16)
                norm(0, g, x_in[:, :], lambda: None)
                mamba(0, g)
                norm(1, g, res[:, :], lambda: act.wait_ge(S("res1"), g + 1))
                act.wait_ge(S("gate_shift"), g + 1)
                act.activation(rl[:, 0:SEQ, 0:8], rl[:, 0:SEQ, 0:8], ACT.Exp).then_inc(S("gate_exp"), 1)
                experts(0, g)
                norm(2, g, None, None)
                act.wait_ge(S("q_mm_x"), g + 1)
                for i in range(4):
                    act.activation(qm[:, i, :], ps[:, 0, :], ACT.Identity, bias=bqm[:, i:i + 1],
                                   scale=W("head_mask")[:, i:i + 1]).then_inc(S("q_masked_x"), 1)
                attend("x", g, L + CTX, 2, DH ** -0.5)
                norm(3, g, None, None)
                act.wait_ge(S("q_mm_f"), g + 1)
                act.activation(qf[:, :], ps[:, 0, :], ACT.Identity, bias=W("fbq")).then_inc(S("q_biased"), 1)
                act.activation(sq[:, :], ps[:, 0, :], ACT.Square, bias=W("fbq")).then_inc(S("q_squared"), 1)
                act.wait_ge(S("q_norm"), g + 1)
                act.activation(rs[:, :], ps[:, 2, :], ACT.Ln).then_inc(S("q_log"), 1)
                act.wait_ge(S("q_log"), g + 1)
                act.activation(rs[:, :], rs[:, :], ACT.Exp, scale=-0.5).then_inc(S("q_rsqrt"), 1)
                attend("f", g, L, 1, DH ** -0.5)
                act.wait_ge(S("f_shift"), g + 1)
                act.activation(rl[:, 0:SEQ, :], rl[:, 0:SEQ, :], ACT.Exp).then_inc(S("f_exp"), 1)
                act.wait_ge(S("scaled_turned"), g + 1)
                act.activation(hT[:, :], ps[:, 5, :], ACT.Copy).then_inc(S("scaled_copied"), 1)
                norm(4, g, None, None)
                mamba(1, g)
                norm(5, g, None, None)
                attend("r", g, CTX, 1, 1.0)
                norm(6, g, None, None)
            act.wait_ge(S("pick_shift"), 1)
            act.activation(r1[:, :], r1[:, :], ACT.Exp).then_inc(S("pick_exp"), 1)
            with act.Fori(0, GROUPS) as g:
                experts(1, g)
                norm(7, g, None, None)

        @block.vector
        def _(dve):
            def norm(i, g, src, dst, ready):
                if i < NORMS:
                    nth, cth = g * NORMS + i, g * (NORMS - 2) + i - 2
                else:
                    nth, cth = g + GROUPS * NORMS, g + GROUPS * (NORMS - 2)
                if i < 2:
                    dve.wait_ge(S("var"), nth + 1)
                    dve.tensor_scalar(rs[:, :], ps[:, 1, :], 1e-24 / D, None, ALU.max).then_inc(S("guarded"), 1)
                else:
                    src = ps[:, 0, :]
                dve.wait_ge(S("rsqrt"), nth + 1)
                dve.tensor_tensor(dst, src, rs[:, :], ALU.mult).then_inc(S(ready), 1)

            def mamba(l, g, c):
                turn = g * 2 + l
                w = W(f"conv_w{l}")
                last = [None, None]
                for tap in range(CONV):
                    for m in range(HALF):
                        src = xp[:, m, :, tap:tap + L]
                        dst = seqs(cv[:, m, :])
                        coef = w[:, m * CONV + tap:m * CONV + tap + 1]
                        if tap == 0:
                            dve.wait_ge(S("x_padded"), turn * HALF + m + 1)
                            last[m] = c.mark(dve.tensor_scalar(dst, src, coef, None, ALU.mult))
                            continue
                        c.wait(last[m])
                        ins = dve.scalar_tensor_tensor(dst, src, coef, dst, ALU.mult, ALU.add)
                        if tap < CONV - 1:
                            last[m] = c.mark(ins)
                        else:
                            ins.then_inc(S("conv"), 1)
                dve.wait_ge(S("xdbl"), turn * 2 + 2)
                first = c.mark(dve.tensor_copy(bc_hi[:, :], ps[0:32, 5, :]))
                dve.tensor_copy(bcs[0:32, :], ps[0:32, 5, :])
                c.wait(first)
                c.link(dve.tensor_tensor(bc_r[:, :], ps[0:32, 5, :], bc_hi[:, :], ALU.subtract))
                second = c.mark(dve.tensor_copy(bc_hi[:, :], bc_r[:, :]))
                dve.tensor_copy(bcs[32:64, :], bc_r[:, :])
                c.wait(second)
                dve.tensor_tensor(bcs[64:96, :], bc_r[:, :], bc_hi[:, :], ALU.subtract).then_inc(S("bc_split"), 1)
                dve.wait_ge(S("abs_z"), turn + 1)
                for m in range(HALF):
                    c.mark(dve.tensor_scalar(rb[:, m, :], ps[:, 6 + m, :], W(f"dt_b{l}")[:, m:m + 1], 0.0,
                                                         ALU.add, ALU.max))
                dve.wait_ge(S("exp_z"), turn + 1)
                dve.tensor_scalar(u1, ab, 1.0, None, ALU.add).then_inc(S("one_plus"), 1)
                dve.wait_ge(S("one_plus"), turn + 1)
                c.link(dve.scalar_tensor_tensor(ab, u1, -1.0, ab, ALU.add, ALU.subtract))
                c.link(dve.tensor_tensor(rb, rb, ab, ALU.subtract))
                dve.wait_ge(S("ln_z"), turn + 1)
                dve.tensor_tensor(dl[:, :, :], rb, lb, ALU.add).then_inc(S("delta"), 1)
                dve.wait_ge(S("delta"), turn + 1)
                dve.wait_ge(S("u_ready"), turn * HALF + HALF)
                c.link(dve.tensor_tensor(dtu[:, :, :], dl[:, :, :], u[:, :, :], ALU.mult))

                def dbu(n):
                    dve.wait_ge(S("b_row"), turn * NS + n + 1)
                    dve.tensor_tensor(ps[:, DBU[n % 2], :], dtu[:, :, :], ps[:, 0:1, :].broadcast_to([128, HALF, TOK]),
                                      ALU.mult).then_inc(S("dbu"), 1)

                def scan(n):
                    dve.wait_ge(S("dbu"), turn * NS + n + 1)
                    dve.wait_ge(S("decay"), turn * NS + n + 1)
                    dve.tensor_tensor_scan(hs[:, n % 2, :], dA[:, n % 2, :, :, :].rearrange("p h s t -> p (h s t)"),
                                           ps[:, DBU[n % 2], :].rearrange("p h t -> p (h t)"), 0.0,
                                           ALU.mult, ALU.add).then_inc(S("scan"), 1)

                dbu(0)
                scan(0)
                for n in range(NS):
                    if n + 1 < NS:
                        dbu(n + 1)
                    dve.wait_ge(S("scan"), turn * NS + n + 1)
                    dve.wait_ge(S("c_row"), turn * NS + n + 1)
                    if n >= 2:
                        dve.wait_ge(S("summed"), turn * NS + n - 1)
                    dve.tensor_tensor(hc[:, n % 2, :, :], hs[:, n % 2, :].rearrange("p (h t) -> p h t", h=HALF),
                                      ps[:, 1:2, :].broadcast_to([128, HALF, TOK]), ALU.mult).then_inc(S("hc"), 1)
                    if n + 1 < NS:
                        scan(n + 1)
                dve.wait_ge(S("summed"), turn * NS + NS)
                dve.wait_ge(S("z_silu"), turn * HALF + HALF)
                dve.tensor_tensor(yacc[:, :, :], yacc[:, :, :], sz[:, :, :], ALU.mult).then_inc(S("gated"), 1)

            def experts(l, g, c, first):
                for e in range(EXPERTS):
                    dve.wait_ge(S(f"down{l}"), g * 32 + e * SLICES + SLICES)
                    dve.wait_ge(S(f"gate_copied{l}"), g * EXPERTS + e + 1)
                    dve.tensor_tensor(weighted, ps[:, 2 + e % 2, :], gate_sb[:, e % 2, :],
                                      ALU.mult).then_inc(S(f"weighted{l}"), 1)
                    dve.wait_ge(S(f"weighted{l}"), g * EXPERTS + e + 1)
                    ins = dve.tensor_tensor(res[:, :], weighted, first if e == 0 else res[:, :], ALU.add)
                    if e < EXPERTS - 1:
                        c.link(ins)
                    else:
                        ins.then_inc(S("res2" if l == 0 else "res7"), 1)

            def attend(a, g, keys, halves, c, done):
                steps = SEQ * halves
                per = 4 // halves
                width = 512 // per
                for k in range(steps):
                    j, half = divmod(k, halves)
                    n = 4 * per * keys
                    s = sc[:, k % 2, 0:n].rearrange("p (q i t) -> p q i t", q=4, i=per)
                    src = ps[:, 0:4, :].rearrange("p q (i t) -> p q i t", i=per)[:, :, :, 0:keys]
                    s3 = sc[:, k % 2, 0:n].rearrange("p (h t) -> p h t", t=keys)
                    top = mx[:, 0:4 * per]
                    dve.wait_ge(S(f"scores{a}"), g * steps + k + 1)
                    if k >= 2:
                        dve.wait_ge(S(f"probs{a}"), g * steps + k - 1)
                    if a == "r":
                        dve.tensor_tensor(s, src, mneg[:, :].unsqueeze(1).unsqueeze(1).broadcast_to([128, 4, per, keys]),
                                          ALU.add).then_inc(S(f"scores_read{a}"), 1)
                        dve.wait_ge(S(f"scores_read{a}"), g * steps + k + 1)
                        c.link(dve.tensor_reduce(top, s3, AX.X, ALU.max))
                        dve.tensor_tensor(s3, s3, top.unsqueeze(2).broadcast_to([128, 4 * per, keys]),
                                          ALU.subtract).then_inc(S(f"shifted{a}"), 1)
                    else:
                        c.link(dve.tensor_reduce(top.rearrange("p (q i) -> p q i", q=4), src, AX.X, ALU.max))
                        ins = dve.tensor_tensor(s, src, top.rearrange("p (q i) -> p q i", q=4).unsqueeze(3)
                                                .broadcast_to([128, 4, per, keys]), ALU.subtract)
                        ins.then_inc(S(f"shifted{a}"), 1)
                    if half == 0 and k:
                        finish(a, g, j - 1, halves, per, steps, c, done)
                finish(a, g, SEQ - 1, halves, per, steps, c, done)

            def finish(a, g, j, halves, per, steps, c, done):
                dve.wait_ge(S(f"product{a}"), g * steps * per + (j + 1) * halves * per)
                prod = ps[:, 7, 0:HEADS * (DH + 1)].rearrange("p (h d) -> p h d", d=DH + 1)
                c.link(dve.reciprocal(rec[:, :], prod[:, :, DH]))
                if a == "r":
                    c.link(dve.tensor_scalar(rec[:, :], rec[:, :], keep[:, 0:1], None, ALU.mult))
                dve.tensor_tensor(ot[:, j, :].rearrange("p (h d) -> p h d", d=DH), prod[:, :, 0:DH],
                                  rec[:, :].unsqueeze(2).broadcast_to([128, HEADS, DH]),
                                  ALU.mult).then_inc(S(f"normed{a}"), 1)
                dve.wait_ge(S(f"head_out{a}"), g * SEQ + j + 1)
                done(j)

            def top_two(tiles, c, values):
                dve.memset(idle[:, :], 0.0)
                for t in range(tiles):
                    m = c.mark(dve.max(v8[:, t, :], values[:, t, :]))
                c.wait(m)
                dve.memset(idle[:, :], 0.0)
                for t in range(tiles):
                    m = c.mark(dve.max_index(i8[:, t, :], v8[:, t, :], values[:, t, :]))
                c.wait(m)
                c.link(dve.tensor_copy(f8[:, 0:tiles, :], i8[:, 0:tiles, :]))

            c = Chain(dve, S("dve_setup"))
            dve.memset(LN_EPS[:, :], 1e-5)
            dve.memset(xp[:, :, :, 0:CONV - 1], 0.0)
            dve.memset(dA[:, :, :, :, 0:1], 0.0)
            dve.memset(va[:, :, :, DH:DH + 1], 1.0)
            dve.memset(vb[:, :, :, DH:DH + 1], 1.0)
            dve.wait_ge(S("params_in"), 16)
            dve.wait_ge(S("a_exp"), 2)
            dve.tensor_scalar(a_neg[:, :, :, :], a_neg[:, :, :, :], -1.0, None, ALU.mult)
            dve.tensor_scalar(bqm[:, :], W("head_mask"), W("xbq"), None, ALU.mult)
            dve.wait_ge(S("temp"), 3)
            c.link(dve.tensor_scalar(tmp[:, 3:4], W("temp"), 0.0, tmp[:, 2:3], ALU.max, ALU.add))
            dve.tensor_scalar(spm[:, :], W("head_mask"), tmp[:, 3:4], None, ALU.mult)
            dve.wait_ge(S("mask_in"), 16)
            c.link(dve.tensor_copy(mneg[:, :], mask8[:, :]))
            c.link(dve.tensor_reduce(keep[:, :], mneg[:, :], AX.X, ALU.min))
            dve.tensor_scalar(keep[:, :], keep[:, :], -1.0, 1.0, ALU.mult, ALU.add)
            dve.tensor_scalar(mneg[:, :], mneg[:, :], NEG, None, ALU.mult).then_inc(S("vector_setup"), 1)
            dve.wait_ge(S("vector_setup"), 1)

            with dve.Fori(0, GROUPS) as g:
                c = Chain(dve, S("dve_order"), g * DVE_LINKS)
                norm(0, g, x_in[:, :], xn[:, :], "n0")
                mamba(0, g, c)
                dve.wait_ge(S("mamba_out"), g * 2 + 1)
                dve.tensor_tensor(res[:, :], ps[:, 4, :], xn[:, :], ALU.add).then_inc(S("res1"), 1)
                norm(1, g, res[:, :], xm[:, :], "n1")
                dve.wait_ge(S("logits0"), g + 1)
                lg = rl[:, 0:SEQ, 0:EXPERTS]
                src = ps[:, 6, 0:SEQ * EXPERTS].rearrange("p (s e) -> p s e", s=SEQ)
                c.link(dve.tensor_reduce(r1[:, 0:SEQ], src, AX.X, ALU.max))
                dve.tensor_tensor(lg, src, r1[:, 0:SEQ].unsqueeze(2).broadcast_to([128, SEQ, EXPERTS]),
                                  ALU.subtract).then_inc(S("gate_shift"), 1)
                dve.wait_ge(S("gate_exp"), g + 1)
                c.link(dve.tensor_reduce(r1[:, 0:SEQ], lg, AX.X, ALU.add))
                c.link(dve.reciprocal(r2[:, 0:SEQ], r1[:, 0:SEQ]))
                c.link(dve.tensor_tensor(t8[:, 0:SEQ, :], lg, r2[:, 0:SEQ].unsqueeze(2).broadcast_to([128, SEQ, EXPERTS]),
                                         ALU.mult))
                top_two(SEQ, c, t8)
                c.link(dve.tensor_tensor(r1[:, 0:SEQ], v8[:, 0:SEQ, 0], v8[:, 0:SEQ, 1], ALU.add))
                c.link(dve.reciprocal(r2[:, 0:SEQ], r1[:, 0:SEQ]))
                c.link(dve.tensor_tensor(v8[:, 0:SEQ, 0:2], v8[:, 0:SEQ, 0:2],
                                         r2[:, 0:SEQ].unsqueeze(2).broadcast_to([128, SEQ, 2]), ALU.mult))
                iota = W("iota").unsqueeze(1).broadcast_to([128, SEQ, EXPERTS])
                for k, dst in ((0, gt[:, :, :]), (1, t8[:, 0:SEQ, :])):
                    c.link(dve.tensor_tensor(dst, f8[:, 0:SEQ, k:k + 1].broadcast_to([128, SEQ, EXPERTS]), iota,
                                             ALU.is_equal))
                    c.link(dve.tensor_tensor(dst, dst, v8[:, 0:SEQ, k:k + 1].broadcast_to([128, SEQ, EXPERTS]),
                                             ALU.mult))
                dve.tensor_tensor(gt[:, :, :], gt[:, :, :], t8[:, 0:SEQ, :], ALU.add).then_inc(S("gates0"), 1)
                dve.tensor_scalar(qf[:, :], x_in[:, :], 2.0, None, ALU.mult).then_inc(S("x_used"), 1)
                dve.wait_ge(S("x_used"), g + 1)
                experts(0, g, c, qf[:, :])
                norm(2, g, None, x1[:, :], "n2")
                dve.wait_ge(S("k_mm_x"), g * 2 + 1)
                dve.tensor_scalar(kt[:, :, 0:L], seqs(ps[:, 1, :]), W("xbk"), None, ALU.add)
                dve.wait_ge(S("k_mm_x"), g * 2 + 2)
                dve.tensor_scalar(kt[:, :, L:L + CTX], ps[:, 2, 0:SEQ * CTX].rearrange("p (s t) -> p s t", s=SEQ),
                                  W("xbk"), None, ALU.add)

                def value(bank, rows, dst, bias):
                    b = W(bias)[0:rows, :].rearrange("p (h d) -> p h d", d=DH)
                    for j in range(SEQ):
                        ins = dve.tensor_tensor(dst[0:rows, j, :, 0:DH],
                                                ps[0:rows, bank, j * D:(j + 1) * D].rearrange("p (h d) -> p h d", d=DH),
                                                b, ALU.add)
                    return ins

                dve.wait_ge(S("v_mm_x"), g * 2 + 1)
                value(3, L, va, "xbv")
                dve.wait_ge(S("v_mm_x"), g * 2 + 2)
                value(4, CTX, vb, "xbv").then_inc(S("qkv_x"), 1)

                def residual_x(j):
                    dve.tensor_tensor(res[:, j * L:(j + 1) * L], ps[:, 7, 256:256 + L], x1[:, j * L:(j + 1) * L],
                                      ALU.add).then_inc(S("res3"), 1)

                attend("x", g, L + CTX, 2, c, residual_x)
                norm(3, g, None, x2[:, :], "n3")

                dve.wait_ge(S("k_mm_f"), g + 1)
                dve.tensor_scalar(kt[:, :, 0:L], seqs(ps[:, 1, :]), W("fbk"), None, ALU.add)
                dve.wait_ge(S("v_mm_f"), g + 1)
                value(3, L, va, "fbv")
                dve.wait_ge(S("q_rsqrt"), g + 1)
                c.link(dve.tensor_tensor(qt[:, :], qf[:, :], rs[:, :], ALU.mult))
                for i in range(4):
                    ins = dve.tensor_scalar(qm[:, i, :], qt[:, :], W("qe"), spm[:, i:i + 1], ALU.add, ALU.mult)
                ins.then_inc(S("qkv_f"), 1)

                def keep_head(sem):
                    def done(j):
                        dve.tensor_copy(hT[:, j * L:(j + 1) * L], ps[:, 7, 256:256 + L]).then_inc(S(sem), 1)
                    return done

                attend("f", g, L, 1, c, keep_head("h_ready"))
                dve.wait_ge(S("logits_f"), g + 1)
                lg = rl[:, 0:SEQ, :]
                c.link(dve.tensor_tensor(lg, ps[:, 6, 0:SEQ * 17].rearrange("p (s e) -> p s e", s=SEQ),
                                         W("fbrs").unsqueeze(1).broadcast_to([128, SEQ, 17]), ALU.add))
                c.mark(dve.tensor_reduce(r1[:, 0:SEQ], rl[:, 0:SEQ, 0:ROUTED], AX.X, ALU.max))
                c.link(dve.tensor_reduce(r2[:, 0:SEQ], rl[:, 0:SEQ, ROUTED:], AX.X, ALU.max))
                c.mark(dve.tensor_tensor(rl[:, 0:SEQ, 0:ROUTED], rl[:, 0:SEQ, 0:ROUTED],
                                         r1[:, 0:SEQ].unsqueeze(2).broadcast_to([128, SEQ, ROUTED]), ALU.subtract))
                dve.tensor_tensor(rl[:, 0:SEQ, ROUTED:], rl[:, 0:SEQ, ROUTED:],
                                  r2[:, 0:SEQ].unsqueeze(2).broadcast_to([128, SEQ, SHARED]),
                                  ALU.subtract).then_inc(S("f_shift"), 1)
                dve.wait_ge(S("f_exp"), g + 1)
                dve.memset(idle[:, :], 0.0)
                for j in range(SEQ):
                    c.mark(dve.max(v8[:, j, :], rl[:, j, 0:ROUTED]))
                c.mark(dve.tensor_reduce(r1[:, 0:SEQ], rl[:, 0:SEQ, 0:ROUTED], AX.X, ALU.add))
                c.link(dve.tensor_reduce(r2[:, 0:SEQ], rl[:, 0:SEQ, ROUTED:], AX.X, ALU.add))
                c.mark(dve.reciprocal(r1[:, SEQ:2 * SEQ], r1[:, 0:SEQ]))
                c.mark(dve.reciprocal(r2[:, SEQ:2 * SEQ], r2[:, 0:SEQ]))
                c.link(dve.tensor_reduce(r1[:, 2 * SEQ:3 * SEQ], v8[:, 0:SEQ, 0:3], AX.X, ALU.add))
                c.mark(dve.tensor_tensor(r1[:, 0:SEQ], r1[:, 2 * SEQ:3 * SEQ], r1[:, SEQ:2 * SEQ], ALU.mult))
                c.link(dve.tensor_tensor(rl[:, 0:SEQ, ROUTED:], rl[:, 0:SEQ, ROUTED:],
                                         r2[:, SEQ:2 * SEQ].unsqueeze(2).broadcast_to([128, SEQ, SHARED]), ALU.mult))
                w0, w1 = rl[:, 0:SEQ, ROUTED], rl[:, 0:SEQ, ROUTED + 1]
                c.mark(dve.tensor_tensor(r2[:, 0:SEQ], w0, w1, ALU.add))
                c.link(dve.scalar_tensor_tensor(r1[:, 0:SEQ], r1[:, 0:SEQ], 6.0, w1, ALU.mult, ALU.mult))
                c.link(dve.scalar_tensor_tensor(r2[:, 0:SEQ], r2[:, 0:SEQ], 2.0, w0, ALU.mult, ALU.mult))
                c.link(dve.tensor_tensor(r1[:, 0:SEQ], r1[:, 0:SEQ], r2[:, 0:SEQ], ALU.add))
                dve.tensor_tensor(qm[:, :, 0:L], ot[:, :, :], r1[:, 0:SEQ].unsqueeze(2).broadcast_to([128, SEQ, L]),
                                  ALU.mult).then_inc(S("scaled_f"), 1)
                dve.wait_ge(S("proj_f"), g + 1)
                dve.scalar_tensor_tensor(res[:, :], ps[:, 4, :], W("fbp"), x2[:, :], ALU.add,
                                         ALU.add).then_inc(S("res4"), 1)
                norm(4, g, None, x3[:, :], "n4")

                mamba(1, g, c)
                dve.wait_ge(S("mamba_out"), g * 2 + 2)
                dve.tensor_tensor(res[:, :], ps[:, 4, :], x3[:, :], ALU.add).then_inc(S("res5"), 1)
                norm(5, g, None, x4[:, :], "n5")

                def rope(bank, n, bias, biass, a, b, dst):
                    src = ps[:, bank, 0:SEQ * n].rearrange("p (s t) -> p s t", s=SEQ)
                    swapped = ps[:, bank + 1, 0:SEQ * n].rearrange("p (s t) -> p s t", s=SEQ)
                    sin = W("rope_sin")[:, 0:n].unsqueeze(1).broadcast_to([128, SEQ, n])
                    cos = W("rope_cos")[:, 0:n].unsqueeze(1).broadcast_to([128, SEQ, n])
                    c.mark(dve.scalar_tensor_tensor(a, src, W(bias), sin, ALU.add, ALU.mult))
                    c.link(dve.scalar_tensor_tensor(b, swapped, W(biass), cos, ALU.add, ALU.mult))
                    c.link(dve.tensor_tensor(dst, a, b, ALU.subtract))

                dve.wait_ge(S("q_mm_r"), g + 1)
                rope(0, L, "rbq", "rbqs", seqs(qf[:, :]), seqs(qt[:, :]), seqs(qf[:, :]))
                for i in range(4):
                    dve.tensor_scalar(qm[:, i, :], qf[:, :], W("head_mask")[:, i:i + 1], None, ALU.mult)
                dve.wait_ge(S("k_mm_r"), g + 1)
                ka = qt[:, 0:SEQ * CTX].rearrange("p (s t) -> p s t", s=SEQ)
                kb = sq[:, 0:SEQ * CTX].rearrange("p (s t) -> p s t", s=SEQ)
                rope(2, CTX, "rbk", "rbks", ka, kb, kt[:, :, 0:CTX])
                dve.wait_ge(S("ctx_used"), g + 1)
                value(4, CTX, vb, "rbv").then_inc(S("qkv_r"), 1)
                attend("r", g, CTX, 1, c, keep_head("r_ready"))
                dve.wait_ge(S("proj_r"), g + 1)
                dve.scalar_tensor_tensor(res[:, :], ps[:, 4, :], W("rbo"), x4[:, :], ALU.add,
                                         ALU.add).then_inc(S("res6"), 1)
                norm(6, g, None, x5[:, bass.ts(g, TOK)], "n6")
                dve.wait_ge(S("n6"), g + 1)
                assert c.n == DVE_LINKS, c.n

            c = Chain(dve, S("dve_rank"))
            dve.wait_ge(S("logits1"), 1)
            c.link(dve.tensor_copy(t8[:, :, :], ps[:, 6, 0:TILES * EXPERTS].rearrange("p (t e) -> p t e", e=EXPERTS)))
            top_two(TILES, c, t8)
            dve.tensor_tensor(r1[:, :], v8[:, :, 1], v8[:, :, 0], ALU.subtract).then_inc(S("pick_shift"), 1)
            iota = W("iota").unsqueeze(1).broadcast_to([128, TILES, EXPERTS])
            for k in range(2):
                ins = dve.tensor_tensor(oh[:, :, k, :].rearrange("p e t -> p t e"),
                                        f8[:, :, k:k + 1].broadcast_to([128, TILES, EXPERTS]), iota, ALU.is_equal)
            ins.then_inc(S("picked"), 1)
            dve.wait_ge(S("pick_exp"), 1)
            c.link(dve.tensor_scalar(r2[:, :], r1[:, :], 1.0, None, ALU.add))
            c.link(dve.reciprocal(v8[:, :, 0], r2[:, :]))
            c.link(dve.tensor_tensor(v8[:, :, 1], v8[:, :, 0], r1[:, :], ALU.mult))
            dve.wait_ge(S("counted"), 1)
            flat = lambda t: t[:, :, :, :].rearrange("p e k t -> p (e k t)")
            c.link(dve.tensor_tensor_scan(flat(tot), W("scan_keep"), ps[:, 5, 0:256], 0.0, ALU.mult, ALU.add))
            c.link(dve.tensor_tensor(flat(rank), flat(tot), ps[:, 5, 0:256], ALU.subtract))
            c.link(dve.tensor_tensor(flat(rank), flat(rank), ps[:, 4, 0:256], ALU.add))
            c.link(dve.scalar_tensor_tensor(flat(rank), flat(rank), float(CAPACITY), flat(oh), ALU.is_le, ALU.mult))
            for k, dst in ((0, gt_all), (1, t8)):
                done = c.mark(dve.tensor_tensor(dst[:, :, :], rank[:, :, k, :].rearrange("p e t -> p t e"),
                                                v8[:, :, k:k + 1].broadcast_to([128, TILES, EXPERTS]), ALU.mult))
            c.wait(done)
            dve.tensor_tensor(gt_all[:, :, :], gt_all[:, :, :], t8[:, :, :], ALU.add).then_inc(S("ranked"), 1)
            dve.wait_ge(S("ranked"), 1)
            with dve.Fori(0, GROUPS) as g:
                c = Chain(dve, S("dve_order2"), g * DVE_LINKS_2)
                dve.tensor_copy(x5g[:, :], x5[:, bass.ts(g, TOK)]).then_inc(S("x5_group"), 1)
                dve.tensor_copy(gt[:, :, :], gt_all[:, bass.ts(g, SEQ), :]).then_inc(S("gates1"), 1)
                dve.wait_ge(S("x5_group"), g + 1)
                experts(1, g, c, x5g[:, :])
                dve.wait_ge(S("out_free"), g + 1)
                norm(7, g, None, yout[:, :], "out_ready")
                dve.wait_ge(S("out_ready"), g + 1)
                assert c.n == DVE_LINKS_2, c.n


_ORDER = ["x_t", "ctx_t", "params", "selectors", "w_in", "w_out", "mask"]


def _shape_constants():
    p = np.arange(128)
    f = np.float32
    c = {}
    c["ident"] = np.eye(128, dtype=f)
    c["mean"] = np.full((128, 128), 1.0 / D, f)
    c["center"] = (np.eye(128) - 1.0 / D).astype(f)
    c["head_ones"] = (p[:, None] // DH == p[None, :] // DH).astype(f)
    c["before"] = (p[:, None] <= p[None, :]).astype(f)
    c["ones"] = np.ones((128, 128), f)
    c["head_mask"] = ((p[:, None] // DH) % 4 == np.arange(4)[None, :]).astype(f)
    c["iota"] = np.broadcast_to(np.arange(EXPERTS, dtype=f), (128, EXPERTS))
    inv = np.exp(np.arange(0, DH, 2, dtype=f) * f(-(4.0 * np.log(f(10.0))) / DH)).astype(f)
    angle = (np.arange(L, dtype=f)[None, :] * inv[(p % DH) // 2][:, None]).astype(f)
    sign = np.where(p % 2 == 0, 1.0, -1.0).astype(f)[:, None]
    c["rope_sin"] = np.sin(angle).astype(f) * sign
    c["rope_cos"] = np.cos(angle).astype(f)
    c["scan_keep"] = np.broadcast_to((np.arange(EXPERTS * 2 * TILES) % (2 * TILES) != 0).astype(f),
                                     (128, EXPERTS * 2 * TILES))
    sel = np.zeros((96, 2 * NS, 128), f)
    for j in range(2 * NS):
        sel[[j, 32 + j, 64 + j], j, :] = 1.0
    return c, sel


def kernel(**inputs):
    import ml_dtypes
    import concourse.bacc as _bacc
    from concourse import mybir as _mybir
    from concourse.bass_utils import run_bass_kernel_spmd as _run

    a = {k: np.asarray(v) for k, v in inputs.items()}
    v, sel = _shape_constants()

    def halves(m):
        m = m.reshape(HALF, 128, -1)
        return np.concatenate([m[0], m[1]], axis=1)

    def col(m):
        return m.reshape(128, 1)

    def rows(m):
        return np.broadcast_to(m.reshape(1, -1), (128, m.size))

    def low(m):
        return np.concatenate([m, np.zeros((128 - m.shape[0], m.shape[1]), m.dtype)])

    swap = np.arange(D) ^ 1
    v["in_w0"], v["in_w1"] = a["L0_attn_in_proj_w"].T, a["L1_attn_W_in"]
    v["x_w0"], v["x_w1"] = halves(a["L0_attn_x_proj_w"].T), halves(a["L1_attn_W_x"])
    v["dt_w0"], v["dt_w1"] = low(a["L0_attn_dt_proj_w"].T), low(a["L1_attn_W_dt"])
    v["out_w0"], v["out_w1"] = halves(a["L0_attn_out_proj_w"].T), halves(a["L1_attn_W_out"])
    v["conv_w0"], v["conv_w1"] = halves(a["L0_attn_conv_w"].reshape(DI, CONV)), halves(a["L1_attn_conv_w"].T)
    for n, k0, k1 in (("conv_b", "conv_b", "conv_b"), ("dt_b", "dt_proj_b", "b_dt"), ("a_log", "A_log", "A_log"),
                      ("d", "D", "D")):
        v[n + "0"] = halves(a["L0_attn_" + k0].reshape(DI, -1))
        v[n + "1"] = halves(a["L1_attn_" + k1].reshape(DI, -1))
    v["gate0"], v["gate1"] = a["L0_attn_gate_w"].T, a["L1_ffn_w_g"]
    for n, p in (("x", "L0_xattn_"), ("f", "L0_ffn_"), ("r", "L1_xattn_")):
        for m in "qkv":
            v[n + m] = a[p + "W" + m].T
        v[n + "bq"], v[n + "bk"], v[n + "bv"] = col(a[p + "bq"]), col(a[p + "bk"]), rows(a[p + "bv"])
    for m in "qk":
        v["r" + m + "s"] = a["L1_xattn_W" + m][swap].T
        v["rb" + m + "s"] = col(a["L1_xattn_b" + m][swap])
    v["fp"], v["fbp"] = a["L0_ffn_Wp"].T, col(a["L0_ffn_bp"])
    v["ro"], v["rbo"] = a["L1_xattn_Wo"].T, col(a["L1_xattn_bo"])
    v["frs"] = np.concatenate([a["L0_ffn_Wr"], a["L0_ffn_Ws"]]).T
    v["fbrs"] = rows(np.concatenate([a["L0_ffn_br"], a["L0_ffn_bs"]]))
    v["temp"] = col(np.repeat(a["L0_ffn_temperature"].reshape(HEADS), DH))
    v["qe"] = col(a["L0_ffn_query_embedding"])
    w_in = np.stack([a["L0_attn_w1"].transpose(2, 0, 1), a["L1_ffn_c_fc"].transpose(1, 0, 2)], axis=1)
    w_out = np.stack([a["L0_attn_w2"].transpose(2, 0, 1).reshape(SLICES, 128, EXPERTS, D).transpose(1, 2, 0, 3),
                      a["L1_ffn_c_proj"].reshape(EXPERTS, SLICES, 128, D).transpose(2, 0, 1, 3)], axis=1)
    arrays = {
        "x_t": a["x"].reshape(B * L, D).T,
        "ctx_t": a["ctx_1024"].reshape(B * CTX, D).T,
        "params": np.concatenate([v[n] for n, _ in PARAMS], axis=1),
        "selectors": sel.astype(ml_dtypes.bfloat16),
        "w_in": w_in,
        "w_out": w_out,
        "mask": a["mask_1x1xSxS2_bk1"].reshape(L, CTX),
    }
    arrays = {k: np.ascontiguousarray(m) for k, m in arrays.items()}
    nc = _bacc.Bacc("TRN2", target_bir_lowering=False, num_devices=1)
    args = [nc.dram_tensor(n, arrays[n].shape, _mybir.dt.from_np(arrays[n].dtype), kind="ExternalInput").ap()
            for n in _ORDER]
    args.append(nc.dram_tensor("out", (D, B * L), F32, kind="ExternalOutput").ap())
    decoder_kernel(nc, *args)
    r = _run(nc, [arrays], core_ids=[0])
    return np.ascontiguousarray(r.results[0]["out"].T).reshape(B, L, D)
```

```python
from contextlib import ExitStack

import numpy as np

import concourse.bass as bass
from concourse import mybir

F32 = mybir.dt.float32
BF16 = mybir.dt.bfloat16
U32 = mybir.dt.uint32
U8 = mybir.dt.uint8
ALU = mybir.AluOpType
ACT = mybir.ActivationFunctionType
AX = mybir.AxisListType

B, L, D = 16, 128, 128
CTX = 77
SEQ = 4
TOK = SEQ * L
GROUPS = B // SEQ
DI, NS, RANK, CONV = 256, 16, 8, 4
HALF = DI // 128
HEADS, DH = 16, 8
EXPERTS, HID = 8, 512
SLICES = HID // 128
CAPACITY = 640
TILES = B
ROUTED, SHARED = 15, 2
VALUES_AT = 32
LOG_EXP = "natural_log_exp_and_others"
NEG = float(np.finfo(np.float32).min)

PARAMS = [
    ("in_w0", 2 * DI), ("in_w1", 2 * DI), ("x_w0", HALF * 40), ("x_w1", HALF * 40),
    ("dt_w0", DI), ("dt_w1", DI), ("out_w0", HALF * D), ("out_w1", HALF * D),
    ("conv_w0", HALF * CONV), ("conv_w1", HALF * CONV), ("conv_b0", HALF), ("conv_b1", HALF),
    ("dt_b0", HALF), ("dt_b1", HALF), ("a_log0", HALF * NS), ("a_log1", HALF * NS),
    ("d0", HALF), ("d1", HALF), ("gate0", EXPERTS), ("gate1", EXPERTS),
    ("xq", D), ("xk", D), ("xv", D), ("xbq", 1), ("xbk", 1), ("xbv", D),
    ("fq", D), ("fk", D), ("fv", D), ("fp", D), ("fbq", 1), ("fbk", 1), ("fbv", D), ("fbp", 1),
    ("frs", ROUTED + SHARED), ("fbrs", ROUTED + SHARED), ("temp", 1), ("qe", 1),
    ("rq", D), ("rqs", D), ("rk", D), ("rks", D), ("rv", D), ("ro", D),
    ("rbq", 1), ("rbqs", 1), ("rbk", 1), ("rbks", 1), ("rbv", D), ("rbo", 1),
    ("ident", 128), ("mean", 128), ("center", 128), ("head_ones", 128), ("before", 128), ("ones", 128),
    ("head_mask", 4), ("iota", EXPERTS), ("rope_sin", L), ("rope_cos", L), ("scan_keep", EXPERTS * 2 * TILES),
]
COLUMN = {}
WIDTH = 0
for _name, _cols in PARAMS:
    COLUMN[_name] = (WIDTH, WIDTH + _cols)
    WIDTH += _cols


class Chain:

    def __init__(self, engine, semaphore, base=0):
        self.engine, self.semaphore, self.base, self.n = engine, semaphore, base, 0

    def mark(self, instruction):
        instruction.then_inc(self.semaphore, 1)
        self.n += 1
        return self.n

    def wait(self, n):
        self.engine.wait_ge(self.semaphore, self.base + n)

    def link(self, instruction):
        self.wait(self.mark(instruction))


DVE_LINKS = 110
DVE_LINKS_2 = 7


def decoder_kernel(nc, x_t, ctx_t, params, selectors, w_in, w_out, mask, out):
    with ExitStack() as ctx:
        def sb(name, shape, dt=F32):
            return ctx.enter_context(nc.sbuf_tensor(name, shape, dt))

        semaphores = {}

        def S(name):
            if name not in semaphores:
                semaphores[name] = ctx.enter_context(nc.semaphore(name))
            return semaphores[name]

        ps = ctx.enter_context(nc.psum_tensor("ps", [128, 8, 512], F32))
        pw = sb("pw", [128, WIDTH])
        sel = sb("sel", [96, 2 * NS, 128], BF16)
        moe_in = sb("moe_in", [128, 2, EXPERTS, HID])
        moe_out = sb("moe_out", [128, 2, EXPERTS, SLICES, D])
        x_in = sb("x_in", [128, TOK])
        ctx_in = sb("ctx_in", [128, SEQ * CTX])
        xn = x1 = x3 = sb("odd_result", [128, TOK])
        xm = x2 = x4 = sb("even_result", [128, TOK])
        x5 = sb("x5", [128, B * L])
        res = sb("res", [128, TOK])
        sq = sb("sq", [128, TOK])
        rs = sb("rs", [128, TOK])
        xp = sb("xp", [128, HALF, SEQ, CONV - 1 + L])
        shared = sb("shared", [128, 6 * HALF * TOK])
        sz, cv, u, dl, dtu, yacc = (
            shared[:, i * HALF * TOK:(i + 1) * HALF * TOK].rearrange("p (h t) -> p h t", h=HALF) for i in range(6))
        bcs = sb("bcs", [96, TOK], BF16)
        bc_hi = sb("bc_hi", [32, TOK], BF16)
        bc_r, dtl = sq[0:32, :], rs[0:RANK, :]
        b_sb = (sq, rs)
        a_neg = sb("a_neg", [128, 2, HALF, NS])
        dA = sb("dA", [128, 2, HALF, SEQ, L])
        arena = sb("arena", [128, 4096])

        def part(a, n):
            return arena[:, a:a + n]

        ab = part(0, 1024).rearrange("p (h t) -> p h t", h=HALF)
        u1 = part(1024, 1024).rearrange("p (h t) -> p h t", h=HALF)
        lb = part(2048, 1024).rearrange("p (h t) -> p h t", h=HALF)
        rb = part(3072, 1024).rearrange("p (h t) -> p h t", h=HALF)
        hs = part(0, 2048).rearrange("p (s h t) -> p s h t", s=2, h=HALF)
        hc = part(2048, 2048).rearrange("p (s h t) -> p s h t", s=2, h=HALF)
        gelu = part(0, 2048).rearrange("p (s t) -> p s t", s=4)
        gate_sb = part(2048, 1024).rearrange("p (s t) -> p s t", s=2)
        weighted = part(3072, 512)
        pr = part(0, 4096).rearrange("p (s n) -> p s n", s=2)
        qm = shared[:, 0:4 * TOK].rearrange("p (i t) -> p i t", i=4)
        pt = shared[:, 2048:3584].rearrange("p (s a b) -> p s a b", s=3, a=4)
        qf, qt, hT = shared[:, 3584:4096], shared[:, 4096:4608], shared[:, 4608:5120]
        kt = shared[:, 5120:5120 + SEQ * (L + CTX)].rearrange("p (s t) -> p s t", s=SEQ)
        vp = sb("vp", [128, VALUES_AT + 2 * SEQ * HEADS * 64 + 24])
        vp_heads = vp[:, VALUES_AT:VALUES_AT + 2 * SEQ * HEADS * 64].rearrange("p (n s h c) -> p n s h c",
                                                                               n=2, s=SEQ, h=HEADS)
        mx = sb("mx", [128, HEADS])
        heads = sb("heads", [128, 2, 2 * L])
        den = sb("den", [128, L])
        rec = sb("rec", [128, L])
        keep_row = sb("keep_row", [128, L])
        bqm = sb("bqm", [128, 4])
        spm = sb("spm", [128, 4])
        tmp = sb("tmp", [128, 4])
        mask8 = sb("mask8", [128, CTX], U8)
        mneg = sb("mneg", [128, CTX])
        keep = sb("keep", [128, 1])
        rl = sb("rl", [128, SEQ, ROUTED + SHARED])
        r1 = sb("r1", [128, TILES])
        r2 = sb("r2", [128, TILES])
        v8, gt_all = (heads[:, i, 0:TILES * 8].rearrange("p (t e) -> p t e", e=8) for i in range(2))
        i8 = sb("i8", [128, TILES, 8], U32)
        f8, t8 = (b[:, :].rearrange("p (t e) -> p t e", e=8) for b in (rec, den))
        gt = sb("gt", [128, SEQ, EXPERTS])
        oh = part(0, 256).rearrange("p (e k t) -> p e k t", e=EXPERTS, k=2)
        tot = part(256, 256).rearrange("p (e k t) -> p e k t", e=EXPERTS, k=2)
        rank = part(512, 256).rearrange("p (e k t) -> p e k t", e=EXPERTS, k=2)
        x5g, yout = x1, x2

        def W(name):
            a, b = COLUMN[name]
            return pw[:, a:b]

        def head_values(n, j, rows):
            return vp_heads[0:rows, n, j, :, 24:24 + DH]

        def value_window(n, j, head, rows):
            quad, i = divmod(head, 4)
            at = VALUES_AT + ((n * SEQ + j) * HEADS + head) * 64 + 24 - 8 * i
            if quad % 2:
                at -= 32
            return vp[0:rows, at:at + 64]

        def held(quad):
            at = 64 * (quad // 2)
            odd = quad % 2
            return (slice(at + 32 * odd, at + 32 * odd + 32), slice(at + 32 - 32 * odd, at + 64 - 32 * odd),
                    slice(odd * L, (odd + 1) * L))

        PHASE = {"x": 0, "f": 1, "r": 2}

        def seqs(ap, width=L):
            return ap.rearrange("p (s t) -> p s t", s=SEQ)

        ident = W("ident")
        idle = sb("idle", [128, 1])
        LN_EPS = sb("ln_eps", [128, 1])

        block = ctx.enter_context(nc.Block())

        B_BANK, C_BANK = (0, 6), (1, 7)
        NORMS = 7

        @block.sync
        def _(sp):
            sp.dma_start(pw[:, :], params).then_inc(S("params_in"), 16)
            sp.dma_start(sel[:, :, :], selectors).then_inc(S("sel_in"), 16)
            sp.dma_start(mask8[:, :], mask).then_inc(S("mask_in"), 16)
            sp.dma_start(x_in[:, :], x_t[:, 0:TOK]).then_inc(S("x_in"), 16)
            sp.dma_start(ctx_in[:, :], ctx_t[:, 0:SEQ * CTX]).then_inc(S("ctx_in"), 16)
            with sp.Fori(1, GROUPS) as g:
                sp.wait_ge(S("x_used"), g)
                sp.dma_start(x_in[:, :], x_t[:, bass.ts(g, TOK)]).then_inc(S("x_in"), 16)
                sp.wait_ge(S("ctx_used"), g)
                sp.dma_start(ctx_in[:, :], ctx_t[:, bass.ts(g, SEQ * CTX)]).then_inc(S("ctx_in"), 16)
            sp.sem_inc(S("out_free"), 1)
            with sp.Fori(0, GROUPS) as g:
                sp.wait_ge(S("out_ready"), g + 1)
                sp.dma_start(out[:, bass.ts(g, TOK)], yout[:, :]).then_inc(S("stored"), 16)
                sp.wait_ge(S("stored"), g * 16 + 16)
                sp.sem_inc(S("out_free"), 1)

        @block.gpsimd
        def _(pool):
            for l in range(2):
                pool.dma_start(moe_in[:, l, :, :], w_in[:, l, :, :]).then_inc(S(f"moe_in{l}"), 16)
                pool.dma_start(moe_out[:, l, :, :, :], w_out[:, l, :, :, :]).then_inc(S(f"moe_in{l}"), 16)
            def head_rows(a, g):
                for j in range(SEQ):
                    nth = (g * 3 + PHASE[a]) * SEQ + j
                    now = slice(j * L, (j + 1) * L)
                    pool.wait_ge(S("sums_inverse"), nth + 1)
                    for quad in range(4):
                        top, bottom, cols = held(quad)
                        rows = slice(32 * quad, 32 * quad + 32)
                        ins = pool.tensor_tensor(hT[rows, now], heads[top, j % 2, cols], rec[rows, :], ALU.mult)
                    if a == "f":
                        ins.then_inc(S("head_done"), 1)
                        continue
                    ins.then_inc(S("head_over_sum"), 1)
                    pool.wait_ge(S("head_over_sum"), g * 2 * SEQ + (SEQ if a == "r" else 0) + j + 1)
                    if a == "x":
                        pool.tensor_tensor(res[:, now], hT[:, now], x1[:, now], ALU.add).then_inc(S("head_done"), 1)
                    else:
                        pool.tensor_tensor(hT[:, now], hT[:, now], keep_row[:, :],
                                           ALU.mult).then_inc(S("head_done"), 1)

            with pool.Fori(0, GROUPS) as g:
                for l in range(2):
                    turn = g * 2 + l
                    pool.wait_ge(S("dtu"), turn + 1)
                    for n in range(NS):
                        pool.wait_ge(S("b_copied"), turn * NS + n + 1)
                        if n >= 2:
                            pool.wait_ge(S("hc"), turn * NS + n - 1)
                        pool.tensor_tensor(hs[:, n % 2, :, :], dtu[:, :, :],
                                           b_sb[n % 2][:, :].unsqueeze(1).broadcast_to([128, HALF, TOK]),
                                           ALU.mult).then_inc(S("dbu"), 1)
                    for a in ("x", "f") if l == 0 else ("r",):
                        head_rows(a, g)

        @block.tensor
        def _(pe):
            def norm(i, g, src, gate):
                if i < NORMS:
                    nth, cth = g * NORMS + i, g * (NORMS - 2) + i - 2
                else:
                    nth, cth = g + GROUPS * NORMS, g + GROUPS * (NORMS - 2)
                if i >= 2:
                    gate()
                    pe.matmul(ps[:, 0, :], W("center"), src, start=True, stop=True).then_inc(S("centred"), 1)
                pe.wait_ge(S("squared"), nth + 1)
                pe.matmul(ps[:, 1, :], W("mean"), sq[:, :], start=True, stop=True).then_inc(S("var"), 1)

            def mamba(l, g, src):
                turn = g * 2 + l
                for m in range(4):
                    pe.matmul(ps[:, m, :], W(f"in_w{l}")[:, m * 128:(m + 1) * 128], src,
                              start=True, stop=True).then_inc(S("proj"), 1)
                pe.wait_ge(S("u_ready"), turn * HALF + HALF)
                for bank, a, n in ((4, 0, RANK), (5, RANK, 2 * NS)):
                    for h in range(HALF):
                        mm = pe.matmul(ps[0:n, bank, :], W(f"x_w{l}")[:, h * 40 + a:h * 40 + a + n], u[:, h, :],
                                       start=(h == 0), stop=(h == HALF - 1))
                    mm.then_inc(S("xdbl"), 1)
                pe.wait_ge(S("dtl"), turn + 1)
                for h in range(HALF):
                    pe.matmul(ps[:, 6 + h, :], W(f"dt_w{l}")[0:RANK, h * 128:(h + 1) * 128], dtl[:, :],
                              start=True, stop=True).then_inc(S("dt_mm"), 1)
                pe.wait_ge(S("bc_split"), turn + 1)
                pe.wait_ge(S("z_silu"), turn * HALF + HALF)
                def add_up(n):
                    for h in range(HALF):
                        mm = pe.matmul(ps[:, 4 + h, :], ident, yacc[:, h, :] if n < 0 else hc[:, n % 2, h, :],
                                       start=(n < 0), stop=(n == NS - 1))
                    mm.then_inc(S("summed"), 1)

                def b_row(n):
                    if n >= 2:
                        pe.wait_ge(S("b_copied"), turn * NS + n - 1)
                    pe.matmul(ps[:, B_BANK[n % 2], :], sel[:, n, :], bcs[:, :], start=True,
                              stop=True).then_inc(S("b_row"), 1)

                def c_row(n):
                    if n >= 2:
                        pe.wait_ge(S("hc"), turn * NS + n - 1)
                    pe.matmul(ps[:, C_BANK[n % 2], :], sel[:, NS + n, :], bcs[:, :], start=True,
                              stop=True).then_inc(S("c_row"), 1)

                b_row(0)
                c_row(0)
                pe.wait_ge(S("seeded"), turn + 1)
                add_up(-1)
                pe.wait_ge(S("dtu"), turn + 1)
                b_row(1)
                c_row(1)
                b_row(2)
                for n in range(NS - 1):
                    if n + 3 < NS:
                        b_row(n + 3)
                    if n + 2 < NS:
                        c_row(n + 2)
                    else:
                        pe.wait_ge(S("hc"), turn * NS + n + 1)
                    add_up(n)
                pe.wait_ge(S("hc"), turn * NS + NS)
                add_up(NS - 1)
                pe.wait_ge(S("gated"), turn + 1)
                for h in range(HALF):
                    mm = pe.matmul(ps[:, 4, :], W(f"out_w{l}")[:, h * D:(h + 1) * D], yacc[:, h, :],
                                   start=(h == 0), stop=(h == HALF - 1))
                mm.then_inc(S("mamba_out"), 1)

            def experts(l, g, src, gates_ready):
                def down(i):
                    e, f = divmod(i, SLICES)
                    pe.wait_ge(S(f"gelu{l}"), g * 32 + i + 1)
                    if f == 0 and e >= 2:
                        pe.wait_ge(S(f"weighted{l}"), g * EXPERTS + e - 1)
                    mm = pe.matmul(ps[:, 2 + e % 2, :], moe_out[:, l, e, f, :], gelu[:, i % 4, :],
                                   start=(f == 0), stop=(f == SLICES - 1))
                    mm.then_inc(S(f"down{l}"), 1)

                def spread(e):
                    if e == 0:
                        gates_ready()
                    if e >= 2:
                        pe.wait_ge(S(f"gate_copied{l}"), g * EXPERTS + e - 1)
                    for j in range(SEQ):
                        mm = pe.matmul(ps[:, 4 + e % 2, j * L:(j + 1) * L],
                                       gt[:, j, e:e + 1].to_broadcast([128, 128]), ident, start=True, stop=True)
                    mm.then_inc(S(f"gate_spread{l}"), 1)

                for i in range(EXPERTS * SLICES):
                    e, f = divmod(i, SLICES)
                    if i >= 2:
                        pe.wait_ge(S(f"gelu{l}"), g * 32 + i - 1)
                    pe.matmul(ps[:, i % 2, :], moe_in[:, l, e, f * 128:(f + 1) * 128], src,
                              start=True, stop=True).then_inc(S(f"up{l}"), 1)
                    if i:
                        down(i - 1)
                    if f == 2:
                        spread(e)
                down(EXPERTS * SLICES - 1)

            def values(src, n, bank, w, rows):
                for j in range(SEQ):
                    mm = pe.matmul(ps[0:rows, bank, j * D:(j + 1) * D], src[:, j * rows:(j + 1) * rows], w,
                                   start=True, stop=True)
                mm.then_inc(S(n), 1)

            def attend(a, g, keys, halves):
                steps = SEQ * halves
                quads = 4 // halves
                per_bank = quads
                width = 512 // per_bank
                parts = {"x": ((0, 0, L), (1, L, CTX)), "f": ((0, 0, L),), "r": ((1, 0, CTX),)}[a]
                blocks = [(k, q, n, at, rows) for k in range(steps) for q in range(quads) for n, at, rows in parts]
                per_step = quads * len(parts)
                base = g * steps * per_step

                def scores(k, part):
                    j, half = divmod(k, halves)
                    if k:
                        pe.wait_ge(S("scores_readr" if a == "r" else f"shifted{a}"), (g * steps + k - 1) * 2 + part + 1)
                    for local in range(part * 2 * per_bank, (part + 1) * 2 * per_bank):
                        quad, i = divmod(half * quads * 4 + local, 4)
                        bank, at = divmod(local, per_bank)
                        p = slice(32 * quad, 32 * quad + 32)
                        mm = pe.matmul(ps[:, bank, at * width:at * width + keys],
                                       qm[p, i, j * L:(j + 1) * L], kt[p, j, 0:keys], start=True, stop=True)
                    mm.then_inc(S(f"scores{a}"), 1)

                def turn(b):
                    k, q, n, at, rows = blocks[b]
                    if b % (per_step // 2) == 0:
                        pe.wait_ge(S(f"probs{a}"), (g * steps + k) * 2 + 1 + (b % per_step > 0))
                    if b >= 3:
                        pe.wait_ge(S(f"turned{a}"), base + b - 2)
                    for i in range(4):
                        c = (q * 4 + i) * keys + at
                        mm = pe.transpose(ps[0:rows, 4 + b % 3, i * 128:(i + 1) * 128],
                                          pr[:, k % 2, c:c + rows], ident)
                    mm.then_inc(S(f"turn{a}"), 1)

                def product(b):
                    k, q, n, at, rows = blocks[b]
                    j, half = divmod(k, halves)
                    quad = half * quads + q
                    pe.wait_ge(S(f"turned{a}"), base + b + 1)
                    if j and b % (halves * per_step) == 0:
                        pe.wait_ge(S("heads"), (g * 3 + PHASE[a]) * SEQ + j)
                    at = 64 * (quad // 2)
                    for i in range(4):
                        mm = pe.matmul(ps[at:at + 64, 7, (quad % 2) * L:(quad % 2 + 1) * L],
                                       value_window(n, j, 4 * quad + i, rows), pt[0:rows, b % 3, i, :],
                                       start=(i == 0 and n == parts[0][0]), stop=(i == 3 and n == parts[-1][0]))
                    mm.then_inc(S(f"product{a}"), 1)

                for k in range(2):
                    for part in range(2):
                        scores(k, part)
                for b in range(len(blocks) + 2):
                    if b < len(blocks):
                        turn(b)
                    if b >= 2:
                        product(b - 2)
                    k, w = divmod(b, per_step)
                    if w >= 2 and k + 2 < steps:
                        scores(k + 2, w - 2)

            pe.wait_ge(S("params_in"), 16)
            pe.wait_ge(S("sel_in"), 16)
            pe.wait_ge(S("keep"), 1)
            pe.matmul(ps[:, 7, 0:L], keep[:, 0:1].to_broadcast([128, 128]), ident,
                      start=True, stop=True).then_inc(S("keep_spread"), 1)
            with pe.Fori(0, GROUPS) as g:
                norm(0, g, None, None)
                pe.wait_ge(S("n0"), g + 1)
                mamba(0, g, xn[:, :])
                norm(1, g, None, None)
                pe.wait_ge(S("n1"), g + 1)
                for j in range(SEQ):
                    mm = pe.matmul(ps[:, 6, j * EXPERTS:(j + 1) * EXPERTS], xm[:, j * L:(j + 1) * L], W("gate0"),
                                   start=True, stop=True)
                mm.then_inc(S("logits0"), 1)
                pe.wait_ge(S("moe_in0"), 32)
                experts(0, g, xm[:, :], lambda: pe.wait_ge(S("gates0"), g + 1))
                norm(2, g, res[:, :], lambda: pe.wait_ge(S("res2"), g + 1))
                pe.wait_ge(S("n2"), g + 1)
                pe.matmul(ps[:, 0, :], W("xq"), x1[:, :], start=True, stop=True).then_inc(S("q_mm_x"), 1)
                pe.matmul(ps[:, 1, :], W("xk"), x1[:, :], start=True, stop=True).then_inc(S("k_mm_x"), 1)
                pe.wait_ge(S("ctx_in"), g * 16 + 16)
                pe.matmul(ps[:, 2, 0:SEQ * CTX], W("xk"), ctx_in[:, :], start=True, stop=True).then_inc(S("k_mm_x"), 1)
                values(x1[:, :], "v_mm_x", 3, W("xv"), L)
                values(ctx_in[:, :], "v_mm_x", 4, W("xv"), CTX)
                pe.wait_ge(S("qkv_x"), g + 1)
                pe.wait_ge(S("q_masked_x"), g * 4 + 4)
                attend("x", g, L + CTX, 2)
                norm(3, g, res[:, :], lambda: pe.wait_ge(S("head_done"), (g * 3 + 0) * SEQ + SEQ))
                pe.wait_ge(S("n3"), g + 1)
                pe.matmul(ps[:, 0, :], W("fq"), x2[:, :], start=True, stop=True).then_inc(S("q_mm_f"), 1)
                pe.matmul(ps[:, 1, :], W("fk"), x2[:, :], start=True, stop=True).then_inc(S("k_mm_f"), 1)
                values(x2[:, :], "v_mm_f", 3, W("fv"), L)
                pe.wait_ge(S("q_squared"), g + 1)
                pe.matmul(ps[:, 2, :], W("head_ones"), sq[:, :], start=True, stop=True).then_inc(S("q_norm"), 1)
                pe.wait_ge(S("qkv_f"), g + 1)
                attend("f", g, L, 1)
                pe.wait_ge(S("head_done"), (g * 3 + 1) * SEQ + SEQ)
                for j in range(SEQ):
                    mm = pe.matmul(ps[:, 6, j * 17:(j + 1) * 17], hT[:, j * L:(j + 1) * L], W("frs"),
                                   start=True, stop=True)
                mm.then_inc(S("logits_f"), 1)
                pe.wait_ge(S("gates_f"), g + 1)
                for j in range(SEQ):
                    mm = pe.matmul(ps[:, 5, j * L:(j + 1) * L], r1[:, j:j + 1].to_broadcast([128, 128]), ident,
                                   start=True, stop=True)
                mm.then_inc(S("gates_f_spread"), 1)
                pe.wait_ge(S("gated_f"), g + 1)
                pe.matmul(ps[:, 4, :], W("fp"), qt[:, :], start=True, stop=True).then_inc(S("proj_f"), 1)
                norm(4, g, res[:, :], lambda: pe.wait_ge(S("res4"), g + 1))
                pe.wait_ge(S("n4"), g + 1)
                mamba(1, g, x3[:, :])
                norm(5, g, res[:, :], lambda: pe.wait_ge(S("res5"), g + 1))
                pe.wait_ge(S("n5"), g + 1)
                pe.matmul(ps[:, 0, :], W("rq"), x4[:, :], start=True, stop=True)
                pe.matmul(ps[:, 1, :], W("rqs"), x4[:, :], start=True, stop=True).then_inc(S("q_mm_r"), 1)
                pe.matmul(ps[:, 2, 0:SEQ * CTX], W("rk"), ctx_in[:, :], start=True, stop=True)
                pe.matmul(ps[:, 3, 0:SEQ * CTX], W("rks"), ctx_in[:, :], start=True, stop=True).then_inc(S("k_mm_r"), 1)
                values(ctx_in[:, :], "ctx_used", 4, W("rv"), CTX)
                pe.wait_ge(S("qkv_r"), g + 1)
                attend("r", g, CTX, 1)
                pe.wait_ge(S("head_done"), (g * 3 + 2) * SEQ + SEQ)
                pe.matmul(ps[:, 4, :], W("ro"), hT[:, :], start=True, stop=True).then_inc(S("proj_r"), 1)
                norm(6, g, res[:, :], lambda: pe.wait_ge(S("res6"), g + 1))
            pe.wait_ge(S("n6"), GROUPS)
            for t in range(TILES):
                mm = pe.matmul(ps[:, 6, t * EXPERTS:(t + 1) * EXPERTS], x5[:, t * L:(t + 1) * L], W("gate1"),
                               start=True, stop=True)
            mm.then_inc(S("logits1"), 1)
            pe.wait_ge(S("picked"), 1)
            picks = oh[:, :, :, :].rearrange("p e k t -> p (e k t)")
            pe.matmul(ps[:, 4, 0:256], W("before"), picks, start=True, stop=True)
            pe.matmul(ps[:, 5, 0:256], W("ones"), picks, start=True, stop=True).then_inc(S("counted"), 1)
            pe.wait_ge(S("moe_in1"), 32)
            pe.wait_ge(S("ranked"), 1)
            with pe.Fori(0, GROUPS) as g:
                pe.wait_ge(S("x5_group"), g + 1)
                experts(1, g, x5g[:, :], lambda: pe.wait_ge(S("gates1"), g + 1))
                norm(7, g, res[:, :], lambda: pe.wait_ge(S("res7"), g + 1))

        @block.scalar
        def _(act):
            def norm(i, g, src, wait):
                if i < NORMS:
                    nth, cth = g * NORMS + i, g * (NORMS - 2) + i - 2
                else:
                    nth, cth = g + GROUPS * NORMS, g + GROUPS * (NORMS - 2)
                if i >= 2:
                    act.wait_ge(S("centred"), cth + 1)
                    src = ps[:, 0, :]
                else:
                    wait()
                act.activation(sq[:, :], src, ACT.Square).then_inc(S("squared"), 1)
                if i >= 2:
                    act.wait_ge(S("var"), nth + 1)
                    act.activation(rs[:, :], ps[:, 1, :], ACT.Ln, bias=LN_EPS[:, 0:1]).then_inc(S("log"), 1)
                else:
                    act.wait_ge(S("guarded"), g * 2 + i + 1)
                    act.activation(rs[:, :], rs[:, :], ACT.Ln).then_inc(S("log"), 1)
                act.wait_ge(S("log"), nth + 1)
                act.activation(rs[:, :], rs[:, :], ACT.Exp, scale=-0.5).then_inc(S("rsqrt"), 1)

            def mamba(l, g):
                turn = g * 2 + l
                for m in range(HALF):
                    act.wait_ge(S("proj"), turn * 4 + m + 1)
                    act.activation(xp[:, m, :, CONV - 1:], seqs(ps[:, m, :]), ACT.Copy).then_inc(S("x_padded"), 1)
                for m in range(HALF):
                    act.wait_ge(S("proj"), turn * 4 + HALF + m + 1)
                    act.activation(sz[:, m, :], ps[:, HALF + m, :], ACT.Silu).then_inc(S("z_silu"), 1)
                for m in range(HALF):
                    act.wait_ge(S("conv"), turn * HALF + m + 1)
                    act.activation(u[:, m, :], cv[:, m, :], ACT.Silu,
                                   bias=W(f"conv_b{l}")[:, m:m + 1]).then_inc(S("u_ready"), 1)
                act.preload_act_table_set(LOG_EXP)
                act.wait_ge(S("xdbl"), turn * 2 + 1)
                act.activation(dtl[:, :], ps[0:RANK, 4, :], ACT.Copy).then_inc(S("dtl"), 1)
                act.wait_ge(S("u_ready"), turn * HALF + HALF)
                for m in range(HALF):
                    ins = act.activation(yacc[:, m, :], u[:, m, :], ACT.Copy, scale=W(f"d{l}")[:, m:m + 1])
                ins.then_inc(S("seeded"), 1)
                for m in range(HALF):
                    act.wait_ge(S("dt_mm"), turn * HALF + m + 1)
                    ins = act.activation(ab[:, m, :], ps[:, 6 + m, :], ACT.Abs, bias=W(f"dt_b{l}")[:, m:m + 1])
                ins.then_inc(S("abs_z"), 1)
                act.wait_ge(S("abs_z"), turn + 1)
                act.activation(ab, ab, ACT.Exp, scale=-1.0).then_inc(S("exp_z"), 1)
                act.preload_act_table_set("natural_log")
                act.wait_ge(S("one_plus"), turn + 1)
                act.activation(lb, u1, ACT.Ln).then_inc(S("ln_z"), 1)
                act.preload_act_table_set(LOG_EXP)
                act.wait_ge(S("delta"), turn + 1)
                def copy_b(n):
                    act.wait_ge(S("b_row"), turn * NS + n + 1)
                    if n >= 2:
                        act.wait_ge(S("dbu"), turn * NS + n - 1)
                    act.activation(b_sb[n % 2][:, :], ps[:, B_BANK[n % 2], :], ACT.Copy).then_inc(S("b_copied"), 1)

                copy_b(0)
                for n in range(NS):
                    if n + 1 < NS:
                        copy_b(n + 1)
                    if n >= 2:
                        act.wait_ge(S("scan"), turn * NS + n - 1)
                    for m in range(HALF):
                        ins = act.activation(dA[:, n % 2, m, :, 1:], seqs(dl[:, m, :])[:, :, 1:], ACT.Exp,
                                             scale=a_neg[:, l, m, n:n + 1])
                    ins.then_inc(S("decay"), 1)

            def experts(l, g):
                for i in range(EXPERTS * SLICES):
                    e, f = divmod(i, SLICES)
                    act.wait_ge(S(f"up{l}"), g * 32 + i + 1)
                    if i >= 4:
                        act.wait_ge(S(f"down{l}"), g * 32 + i - 3)
                    act.activation(gelu[:, i % 4, :], ps[:, i % 2, :], ACT.Gelu).then_inc(S(f"gelu{l}"), 1)
                    if f == 3:
                        act.wait_ge(S(f"gate_spread{l}"), g * EXPERTS + e + 1)
                        if e >= 2:
                            act.wait_ge(S(f"weighted{l}"), g * EXPERTS + e - 1)
                        act.activation(gate_sb[:, e % 2, :], ps[:, 4 + e % 2, :],
                                       ACT.Copy).then_inc(S(f"gate_copied{l}"), 1)
                act.preload_act_table_set(LOG_EXP)

            def attend(a, g, keys, halves, scale):
                steps = SEQ * halves
                per = 4 // halves
                parts = {"x": (L, CTX), "f": (L,), "r": (CTX,)}[a]
                blocks = [(k, rows) for k in range(steps) for q in range(per) for rows in parts]
                per_step = per * len(parts)
                base = g * steps * per_step

                def exps(k, part):
                    act.wait_ge(S(f"shifted{a}"), (g * steps + k) * 2 + part + 1)
                    s = pr[:, k % 2, part * 2 * per * keys:(part + 1) * 2 * per * keys]
                    act.activation(s, s, ACT.Exp, scale=scale).then_inc(S(f"probs{a}"), 1)

                exps(0, 0)
                exps(0, 1)
                for b in range(len(blocks) + 2):
                    if b < len(blocks):
                        rows = blocks[b][1]
                        act.wait_ge(S(f"turn{a}"), base + b + 1)
                        if b >= 3:
                            act.wait_ge(S(f"product{a}"), base + b - 2)
                        act.activation(pt[0:rows, b % 3, :, :],
                                       ps[0:rows, 4 + b % 3, :].rearrange("p (a b) -> p a b", a=4),
                                       ACT.Copy).then_inc(S(f"turned{a}"), 1)
                    k, w = divmod(b, per_step)
                    if w == 1 and k % halves == 0 and k:
                        j = k // halves - 1
                        act.wait_ge(S(f"product{a}"), base + k * per_step)
                        if j >= 2:
                            act.wait_ge(S("head_done"), (g * 3 + PHASE[a]) * SEQ + j - 1)
                        act.activation(heads[:, j % 2, :], ps[:, 7, 0:2 * L], ACT.Copy).then_inc(S("heads"), 1)
                    if w == (3 if k < steps else 1) and k % halves == 0 and k:
                        j = k // halves - 1
                        nth = (g * 3 + PHASE[a]) * SEQ + j
                        act.wait_ge(S("heads"), nth + 1)
                        if j:
                            act.wait_ge(S("sums_inverse"), nth)
                        for quad in range(4):
                            top, bottom, cols = held(quad)
                            ins = act.activation(den[32 * quad:32 * quad + 32, :], heads[bottom, j % 2, cols], ACT.Copy)
                        ins.then_inc(S("sums"), 1)
                    if w in (1, 2) and k + 1 < steps:
                        exps(k + 1, w - 1)

            act.preload_act_table_set(LOG_EXP)
            act.wait_ge(S("params_in"), 16)
            for l in range(2):
                act.activation(a_neg[:, l, :, :].rearrange("p h n -> p (h n)"), W(f"a_log{l}"), ACT.Exp).then_inc(S("a_exp"), 1)
            act.activation(tmp[:, 0:1], W("temp"), ACT.Abs).then_inc(S("temp"), 1)
            act.wait_ge(S("temp"), 1)
            act.activation(tmp[:, 1:2], tmp[:, 0:1], ACT.Exp, scale=-1.0).then_inc(S("temp"), 1)
            act.wait_ge(S("temp"), 2)
            act.activation(tmp[:, 2:3], tmp[:, 1:2], ACT.Ln, bias=W("ones")[:, 0:1]).then_inc(S("temp"), 1)
            act.wait_ge(S("vector_setup"), 1)
            with act.Fori(0, GROUPS) as g:
                act.wait_ge(S("x_in"), g * 16 + 16)
                norm(0, g, x_in[:, :], lambda: None)
                mamba(0, g)
                norm(1, g, res[:, :], lambda: act.wait_ge(S("res1"), g + 1))
                act.wait_ge(S("gate_shift"), g + 1)
                act.activation(rl[:, 0:SEQ, 0:8], rl[:, 0:SEQ, 0:8], ACT.Exp).then_inc(S("gate_exp"), 1)
                experts(0, g)
                norm(2, g, None, None)
                act.wait_ge(S("q_mm_x"), g + 1)
                for i in range(4):
                    act.activation(qm[:, i, :], ps[:, 0, :], ACT.Identity, bias=bqm[:, i:i + 1],
                                   scale=W("head_mask")[:, i:i + 1]).then_inc(S("q_masked_x"), 1)
                attend("x", g, L + CTX, 2, DH ** -0.5)
                norm(3, g, None, None)
                act.wait_ge(S("q_mm_f"), g + 1)
                act.activation(qf[:, :], ps[:, 0, :], ACT.Identity, bias=W("fbq")).then_inc(S("q_biased"), 1)
                act.activation(sq[:, :], ps[:, 0, :], ACT.Square, bias=W("fbq")).then_inc(S("q_squared"), 1)
                act.wait_ge(S("q_norm"), g + 1)
                act.activation(rs[:, :], ps[:, 2, :], ACT.Ln).then_inc(S("q_log"), 1)
                act.wait_ge(S("q_log"), g + 1)
                act.activation(rs[:, :], rs[:, :], ACT.Exp, scale=-0.5).then_inc(S("q_rsqrt"), 1)
                attend("f", g, L, 1, DH ** -0.5)
                act.wait_ge(S("f_shift"), g + 1)
                act.activation(rl[:, 0:SEQ, :], rl[:, 0:SEQ, :], ACT.Exp).then_inc(S("f_exp"), 1)
                norm(4, g, None, None)
                mamba(1, g)
                norm(5, g, None, None)
                attend("r", g, CTX, 1, 1.0)
                norm(6, g, None, None)
            act.wait_ge(S("pick_shift"), 1)
            act.activation(r1[:, :], r1[:, :], ACT.Exp).then_inc(S("pick_exp"), 1)
            with act.Fori(0, GROUPS) as g:
                experts(1, g)
                norm(7, g, None, None)

        @block.vector
        def _(dve):
            def norm(i, g, src, dst, ready):
                if i < NORMS:
                    nth, cth = g * NORMS + i, g * (NORMS - 2) + i - 2
                else:
                    nth, cth = g + GROUPS * NORMS, g + GROUPS * (NORMS - 2)
                if i < 2:
                    dve.wait_ge(S("var"), nth + 1)
                    dve.tensor_scalar(rs[:, :], ps[:, 1, :], 1e-24 / D, None, ALU.max).then_inc(S("guarded"), 1)
                else:
                    src = ps[:, 0, :]
                dve.wait_ge(S("rsqrt"), nth + 1)
                dve.tensor_tensor(dst, src, rs[:, :], ALU.mult).then_inc(S(ready), 1)

            def mamba(l, g, c):
                turn = g * 2 + l
                w = W(f"conv_w{l}")
                last = [None, None]
                for tap in range(CONV):
                    for m in range(HALF):
                        src = xp[:, m, :, tap:tap + L]
                        dst = seqs(cv[:, m, :])
                        coef = w[:, m * CONV + tap:m * CONV + tap + 1]
                        if tap == 0:
                            dve.wait_ge(S("x_padded"), turn * HALF + m + 1)
                            last[m] = c.mark(dve.tensor_scalar(dst, src, coef, None, ALU.mult))
                            continue
                        c.wait(last[m])
                        ins = dve.scalar_tensor_tensor(dst, src, coef, dst, ALU.mult, ALU.add)
                        if tap < CONV - 1:
                            last[m] = c.mark(ins)
                        else:
                            ins.then_inc(S("conv"), 1)
                dve.wait_ge(S("xdbl"), turn * 2 + 2)
                first = c.mark(dve.tensor_copy(bc_hi[:, :], ps[0:32, 5, :]))
                dve.tensor_copy(bcs[0:32, :], ps[0:32, 5, :])
                c.wait(first)
                c.link(dve.tensor_tensor(bc_r[:, :], ps[0:32, 5, :], bc_hi[:, :], ALU.subtract))
                second = c.mark(dve.tensor_copy(bc_hi[:, :], bc_r[:, :]))
                dve.tensor_copy(bcs[32:64, :], bc_r[:, :])
                c.wait(second)
                dve.tensor_tensor(bcs[64:96, :], bc_r[:, :], bc_hi[:, :], ALU.subtract).then_inc(S("bc_split"), 1)
                dve.wait_ge(S("abs_z"), turn + 1)
                for m in range(HALF):
                    c.mark(dve.tensor_scalar(rb[:, m, :], ps[:, 6 + m, :], W(f"dt_b{l}")[:, m:m + 1], 0.0,
                                                         ALU.add, ALU.max))
                dve.wait_ge(S("exp_z"), turn + 1)
                dve.tensor_scalar(u1, ab, 1.0, None, ALU.add).then_inc(S("one_plus"), 1)
                dve.wait_ge(S("one_plus"), turn + 1)
                c.link(dve.scalar_tensor_tensor(ab, u1, -1.0, ab, ALU.add, ALU.subtract))
                c.link(dve.tensor_tensor(rb, rb, ab, ALU.subtract))
                dve.wait_ge(S("ln_z"), turn + 1)
                dve.tensor_tensor(dl[:, :, :], rb, lb, ALU.add).then_inc(S("delta"), 1)
                dve.wait_ge(S("delta"), turn + 1)
                dve.wait_ge(S("u_ready"), turn * HALF + HALF)
                dve.tensor_tensor(dtu[:, :, :], dl[:, :, :], u[:, :, :], ALU.mult).then_inc(S("dtu"), 1)

                for n in range(NS):
                    dve.wait_ge(S("dbu"), turn * NS + n + 1)
                    dve.wait_ge(S("decay"), turn * NS + n + 1)
                    states = hs[:, n % 2, :, :].rearrange("p h t -> p (h t)")
                    dve.tensor_tensor_scan(states, dA[:, n % 2, :, :, :].rearrange("p h s t -> p (h s t)"),
                                           states, 0.0, ALU.mult, ALU.add).then_inc(S("scan"), 1)
                    dve.wait_ge(S("scan"), turn * NS + n + 1)
                    dve.wait_ge(S("c_row"), turn * NS + n + 1)
                    if n >= 2:
                        dve.wait_ge(S("summed"), turn * (NS + 1) + n)
                    b = C_BANK[n % 2]
                    dve.tensor_tensor(hc[:, n % 2, :, :], hs[:, n % 2, :, :],
                                      ps[:, b:b + 1, :].broadcast_to([128, HALF, TOK]), ALU.mult).then_inc(S("hc"), 1)
                dve.wait_ge(S("summed"), (turn + 1) * (NS + 1))
                dve.wait_ge(S("z_silu"), turn * HALF + HALF)
                dve.tensor_tensor(yacc[:, :, :], ps[:, 4:6, :], sz[:, :, :], ALU.mult).then_inc(S("gated"), 1)

            def experts(l, g, c, first):
                for e in range(EXPERTS):
                    dve.wait_ge(S(f"down{l}"), g * 32 + e * SLICES + SLICES)
                    dve.wait_ge(S(f"gate_copied{l}"), g * EXPERTS + e + 1)
                    dve.tensor_tensor(weighted, ps[:, 2 + e % 2, :], gate_sb[:, e % 2, :],
                                      ALU.mult).then_inc(S(f"weighted{l}"), 1)
                    dve.wait_ge(S(f"weighted{l}"), g * EXPERTS + e + 1)
                    ins = dve.tensor_tensor(res[:, :], weighted, first if e == 0 else res[:, :], ALU.add)
                    if e < EXPERTS - 1:
                        c.link(ins)
                    else:
                        ins.then_inc(S("res2" if l == 0 else "res7"), 1)

            def attend(a, g, keys, halves, c):
                steps = SEQ * halves
                per = 4 // halves
                width = 512 // per
                per_step = 4

                def shift(k, part):
                    nth = (g * steps + k) * 2 + part
                    n = 2 * per * keys
                    at = part * n
                    s = pr[:, k % 2, at:at + n].rearrange("p (q i t) -> p q i t", q=2, i=per)
                    s3 = pr[:, k % 2, at:at + n].rearrange("p (h t) -> p h t", t=keys)
                    src = ps[:, 2 * part:2 * part + 2, :].rearrange("p q (i t) -> p q i t", i=per)[:, :, :, 0:keys]
                    top = mx[:, part * 2 * per:(part + 1) * 2 * per]
                    dve.wait_ge(S(f"scores{a}"), nth + 1)
                    if k >= 2:
                        dve.wait_ge(S(f"turn{a}"), (g * steps + k - 2) * per_step + (part + 1) * per_step // 2)
                    if a == "r":
                        dve.tensor_tensor(s, src, mneg[:, :].unsqueeze(1).unsqueeze(1).broadcast_to([128, 2, per, keys]),
                                          ALU.add).then_inc(S(f"scores_read{a}"), 1)
                        dve.wait_ge(S(f"scores_read{a}"), nth + 1)
                        c.link(dve.tensor_reduce(top, s3, AX.X, ALU.max))
                        dve.tensor_tensor(s3, s3, top.unsqueeze(2).broadcast_to([128, 2 * per, keys]),
                                          ALU.subtract).then_inc(S(f"shifted{a}"), 1)
                    else:
                        c.link(dve.tensor_reduce(top.rearrange("p (q i) -> p q i", q=2), src, AX.X, ALU.max))
                        dve.tensor_tensor(s, src, top.rearrange("p (q i) -> p q i", q=2).unsqueeze(3)
                                          .broadcast_to([128, 2, per, keys]),
                                          ALU.subtract).then_inc(S(f"shifted{a}"), 1)

                for k in range(steps):
                    shift(k, 0)
                    shift(k, 1)
                    if k > halves and (k - 1) % halves == 0:
                        inverse(a, g, (k - 1) // halves - 1)
                for j in range((steps - 2) // halves, SEQ):
                    inverse(a, g, j)

            def inverse(a, g, j):
                nth = (g * 3 + PHASE[a]) * SEQ + j
                dve.wait_ge(S("sums"), nth + 1)
                if j:
                    dve.wait_ge(S("head_done"), nth)
                dve.reciprocal(rec[:, :], den[:, :]).then_inc(S("sums_inverse"), 1)

            def top_two(tiles, c, values):
                dve.memset(idle[:, :], 0.0)
                for t in range(tiles):
                    m = c.mark(dve.max(v8[:, t, :], values[:, t, :]))
                c.wait(m)
                dve.memset(idle[:, :], 0.0)
                for t in range(tiles):
                    m = c.mark(dve.max_index(i8[:, t, :], v8[:, t, :], values[:, t, :]))
                c.wait(m)
                c.link(dve.tensor_copy(f8[:, 0:tiles, :], i8[:, 0:tiles, :]))

            c = Chain(dve, S("dve_setup"))
            dve.memset(LN_EPS[:, :], 1e-5)
            dve.memset(xp[:, :, :, 0:CONV - 1], 0.0)
            dve.memset(dA[:, :, :, :, 0:1], 0.0)
            c.link(dve.memset(vp[:, :], 0.0))
            dve.memset(vp[:, VALUES_AT - 8:VALUES_AT], 1.0)
            dve.memset(vp_heads[:, :, :, :, 56:64].rearrange("p n s h c -> p (n s h) c"), 1.0)
            dve.wait_ge(S("params_in"), 16)
            dve.wait_ge(S("a_exp"), 2)
            dve.tensor_scalar(a_neg[:, :, :, :], a_neg[:, :, :, :], -1.0, None, ALU.mult)
            dve.tensor_scalar(bqm[:, :], W("head_mask"), W("xbq"), None, ALU.mult)
            dve.wait_ge(S("temp"), 3)
            c.link(dve.tensor_scalar(tmp[:, 3:4], W("temp"), 0.0, tmp[:, 2:3], ALU.max, ALU.add))
            dve.tensor_scalar(spm[:, :], W("head_mask"), tmp[:, 3:4], None, ALU.mult)
            dve.wait_ge(S("mask_in"), 16)
            c.link(dve.tensor_copy(mneg[:, :], mask8[:, :]))
            c.link(dve.tensor_reduce(keep[:, :], mneg[:, :], AX.X, ALU.min))
            dve.tensor_scalar(keep[:, :], keep[:, :], -1.0, 1.0, ALU.mult, ALU.add).then_inc(S("keep"), 1)
            dve.wait_ge(S("keep_spread"), 1)
            dve.tensor_copy(keep_row[:, :], ps[:, 7, 0:L])
            dve.tensor_scalar(mneg[:, :], mneg[:, :], NEG, None, ALU.mult).then_inc(S("vector_setup"), 1)
            dve.wait_ge(S("vector_setup"), 1)

            with dve.Fori(0, GROUPS) as g:
                c = Chain(dve, S("dve_order"), g * DVE_LINKS)
                norm(0, g, x_in[:, :], xn[:, :], "n0")
                mamba(0, g, c)
                dve.wait_ge(S("mamba_out"), g * 2 + 1)
                dve.tensor_tensor(res[:, :], ps[:, 4, :], xn[:, :], ALU.add).then_inc(S("res1"), 1)
                norm(1, g, res[:, :], xm[:, :], "n1")
                dve.wait_ge(S("logits0"), g + 1)
                lg = rl[:, 0:SEQ, 0:EXPERTS]
                src = ps[:, 6, 0:SEQ * EXPERTS].rearrange("p (s e) -> p s e", s=SEQ)
                c.link(dve.tensor_reduce(r1[:, 0:SEQ], src, AX.X, ALU.max))
                dve.tensor_tensor(lg, src, r1[:, 0:SEQ].unsqueeze(2).broadcast_to([128, SEQ, EXPERTS]),
                                  ALU.subtract).then_inc(S("gate_shift"), 1)
                dve.wait_ge(S("gate_exp"), g + 1)
                c.link(dve.tensor_reduce(r1[:, 0:SEQ], lg, AX.X, ALU.add))
                c.link(dve.reciprocal(r2[:, 0:SEQ], r1[:, 0:SEQ]))
                c.link(dve.tensor_tensor(t8[:, 0:SEQ, :], lg, r2[:, 0:SEQ].unsqueeze(2).broadcast_to([128, SEQ, EXPERTS]),
                                         ALU.mult))
                top_two(SEQ, c, t8)
                c.link(dve.tensor_tensor(r1[:, 0:SEQ], v8[:, 0:SEQ, 0], v8[:, 0:SEQ, 1], ALU.add))
                c.link(dve.reciprocal(r2[:, 0:SEQ], r1[:, 0:SEQ]))
                c.link(dve.tensor_tensor(v8[:, 0:SEQ, 0:2], v8[:, 0:SEQ, 0:2],
                                         r2[:, 0:SEQ].unsqueeze(2).broadcast_to([128, SEQ, 2]), ALU.mult))
                iota = W("iota").unsqueeze(1).broadcast_to([128, SEQ, EXPERTS])
                for k, dst in ((0, gt[:, :, :]), (1, t8[:, 0:SEQ, :])):
                    c.link(dve.tensor_tensor(dst, f8[:, 0:SEQ, k:k + 1].broadcast_to([128, SEQ, EXPERTS]), iota,
                                             ALU.is_equal))
                    c.link(dve.tensor_tensor(dst, dst, v8[:, 0:SEQ, k:k + 1].broadcast_to([128, SEQ, EXPERTS]),
                                             ALU.mult))
                dve.tensor_tensor(gt[:, :, :], gt[:, :, :], t8[:, 0:SEQ, :], ALU.add).then_inc(S("gates0"), 1)
                dve.tensor_scalar(qf[:, :], x_in[:, :], 2.0, None, ALU.mult).then_inc(S("x_used"), 1)
                dve.wait_ge(S("x_used"), g + 1)
                experts(0, g, c, qf[:, :])
                norm(2, g, None, x1[:, :], "n2")
                dve.wait_ge(S("k_mm_x"), g * 2 + 1)
                dve.tensor_scalar(kt[:, :, 0:L], seqs(ps[:, 1, :]), W("xbk"), None, ALU.add)
                dve.wait_ge(S("k_mm_x"), g * 2 + 2)
                dve.tensor_scalar(kt[:, :, L:L + CTX], ps[:, 2, 0:SEQ * CTX].rearrange("p (s t) -> p s t", s=SEQ),
                                  W("xbk"), None, ALU.add)

                def value(bank, rows, n, bias):
                    b = W(bias)[0:rows, :].rearrange("p (h d) -> p h d", d=DH)
                    for j in range(SEQ):
                        ins = dve.tensor_tensor(head_values(n, j, rows),
                                                ps[0:rows, bank, j * D:(j + 1) * D].rearrange("p (h d) -> p h d", d=DH),
                                                b, ALU.add)
                    return ins

                dve.wait_ge(S("v_mm_x"), g * 2 + 1)
                value(3, L, 0, "xbv")
                dve.wait_ge(S("v_mm_x"), g * 2 + 2)
                value(4, CTX, 1, "xbv").then_inc(S("qkv_x"), 1)

                attend("x", g, L + CTX, 2, c)
                norm(3, g, None, x2[:, :], "n3")

                dve.wait_ge(S("k_mm_f"), g + 1)
                dve.tensor_scalar(kt[:, :, 0:L], seqs(ps[:, 1, :]), W("fbk"), None, ALU.add)
                dve.wait_ge(S("v_mm_f"), g + 1)
                value(3, L, 0, "fbv")
                dve.wait_ge(S("q_rsqrt"), g + 1)
                c.link(dve.tensor_tensor(qt[:, :], qf[:, :], rs[:, :], ALU.mult))
                for i in range(4):
                    ins = dve.tensor_scalar(qm[:, i, :], qt[:, :], W("qe"), spm[:, i:i + 1], ALU.add, ALU.mult)
                ins.then_inc(S("qkv_f"), 1)

                attend("f", g, L, 1, c)
                dve.wait_ge(S("logits_f"), g + 1)
                lg = rl[:, 0:SEQ, :]
                c.link(dve.tensor_tensor(lg, ps[:, 6, 0:SEQ * 17].rearrange("p (s e) -> p s e", s=SEQ),
                                         W("fbrs").unsqueeze(1).broadcast_to([128, SEQ, 17]), ALU.add))
                c.mark(dve.tensor_reduce(r1[:, 0:SEQ], rl[:, 0:SEQ, 0:ROUTED], AX.X, ALU.max))
                c.link(dve.tensor_reduce(r2[:, 0:SEQ], rl[:, 0:SEQ, ROUTED:], AX.X, ALU.max))
                c.mark(dve.tensor_tensor(rl[:, 0:SEQ, 0:ROUTED], rl[:, 0:SEQ, 0:ROUTED],
                                         r1[:, 0:SEQ].unsqueeze(2).broadcast_to([128, SEQ, ROUTED]), ALU.subtract))
                dve.tensor_tensor(rl[:, 0:SEQ, ROUTED:], rl[:, 0:SEQ, ROUTED:],
                                  r2[:, 0:SEQ].unsqueeze(2).broadcast_to([128, SEQ, SHARED]),
                                  ALU.subtract).then_inc(S("f_shift"), 1)
                dve.wait_ge(S("f_exp"), g + 1)
                dve.memset(idle[:, :], 0.0)
                for j in range(SEQ):
                    c.mark(dve.max(v8[:, j, :], rl[:, j, 0:ROUTED]))
                c.mark(dve.tensor_reduce(r1[:, 0:SEQ], rl[:, 0:SEQ, 0:ROUTED], AX.X, ALU.add))
                c.link(dve.tensor_reduce(r2[:, 0:SEQ], rl[:, 0:SEQ, ROUTED:], AX.X, ALU.add))
                c.mark(dve.reciprocal(r1[:, SEQ:2 * SEQ], r1[:, 0:SEQ]))
                c.mark(dve.reciprocal(r2[:, SEQ:2 * SEQ], r2[:, 0:SEQ]))
                c.link(dve.tensor_reduce(r1[:, 2 * SEQ:3 * SEQ], v8[:, 0:SEQ, 0:3], AX.X, ALU.add))
                c.mark(dve.tensor_tensor(r1[:, 0:SEQ], r1[:, 2 * SEQ:3 * SEQ], r1[:, SEQ:2 * SEQ], ALU.mult))
                c.link(dve.tensor_tensor(rl[:, 0:SEQ, ROUTED:], rl[:, 0:SEQ, ROUTED:],
                                         r2[:, SEQ:2 * SEQ].unsqueeze(2).broadcast_to([128, SEQ, SHARED]), ALU.mult))
                w0, w1 = rl[:, 0:SEQ, ROUTED], rl[:, 0:SEQ, ROUTED + 1]
                c.mark(dve.tensor_tensor(r2[:, 0:SEQ], w0, w1, ALU.add))
                c.link(dve.scalar_tensor_tensor(r1[:, 0:SEQ], r1[:, 0:SEQ], 6.0, w1, ALU.mult, ALU.mult))
                c.link(dve.scalar_tensor_tensor(r2[:, 0:SEQ], r2[:, 0:SEQ], 2.0, w0, ALU.mult, ALU.mult))
                dve.tensor_tensor(r1[:, 0:SEQ], r1[:, 0:SEQ], r2[:, 0:SEQ], ALU.add).then_inc(S("gates_f"), 1)
                dve.wait_ge(S("gates_f_spread"), g + 1)
                dve.tensor_tensor(qt[:, :], hT[:, :], ps[:, 5, :], ALU.mult).then_inc(S("gated_f"), 1)
                dve.wait_ge(S("proj_f"), g + 1)
                dve.scalar_tensor_tensor(res[:, :], ps[:, 4, :], W("fbp"), x2[:, :], ALU.add,
                                         ALU.add).then_inc(S("res4"), 1)
                norm(4, g, None, x3[:, :], "n4")

                mamba(1, g, c)
                dve.wait_ge(S("mamba_out"), g * 2 + 2)
                dve.tensor_tensor(res[:, :], ps[:, 4, :], x3[:, :], ALU.add).then_inc(S("res5"), 1)
                norm(5, g, None, x4[:, :], "n5")

                def rope(bank, n, bias, biass, a, b, dst):
                    src = ps[:, bank, 0:SEQ * n].rearrange("p (s t) -> p s t", s=SEQ)
                    swapped = ps[:, bank + 1, 0:SEQ * n].rearrange("p (s t) -> p s t", s=SEQ)
                    sin = W("rope_sin")[:, 0:n].unsqueeze(1).broadcast_to([128, SEQ, n])
                    cos = W("rope_cos")[:, 0:n].unsqueeze(1).broadcast_to([128, SEQ, n])
                    c.mark(dve.scalar_tensor_tensor(a, src, W(bias), sin, ALU.add, ALU.mult))
                    c.link(dve.scalar_tensor_tensor(b, swapped, W(biass), cos, ALU.add, ALU.mult))
                    c.link(dve.tensor_tensor(dst, a, b, ALU.subtract))

                dve.wait_ge(S("q_mm_r"), g + 1)
                rope(0, L, "rbq", "rbqs", seqs(qf[:, :]), seqs(qt[:, :]), seqs(qf[:, :]))
                for i in range(4):
                    dve.tensor_scalar(qm[:, i, :], qf[:, :], W("head_mask")[:, i:i + 1], None, ALU.mult)
                dve.wait_ge(S("k_mm_r"), g + 1)
                ka = qt[:, 0:SEQ * CTX].rearrange("p (s t) -> p s t", s=SEQ)
                kb = sq[:, 0:SEQ * CTX].rearrange("p (s t) -> p s t", s=SEQ)
                rope(2, CTX, "rbk", "rbks", ka, kb, kt[:, :, 0:CTX])
                dve.wait_ge(S("ctx_used"), g + 1)
                value(4, CTX, 1, "rbv").then_inc(S("qkv_r"), 1)
                attend("r", g, CTX, 1, c)
                dve.wait_ge(S("proj_r"), g + 1)
                dve.scalar_tensor_tensor(res[:, :], ps[:, 4, :], W("rbo"), x4[:, :], ALU.add,
                                         ALU.add).then_inc(S("res6"), 1)
                norm(6, g, None, x5[:, bass.ts(g, TOK)], "n6")
                dve.wait_ge(S("n6"), g + 1)
                assert c.n == DVE_LINKS, c.n

            c = Chain(dve, S("dve_rank"))
            dve.wait_ge(S("logits1"), 1)
            c.link(dve.tensor_copy(t8[:, :, :], ps[:, 6, 0:TILES * EXPERTS].rearrange("p (t e) -> p t e", e=EXPERTS)))
            top_two(TILES, c, t8)
            dve.tensor_tensor(r1[:, :], v8[:, :, 1], v8[:, :, 0], ALU.subtract).then_inc(S("pick_shift"), 1)
            iota = W("iota").unsqueeze(1).broadcast_to([128, TILES, EXPERTS])
            for k in range(2):
                ins = dve.tensor_tensor(oh[:, :, k, :].rearrange("p e t -> p t e"),
                                        f8[:, :, k:k + 1].broadcast_to([128, TILES, EXPERTS]), iota, ALU.is_equal)
            ins.then_inc(S("picked"), 1)
            dve.wait_ge(S("pick_exp"), 1)
            c.link(dve.tensor_scalar(r2[:, :], r1[:, :], 1.0, None, ALU.add))
            c.link(dve.reciprocal(v8[:, :, 0], r2[:, :]))
            c.link(dve.tensor_tensor(v8[:, :, 1], v8[:, :, 0], r1[:, :], ALU.mult))
            dve.wait_ge(S("counted"), 1)
            flat = lambda t: t[:, :, :, :].rearrange("p e k t -> p (e k t)")
            c.link(dve.tensor_tensor_scan(flat(tot), W("scan_keep"), ps[:, 5, 0:256], 0.0, ALU.mult, ALU.add))
            c.link(dve.tensor_tensor(flat(rank), flat(tot), ps[:, 5, 0:256], ALU.subtract))
            c.link(dve.tensor_tensor(flat(rank), flat(rank), ps[:, 4, 0:256], ALU.add))
            c.link(dve.scalar_tensor_tensor(flat(rank), flat(rank), float(CAPACITY), flat(oh), ALU.is_le, ALU.mult))
            for k, dst in ((0, gt_all), (1, t8)):
                done = c.mark(dve.tensor_tensor(dst[:, :, :], rank[:, :, k, :].rearrange("p e t -> p t e"),
                                                v8[:, :, k:k + 1].broadcast_to([128, TILES, EXPERTS]), ALU.mult))
            c.wait(done)
            dve.tensor_tensor(gt_all[:, :, :], gt_all[:, :, :], t8[:, :, :], ALU.add).then_inc(S("ranked"), 1)
            dve.wait_ge(S("ranked"), 1)
            with dve.Fori(0, GROUPS) as g:
                c = Chain(dve, S("dve_order2"), g * DVE_LINKS_2)
                dve.tensor_copy(x5g[:, :], x5[:, bass.ts(g, TOK)]).then_inc(S("x5_group"), 1)
                dve.tensor_copy(gt[:, :, :], gt_all[:, bass.ts(g, SEQ), :]).then_inc(S("gates1"), 1)
                dve.wait_ge(S("x5_group"), g + 1)
                experts(1, g, c, x5g[:, :])
                dve.wait_ge(S("out_free"), g + 1)
                norm(7, g, None, yout[:, :], "out_ready")
                dve.wait_ge(S("out_ready"), g + 1)
                assert c.n == DVE_LINKS_2, c.n


_ORDER = ["x_t", "ctx_t", "params", "selectors", "w_in", "w_out", "mask"]


def _shape_constants():
    p = np.arange(128)
    f = np.float32
    c = {}
    c["ident"] = np.eye(128, dtype=f)
    c["mean"] = np.full((128, 128), 1.0 / D, f)
    c["center"] = (np.eye(128) - 1.0 / D).astype(f)
    c["head_ones"] = (p[:, None] // DH == p[None, :] // DH).astype(f)
    c["before"] = (p[:, None] <= p[None, :]).astype(f)
    c["ones"] = np.ones((128, 128), f)
    c["head_mask"] = ((p[:, None] // DH) % 4 == np.arange(4)[None, :]).astype(f)
    c["iota"] = np.broadcast_to(np.arange(EXPERTS, dtype=f), (128, EXPERTS))
    inv = np.exp(np.arange(0, DH, 2, dtype=f) * f(-(4.0 * np.log(f(10.0))) / DH)).astype(f)
    angle = (np.arange(L, dtype=f)[None, :] * inv[(p % DH) // 2][:, None]).astype(f)
    sign = np.where(p % 2 == 0, 1.0, -1.0).astype(f)[:, None]
    c["rope_sin"] = np.sin(angle).astype(f) * sign
    c["rope_cos"] = np.cos(angle).astype(f)
    c["scan_keep"] = np.broadcast_to((np.arange(EXPERTS * 2 * TILES) % (2 * TILES) != 0).astype(f),
                                     (128, EXPERTS * 2 * TILES))
    sel = np.zeros((96, 2 * NS, 128), f)
    for j in range(2 * NS):
        sel[[j, 32 + j, 64 + j], j, :] = 1.0
    return c, sel


def kernel(**inputs):
    import ml_dtypes
    import concourse.bacc as _bacc
    from concourse import mybir as _mybir
    from concourse.bass_utils import run_bass_kernel_spmd as _run

    a = {k: np.asarray(v) for k, v in inputs.items()}
    v, sel = _shape_constants()

    def halves(m):
        m = m.reshape(HALF, 128, -1)
        return np.concatenate([m[0], m[1]], axis=1)

    def col(m):
        return m.reshape(128, 1)

    def rows(m):
        return np.broadcast_to(m.reshape(1, -1), (128, m.size))

    def low(m):
        return np.concatenate([m, np.zeros((128 - m.shape[0], m.shape[1]), m.dtype)])

    swap = np.arange(D) ^ 1
    v["in_w0"], v["in_w1"] = a["L0_attn_in_proj_w"].T, a["L1_attn_W_in"]
    v["x_w0"], v["x_w1"] = halves(a["L0_attn_x_proj_w"].T), halves(a["L1_attn_W_x"])
    v["dt_w0"], v["dt_w1"] = low(a["L0_attn_dt_proj_w"].T), low(a["L1_attn_W_dt"])
    v["out_w0"], v["out_w1"] = halves(a["L0_attn_out_proj_w"].T), halves(a["L1_attn_W_out"])
    v["conv_w0"], v["conv_w1"] = halves(a["L0_attn_conv_w"].reshape(DI, CONV)), halves(a["L1_attn_conv_w"].T)
    for n, k0, k1 in (("conv_b", "conv_b", "conv_b"), ("dt_b", "dt_proj_b", "b_dt"), ("a_log", "A_log", "A_log"),
                      ("d", "D", "D")):
        v[n + "0"] = halves(a["L0_attn_" + k0].reshape(DI, -1))
        v[n + "1"] = halves(a["L1_attn_" + k1].reshape(DI, -1))
    v["gate0"], v["gate1"] = a["L0_attn_gate_w"].T, a["L1_ffn_w_g"]
    for n, p in (("x", "L0_xattn_"), ("f", "L0_ffn_"), ("r", "L1_xattn_")):
        for m in "qkv":
            v[n + m] = a[p + "W" + m].T
        v[n + "bq"], v[n + "bk"], v[n + "bv"] = col(a[p + "bq"]), col(a[p + "bk"]), rows(a[p + "bv"])
    for m in "qk":
        v["r" + m + "s"] = a["L1_xattn_W" + m][swap].T
        v["rb" + m + "s"] = col(a["L1_xattn_b" + m][swap])
    v["fp"], v["fbp"] = a["L0_ffn_Wp"].T, col(a["L0_ffn_bp"])
    v["ro"], v["rbo"] = a["L1_xattn_Wo"].T, col(a["L1_xattn_bo"])
    v["frs"] = np.concatenate([a["L0_ffn_Wr"], a["L0_ffn_Ws"]]).T
    v["fbrs"] = rows(np.concatenate([a["L0_ffn_br"], a["L0_ffn_bs"]]))
    v["temp"] = col(np.repeat(a["L0_ffn_temperature"].reshape(HEADS), DH))
    v["qe"] = col(a["L0_ffn_query_embedding"])
    w_in = np.stack([a["L0_attn_w1"].transpose(2, 0, 1), a["L1_ffn_c_fc"].transpose(1, 0, 2)], axis=1)
    w_out = np.stack([a["L0_attn_w2"].transpose(2, 0, 1).reshape(SLICES, 128, EXPERTS, D).transpose(1, 2, 0, 3),
                      a["L1_ffn_c_proj"].reshape(EXPERTS, SLICES, 128, D).transpose(2, 0, 1, 3)], axis=1)
    arrays = {
        "x_t": a["x"].reshape(B * L, D).T,
        "ctx_t": a["ctx_1024"].reshape(B * CTX, D).T,
        "params": np.concatenate([v[n] for n, _ in PARAMS], axis=1),
        "selectors": sel.astype(ml_dtypes.bfloat16),
        "w_in": w_in,
        "w_out": w_out,
        "mask": a["mask_1x1xSxS2_bk1"].reshape(L, CTX),
    }
    arrays = {k: np.ascontiguousarray(m) for k, m in arrays.items()}
    nc = _bacc.Bacc("TRN2", target_bir_lowering=False, num_devices=1)
    args = [nc.dram_tensor(n, arrays[n].shape, _mybir.dt.from_np(arrays[n].dtype), kind="ExternalInput").ap()
            for n in _ORDER]
    args.append(nc.dram_tensor("out", (D, B * L), F32, kind="ExternalOutput").ap())
    decoder_kernel(nc, *args)
    r = _run(nc, [arrays], core_ids=[0])
    return np.ascontiguousarray(r.results[0]["out"].T).reshape(B, L, D)
```

```python
from contextlib import ExitStack

import numpy as np

import concourse.bass as bass
from concourse import mybir

F32 = mybir.dt.float32
BF16 = mybir.dt.bfloat16
U32 = mybir.dt.uint32
U8 = mybir.dt.uint8
ALU = mybir.AluOpType
ACT = mybir.ActivationFunctionType
AX = mybir.AxisListType

B, L, D = 16, 128, 128
CTX = 77
SEQ = 4
TOK = SEQ * L
GROUPS = B // SEQ
DI, NS, RANK, CONV = 256, 16, 8, 4
HALF = DI // 128
HEADS, DH = 16, 8
EXPERTS, HID = 8, 512
SLICES = HID // 128
CAPACITY = 640
TILES = B
ROUTED, SHARED = 15, 2
VALUES_AT = 32
LOG_EXP = "natural_log_exp_and_others"
NEG = float(np.finfo(np.float32).min)

PARAMS = [
    ("in_w0", 2 * DI), ("x_w0", HALF * 40), ("dt_w0", DI),
    ("conv_w0", HALF * CONV), ("conv_w1", HALF * CONV), ("conv_b0", HALF), ("conv_b1", HALF),
    ("dt_b0", HALF), ("dt_b1", HALF), ("a_log0", HALF * NS), ("a_log1", HALF * NS),
    ("d0", HALF), ("d1", HALF), ("gate0", EXPERTS), ("gate1", EXPERTS),
    ("xbq", 1), ("xbk", 1), ("fbq", 1), ("fbk", 1), ("fbp", 1), ("temp", 1), ("qe", 1),
    ("rbq", 1), ("rbqs", 1), ("rbk", 1), ("rbks", 1), ("rbo", 1),
    ("ident", 128), ("mean", 128), ("ones", 128), ("head_mask", 4), ("iota", EXPERTS),
    ("out_w0", HALF * D), ("in_w1", 2 * DI), ("x_w1", HALF * 40), ("dt_w1", DI), ("out_w1", HALF * D),
    ("xq", D), ("xk", D), ("xv", D), ("xbv", D),
    ("fq", D), ("fk", D), ("fv", D), ("fp", D), ("fbv", D), ("frs", ROUTED + SHARED), ("fbrs", ROUTED + SHARED),
    ("rq", D), ("rqs", D), ("rk", D), ("rks", D), ("rv", D), ("ro", D), ("rbv", D),
    ("center", 128), ("head_ones", 128), ("before", 128),
    ("rope_sin", L), ("rope_cos", L), ("scan_keep", EXPERTS * 2 * TILES),
]
COLUMN = {}
WIDTH = 0
for _name, _cols in PARAMS:
    COLUMN[_name] = (WIDTH, WIDTH + _cols)
    WIDTH += _cols


class Chain:

    def __init__(self, engine, semaphore, base=0):
        self.engine, self.semaphore, self.base, self.n = engine, semaphore, base, 0

    def mark(self, instruction):
        instruction.then_inc(self.semaphore, 1)
        self.n += 1
        return self.n

    def wait(self, n):
        self.engine.wait_ge(self.semaphore, self.base + n)

    def link(self, instruction):
        self.wait(self.mark(instruction))


DVE_LINKS = 117
DVE_LINKS_2 = 10


def decoder_kernel(nc, x_t, ctx_t, params, selectors, w_in, w_out, mask, out):
    with ExitStack() as ctx:
        def sb(name, shape, dt=F32):
            return ctx.enter_context(nc.sbuf_tensor(name, shape, dt))

        semaphores = {}

        def S(name):
            if name not in semaphores:
                semaphores[name] = ctx.enter_context(nc.semaphore(name))
            return semaphores[name]

        ps = ctx.enter_context(nc.psum_tensor("ps", [128, 8, 512], F32))
        pw = sb("pw", [128, WIDTH])
        sel = sb("sel", [96, 2 * NS, 128], BF16)
        moe_in = sb("moe_in", [128, 2, EXPERTS, HID])
        moe_out = sb("moe_out", [128, 2, EXPERTS, SLICES, D])
        x_in = sb("x_in", [128, TOK])
        ctx_in = sb("ctx_in", [128, SEQ * CTX])
        xn = x1 = x3 = sb("odd_result", [128, TOK])
        xm = x2 = x4 = sb("even_result", [128, TOK])
        x5 = sb("x5", [128, B * L])
        res = sb("res", [128, TOK])
        sq = sb("sq", [128, TOK])
        rs = sb("rs", [128, TOK])
        xp = sb("xp", [128, HALF, SEQ, CONV - 1 + L])
        shared = sb("shared", [128, 6 * HALF * TOK])
        sz, cv, u, dl, dtu, yacc = (
            shared[:, i * HALF * TOK:(i + 1) * HALF * TOK].rearrange("p (h t) -> p h t", h=HALF) for i in range(6))
        bcs = sb("bcs", [96, TOK], BF16)
        bc_hi = sb("bc_hi", [32, TOK], BF16)
        bc_r, dtl = sq[0:32, :], rs[0:RANK, :]
        b_sb = (sq, rs)
        a_neg = sb("a_neg", [128, 2, HALF, NS])
        dA = sb("dA", [128, 2, HALF, SEQ, L])
        arena = sb("arena", [128, 4096])

        def part(a, n):
            return arena[:, a:a + n]

        ab = part(0, 1024).rearrange("p (h t) -> p h t", h=HALF)
        u1 = part(1024, 1024).rearrange("p (h t) -> p h t", h=HALF)
        lb = part(2048, 1024).rearrange("p (h t) -> p h t", h=HALF)
        rb = part(3072, 1024).rearrange("p (h t) -> p h t", h=HALF)
        hs = part(0, 2048).rearrange("p (s h t) -> p s h t", s=2, h=HALF)
        hc = part(2048, 2048).rearrange("p (s h t) -> p s h t", s=2, h=HALF)
        gelu = part(0, 2048).rearrange("p (s t) -> p s t", s=4)
        gate_sb = part(2048, 1024).rearrange("p (s t) -> p s t", s=2)
        weighted = part(3072, 512)
        pr = part(0, 4096).rearrange("p (s n) -> p s n", s=2)
        qm = shared[:, 0:4 * TOK].rearrange("p (i t) -> p i t", i=4)
        pt = shared[:, 2048:3584].rearrange("p (s a b) -> p s a b", s=3, a=4)
        qf, qt, hT = shared[:, 3584:4096], shared[:, 4096:4608], shared[:, 4608:5120]
        kt = shared[:, 5120:5120 + SEQ * (L + CTX)].rearrange("p (s t) -> p s t", s=SEQ)
        vp = sb("vp", [128, VALUES_AT + 2 * SEQ * HEADS * 64 + 24])
        vp_heads = vp[:, VALUES_AT:VALUES_AT + 2 * SEQ * HEADS * 64].rearrange("p (n s h c) -> p n s h c",
                                                                               n=2, s=SEQ, h=HEADS)
        mx = sb("mx", [128, HEADS])
        heads = sb("heads", [128, 2, 2 * L])
        den = sb("den", [128, L])
        rec = sb("rec", [128, L])
        keep_row = sb("keep_row", [128, L])
        bqm = sb("bqm", [128, 4])
        spm = sb("spm", [128, 4])
        tmp = sb("tmp", [128, 4])
        mask8 = sb("mask8", [128, CTX], U8)
        mneg = sb("mneg", [128, CTX])
        keep = sb("keep", [128, 1])
        rl = sb("rl", [128, SEQ, ROUTED + SHARED])
        r1 = sb("r1", [128, TILES])
        r2 = sb("r2", [128, TILES])
        v8, gt_all = (heads[:, i, 0:TILES * 8].rearrange("p (t e) -> p t e", e=8) for i in range(2))
        i8 = sb("i8", [128, TILES, 8], U32)
        f8, t8 = (b[:, :].rearrange("p (t e) -> p t e", e=8) for b in (rec, den))
        gt = sb("gt", [128, SEQ, EXPERTS])
        oh = part(0, 256).rearrange("p (e k t) -> p e k t", e=EXPERTS, k=2)
        tot = part(256, 256).rearrange("p (e k t) -> p e k t", e=EXPERTS, k=2)
        rank = part(512, 256).rearrange("p (e k t) -> p e k t", e=EXPERTS, k=2)
        yout = x2

        def W(name):
            a, b = COLUMN[name]
            return pw[:, a:b]

        def head_values(n, j, rows):
            return vp_heads[0:rows, n, j, :, 24:24 + DH]

        def value_window(n, j, head, rows):
            quad, i = divmod(head, 4)
            at = VALUES_AT + ((n * SEQ + j) * HEADS + head) * 64 + 24 - 8 * i
            if quad % 2:
                at -= 32
            return vp[0:rows, at:at + 64]

        def held(quad):
            at = 64 * (quad // 2)
            odd = quad % 2
            return (slice(at + 32 * odd, at + 32 * odd + 32), slice(at + 32 - 32 * odd, at + 64 - 32 * odd),
                    slice(odd * L, (odd + 1) * L))

        POOL_HEADS = 2
        PHASE = {"x": 0, "f": 1, "r": 2}

        def seqs(ap, width=L):
            return ap.rearrange("p (s t) -> p s t", s=SEQ)

        ident = W("ident")
        idle = sb("idle", [128, 1])
        LN_EPS = sb("ln_eps", [128, 1])

        block = ctx.enter_context(nc.Block())

        B_BANK, C_BANK = (0, 6), (1, 7)
        NORMS = 7
        CENTRE, MEAN = [0] * 6 + [7] * 2, [1] * 6 + [6] * 2

        FIRST = None

        def norms_before(i, g):
            if i == 0:
                return 0 if g is FIRST else g * NORMS - 1
            return g * NORMS + (i if i < 6 else NORMS) if i < 7 else GROUPS * NORMS + 1 + g

        def centred_before(i, g):
            return g * (NORMS - 2) + i - 2 if i < 7 else GROUPS * (NORMS - 2) + g

        def guarded_before(i, g):
            return 0 if g is FIRST else g * 2 + i

        @block.sync
        def _(sp):
            early = COLUMN["out_w0"][0]
            sp.dma_start(x_in[:, :], x_t[:, 0:TOK]).then_inc(S("x_in"), 16)
            sp.dma_start(pw[:, 0:early], params[:, 0:early]).then_inc(S("params_in"), 16)
            sp.dma_start(mask8[:, :], mask).then_inc(S("mask_in"), 16)
            sp.dma_start(sel[:, :, :], selectors).then_inc(S("sel_in"), 16)
            sp.dma_start(pw[:, early:], params[:, early:]).then_inc(S("rest_in"), 16)
            sp.dma_start(ctx_in[:, :], ctx_t[:, 0:SEQ * CTX]).then_inc(S("ctx_in"), 16)
            with sp.Fori(1, GROUPS) as g:
                sp.wait_ge(S("x_used"), g)
                sp.dma_start(x_in[:, :], x_t[:, bass.ts(g, TOK)]).then_inc(S("x_in"), 16)
                sp.wait_ge(S("ctx_used"), g)
                sp.dma_start(ctx_in[:, :], ctx_t[:, bass.ts(g, SEQ * CTX)]).then_inc(S("ctx_in"), 16)
            sp.wait_ge(S("x_used"), GROUPS)
            sp.dma_start(x_in[:, :], x_t[:, 0:TOK]).then_inc(S("x_in"), 16)
            sp.sem_inc(S("out_free"), 1)
            with sp.Fori(0, GROUPS) as g:
                sp.wait_ge(S("out_ready"), g + 1)
                sp.dma_start(out[:, bass.ts(g, TOK)], yout[:, :]).then_inc(S("stored"), 16)
                sp.wait_ge(S("stored"), g * 16 + 16)
                sp.sem_inc(S("out_free"), 1)

        @block.gpsimd
        def _(pool):
            pool.wait_ge(S("rest_in"), 16)
            for l in range(2):
                pool.dma_start(moe_in[:, l, :, :], w_in[:, l, :, :]).then_inc(S(f"moe_in{l}"), 16)
                pool.dma_start(moe_out[:, l, :, :, :], w_out[:, l, :, :, :]).then_inc(S(f"moe_in{l}"), 16)
            def head_rows(a, g):
                for j in range(POOL_HEADS):
                    nth = (g * 3 + PHASE[a]) * SEQ + j
                    now = slice(j * L, (j + 1) * L)
                    pool.wait_ge(S("sums_inverse"), nth + 1)
                    for quad in range(4):
                        top, bottom, cols = held(quad)
                        rows = slice(32 * quad, 32 * quad + 32)
                        ins = pool.tensor_tensor(hT[rows, now], heads[top, j % 2, cols], rec[rows, :], ALU.mult)
                    if a == "f":
                        ins.then_inc(S("head_done"), 1)
                        continue
                    ins.then_inc(S("head_over_sum"), 1)
                    pool.wait_ge(S("head_over_sum"), (g * 2 + (a == "r")) * POOL_HEADS + j + 1)
                    if a == "x":
                        pool.tensor_tensor(res[:, now], hT[:, now], x1[:, now], ALU.add).then_inc(S("head_done"), 1)
                    else:
                        pool.tensor_tensor(hT[:, now], hT[:, now], keep_row[:, :],
                                           ALU.mult).then_inc(S("head_done"), 1)

            with pool.Fori(0, GROUPS) as g:
                for l in range(2):
                    turn = g * 2 + l
                    pool.wait_ge(S("dtu"), turn + 1)
                    for n in range(NS):
                        pool.wait_ge(S("b_copied"), turn * NS + n + 1)
                        if n >= 2:
                            pool.wait_ge(S("hc"), turn * NS + n - 1)
                        pool.tensor_tensor(hs[:, n % 2, :, :], dtu[:, :, :],
                                           b_sb[n % 2][:, :].unsqueeze(1).broadcast_to([128, HALF, TOK]),
                                           ALU.mult).then_inc(S("dbu"), 1)
                    for a in ("x", "f") if l == 0 else ("r",):
                        head_rows(a, g)

        @block.tensor
        def _(pe):
            def norm(i, g, src, gate):
                nth = norms_before(i, g)
                if gate:
                    gate()
                if i >= 2:
                    pe.matmul(ps[:, CENTRE[i], :], W("center"), src, start=True, stop=True).then_inc(S("centred"), 1)
                pe.wait_ge(S("squared"), nth + 1)
                pe.matmul(ps[:, MEAN[i], :], W("mean"), sq[:, :], start=True, stop=True).then_inc(S("var"), 1)

            def project(l, src):
                for m in range(4):
                    pe.matmul(ps[:, m, :], W(f"in_w{l}")[:, m * 128:(m + 1) * 128], src,
                              start=True, stop=True).then_inc(S("proj"), 1)

            def mamba(l, g):
                turn = g * 2 + l
                pe.wait_ge(S("u_ready"), turn * HALF + HALF)
                for bank, a, n in ((4, 0, RANK), (5, RANK, 2 * NS)):
                    for h in range(HALF):
                        mm = pe.matmul(ps[0:n, bank, :], W(f"x_w{l}")[:, h * 40 + a:h * 40 + a + n], u[:, h, :],
                                       start=(h == 0), stop=(h == HALF - 1))
                    mm.then_inc(S("xdbl"), 1)
                pe.wait_ge(S("dtl"), turn + 1)
                for h in range(HALF):
                    pe.matmul(ps[:, 6 + h, :], W(f"dt_w{l}")[0:RANK, h * 128:(h + 1) * 128], dtl[:, :],
                              start=True, stop=True).then_inc(S("dt_mm"), 1)
                pe.wait_ge(S("bc_split"), turn + 1)
                pe.wait_ge(S("z_silu"), turn * HALF + HALF)
                def add_up(n):
                    for h in range(HALF):
                        mm = pe.matmul(ps[:, 4 + h, :], ident, yacc[:, h, :] if n < 0 else hc[:, n % 2, h, :],
                                       start=(n < 0), stop=(n == NS - 1))
                    mm.then_inc(S("summed"), 1)

                def b_row(n):
                    if n >= 2:
                        pe.wait_ge(S("b_copied"), turn * NS + n - 1)
                    pe.matmul(ps[:, B_BANK[n % 2], :], sel[:, n, :], bcs[:, :], start=True,
                              stop=True).then_inc(S("b_row"), 1)

                def c_row(n):
                    if n >= 2:
                        pe.wait_ge(S("hc"), turn * NS + n - 1)
                    pe.matmul(ps[:, C_BANK[n % 2], :], sel[:, NS + n, :], bcs[:, :], start=True,
                              stop=True).then_inc(S("c_row"), 1)

                pe.wait_ge(S("sel_in"), 16)
                b_row(0)
                c_row(0)
                pe.wait_ge(S("seeded"), turn + 1)
                add_up(-1)
                pe.wait_ge(S("dtu"), turn + 1)
                b_row(1)
                c_row(1)
                b_row(2)
                for n in range(NS - 1):
                    if n + 3 < NS:
                        b_row(n + 3)
                    if n + 2 < NS:
                        c_row(n + 2)
                    else:
                        pe.wait_ge(S("hc"), turn * NS + n + 1)
                    add_up(n)
                pe.wait_ge(S("hc"), turn * NS + NS)
                add_up(NS - 1)
                pe.wait_ge(S("rest_in"), 16)
                pe.wait_ge(S("gated"), turn + 1)
                for h in range(HALF):
                    mm = pe.matmul(ps[:, 4, :], W(f"out_w{l}")[:, h * D:(h + 1) * D], yacc[:, h, :],
                                   start=(h == 0), stop=(h == HALF - 1))
                mm.then_inc(S("mamba_out"), 1)

            def experts(l, g, src, gates_ready, last=None):
                def down(i):
                    e, f = divmod(i, SLICES)
                    pe.wait_ge(S(f"gelu{l}"), g * 32 + i + 1)
                    if f == 0 and (e >= 2 or last is not None):
                        pe.wait_ge(S(f"weighted{l}"), g * EXPERTS + e - 1)
                    mm = pe.matmul(ps[:, 2 + e % 2, :], moe_out[:, l, e, f, :], gelu[:, i % 4, :],
                                   start=(f == 0), stop=(f == SLICES - 1))
                    mm.then_inc(S(f"down{l}"), 1)

                def spread(e):
                    if e == 0:
                        pe.wait_ge(S("gates_split"), l * GROUPS + g + 1)
                    if e >= 2 or last is not None:
                        pe.wait_ge(S(f"gate_copied{l}"), g * EXPERTS + e - 1)
                    pe.matmul(ps[:, 4 + e % 2, :], sel[:, e, :], bcs[:, :], start=True,
                              stop=True).then_inc(S(f"gate_spread{l}"), 1)

                for i in range(EXPERTS * SLICES):
                    e, f = divmod(i, SLICES)
                    if i >= 2 or last is not None:
                        pe.wait_ge(S(f"gelu{l}"), g * 32 + i - 1)
                    pe.matmul(ps[:, i % 2, :], moe_in[:, l, e, f * 128:(f + 1) * 128], src,
                              start=True, stop=True).then_inc(S(f"up{l}"), 1)
                    if i:
                        down(i - 1)
                    if i == 2:
                        gates_ready()
                        for j in range(SEQ):
                            mm = pe.transpose(ps[0:EXPERTS, 6, j * L:(j + 1) * L], gt[:, j, :], ident)
                        mm.then_inc(S("gates_turned"), 1)
                    if i and f == 0:
                        spread(e - 1)
                    if last is not None and i == 6:
                        pe.matmul(ps[:, CENTRE[7], :], W("center"), res[:, :], start=True,
                                  stop=True).then_inc(S("centred"), 1)
                    if last is not None and i == 10:
                        pe.wait_ge(S("squared"), norms_before(7, last) + 1)
                        pe.matmul(ps[:, MEAN[7], :], W("mean"), sq[:, :], start=True, stop=True).then_inc(S("var"), 1)
                spread(EXPERTS - 1)
                down(EXPERTS * SLICES - 1)

            def values(src, n, bank, w, rows):
                for j in range(SEQ):
                    mm = pe.matmul(ps[0:rows, bank, j * D:(j + 1) * D], src[:, j * rows:(j + 1) * rows], w,
                                   start=True, stop=True)
                mm.then_inc(S(n), 1)

            def attend(a, g, keys, halves):
                steps = SEQ * halves
                quads = 4 // halves
                per_bank = quads
                width = 512 // per_bank
                parts = {"x": ((0, 0, L), (1, L, CTX)), "f": ((0, 0, L),), "r": ((1, 0, CTX),)}[a]
                blocks = [(k, q, n, at, rows) for k in range(steps) for q in range(quads) for n, at, rows in parts]
                per_step = quads * len(parts)
                base = g * steps * per_step

                def scores(k, part):
                    j, half = divmod(k, halves)
                    if k:
                        pe.wait_ge(S("scores_readr" if a == "r" else f"shifted{a}"), (g * steps + k - 1) * 2 + part + 1)
                    for local in range(part * 2 * per_bank, (part + 1) * 2 * per_bank):
                        quad, i = divmod(half * quads * 4 + local, 4)
                        bank, at = divmod(local, per_bank)
                        p = slice(32 * quad, 32 * quad + 32)
                        mm = pe.matmul(ps[:, bank, at * width:at * width + keys],
                                       qm[p, i, j * L:(j + 1) * L], kt[p, j, 0:keys], start=True, stop=True)
                    mm.then_inc(S(f"scores{a}"), 1)

                def turn(b):
                    k, q, n, at, rows = blocks[b]
                    if b % (per_step // 2) == 0:
                        pe.wait_ge(S(f"probs{a}"), (g * steps + k) * 2 + 1 + (b % per_step > 0))
                    if b >= 3:
                        pe.wait_ge(S(f"turned{a}"), base + b - 2)
                    for i in range(4):
                        c = (q * 4 + i) * keys + at
                        mm = pe.transpose(ps[0:rows, 4 + b % 3, i * 128:(i + 1) * 128],
                                          pr[:, k % 2, c:c + rows], ident)
                    mm.then_inc(S(f"turn{a}"), 1)

                def product(b):
                    k, q, n, at, rows = blocks[b]
                    j, half = divmod(k, halves)
                    quad = half * quads + q
                    pe.wait_ge(S(f"turned{a}"), base + b + 1)
                    if j and b % (halves * per_step) == 0:
                        pe.wait_ge(S("heads"), (g * 3 + PHASE[a]) * SEQ + j)
                    at = 64 * (quad // 2)
                    for i in range(4):
                        mm = pe.matmul(ps[at:at + 64, 7, (quad % 2) * L:(quad % 2 + 1) * L],
                                       value_window(n, j, 4 * quad + i, rows), pt[0:rows, b % 3, i, :],
                                       start=(i == 0 and n == parts[0][0]), stop=(i == 3 and n == parts[-1][0]))
                    mm.then_inc(S(f"product{a}"), 1)

                for k in range(2):
                    for part in range(2):
                        scores(k, part)
                for b in range(len(blocks) + 2):
                    if b < len(blocks):
                        turn(b)
                    if b >= 2:
                        product(b - 2)
                    k, w = divmod(b, per_step)
                    if w >= 2 and k + 2 < steps:
                        scores(k + 2, w - 2)

            pe.wait_ge(S("params_in"), 16)
            pe.wait_ge(S("keep"), 1)
            pe.matmul(ps[:, 7, 0:L], keep[:, 0:1].to_broadcast([128, 128]), ident,
                      start=True, stop=True).then_inc(S("keep_spread"), 1)
            norm(0, FIRST, None, None)
            pe.wait_ge(S("n0"), 1)
            project(0, xn[:, :])
            with pe.Fori(0, GROUPS) as g:
                mamba(0, g)
                norm(1, g, None, None)
                pe.wait_ge(S("n1"), g + 1)
                for j in range(SEQ):
                    mm = pe.matmul(ps[:, 6, j * EXPERTS:(j + 1) * EXPERTS], xm[:, j * L:(j + 1) * L], W("gate0"),
                                   start=True, stop=True)
                mm.then_inc(S("logits0"), 1)
                pe.wait_ge(S("moe_in0"), 32)
                experts(0, g, xm[:, :], lambda: pe.wait_ge(S("gates0"), g + 1))
                norm(2, g, res[:, :], lambda: pe.wait_ge(S("res2"), g + 1))
                pe.wait_ge(S("n2"), g + 1)
                pe.matmul(ps[:, 0, :], W("xq"), x1[:, :], start=True, stop=True).then_inc(S("q_mm_x"), 1)
                pe.matmul(ps[:, 1, :], W("xk"), x1[:, :], start=True, stop=True).then_inc(S("k_mm_x"), 1)
                pe.wait_ge(S("ctx_in"), g * 16 + 16)
                pe.matmul(ps[:, 2, 0:SEQ * CTX], W("xk"), ctx_in[:, :], start=True, stop=True).then_inc(S("k_mm_x"), 1)
                values(x1[:, :], "v_mm_x", 3, W("xv"), L)
                values(ctx_in[:, :], "v_mm_x", 4, W("xv"), CTX)
                pe.wait_ge(S("qkv_x"), g + 1)
                pe.wait_ge(S("q_masked_x"), g * 4 + 4)
                attend("x", g, L + CTX, 2)
                norm(3, g, res[:, :], lambda: pe.wait_ge(S("head_done"), (g * 3 + 0) * SEQ + SEQ))
                pe.wait_ge(S("n3"), g + 1)
                pe.matmul(ps[:, 0, :], W("fq"), x2[:, :], start=True, stop=True).then_inc(S("q_mm_f"), 1)
                pe.matmul(ps[:, 1, :], W("fk"), x2[:, :], start=True, stop=True).then_inc(S("k_mm_f"), 1)
                values(x2[:, :], "v_mm_f", 3, W("fv"), L)
                pe.wait_ge(S("q_squared"), g + 1)
                pe.matmul(ps[:, 2, :], W("head_ones"), sq[:, :], start=True, stop=True).then_inc(S("q_norm"), 1)
                pe.wait_ge(S("qkv_f"), g + 1)
                attend("f", g, L, 1)
                pe.wait_ge(S("head_done"), (g * 3 + 1) * SEQ + SEQ)
                for j in range(SEQ):
                    mm = pe.matmul(ps[:, 6, j * 17:(j + 1) * 17], hT[:, j * L:(j + 1) * L], W("frs"),
                                   start=True, stop=True)
                mm.then_inc(S("logits_f"), 1)
                pe.wait_ge(S("gates_f"), g + 1)
                for j in range(SEQ):
                    mm = pe.matmul(ps[:, 5, j * L:(j + 1) * L], r1[:, j:j + 1].to_broadcast([128, 128]), ident,
                                   start=True, stop=True)
                mm.then_inc(S("gates_f_spread"), 1)
                pe.wait_ge(S("gated_f"), g + 1)
                pe.matmul(ps[:, 4, :], W("fp"), qt[:, :], start=True, stop=True).then_inc(S("proj_f"), 1)
                norm(4, g, res[:, :], lambda: pe.wait_ge(S("res4"), g + 1))
                pe.wait_ge(S("n4"), g + 1)
                project(1, x3[:, :])
                mamba(1, g)
                norm(5, g, res[:, :], lambda: pe.wait_ge(S("res5"), g + 1))
                pe.wait_ge(S("n5"), g + 1)
                pe.matmul(ps[:, 0, :], W("rq"), x4[:, :], start=True, stop=True)
                pe.matmul(ps[:, 1, :], W("rqs"), x4[:, :], start=True, stop=True).then_inc(S("q_mm_r"), 1)
                pe.matmul(ps[:, 2, 0:SEQ * CTX], W("rk"), ctx_in[:, :], start=True, stop=True)
                pe.matmul(ps[:, 3, 0:SEQ * CTX], W("rks"), ctx_in[:, :], start=True, stop=True).then_inc(S("k_mm_r"), 1)
                values(ctx_in[:, :], "ctx_used", 4, W("rv"), CTX)
                pe.wait_ge(S("qkv_r"), g + 1)
                attend("r", g, CTX, 1)
                pe.wait_ge(S("scores_readr"), g * SEQ * 2 + SEQ * 2)
                norm(0, g + 1, None, None)
                pe.wait_ge(S("head_done"), (g * 3 + 2) * SEQ + SEQ)
                pe.matmul(ps[:, 4, :], W("ro"), hT[:, :], start=True, stop=True).then_inc(S("proj_r"), 1)
                pe.wait_ge(S("n0"), g + 2)
                project(0, xn[:, :])
                norm(6, g, res[:, :], lambda: pe.wait_ge(S("res6"), g + 1))
            pe.wait_ge(S("n6"), GROUPS)
            for t in range(TILES):
                mm = pe.matmul(ps[:, 6, t * EXPERTS:(t + 1) * EXPERTS], x5[:, t * L:(t + 1) * L], W("gate1"),
                               start=True, stop=True)
            mm.then_inc(S("logits1"), 1)
            pe.wait_ge(S("picked"), 1)
            picks = oh[:, :, :, :].rearrange("p e k t -> p (e k t)")
            pe.matmul(ps[:, 4, 0:256], W("before"), picks, start=True, stop=True)
            pe.matmul(ps[:, 5, 0:256], W("ones"), picks, start=True, stop=True).then_inc(S("counted"), 1)
            pe.wait_ge(S("moe_in1"), 32)
            pe.wait_ge(S("ranked"), 1)
            gates1 = lambda g: (lambda: pe.wait_ge(S("gates1"), g + 1))
            experts(1, 0, x5[:, 0:TOK], gates1(0))
            with pe.Fori(1, GROUPS) as g:
                experts(1, g, x5[:, bass.ts(g, TOK)], gates1(g), last=g - 1)
            norm(7, GROUPS - 1, res[:, :], lambda: pe.wait_ge(S("res7"), GROUPS))

        @block.scalar
        def _(act):
            def norm(i, g, src, wait):
                if i >= 2:
                    act.wait_ge(S("centred"), centred_before(i, g) + 1)
                    src = ps[:, CENTRE[i], :]
                else:
                    wait()
                act.activation(sq[:, :], src, ACT.Square).then_inc(S("squared"), 1)
                if i:
                    root(i, g)

            def root(i, g):
                nth = norms_before(i, g)
                if i < 2:
                    act.wait_ge(S("guarded"), guarded_before(i, g) + 1)
                    act.activation(rs[:, :], rs[:, :], ACT.Ln).then_inc(S("log"), 1)
                else:
                    act.wait_ge(S("var"), nth + 1)
                    act.activation(rs[:, :], ps[:, MEAN[i], :], ACT.Ln, bias=LN_EPS[:, 0:1]).then_inc(S("log"), 1)
                act.wait_ge(S("log"), nth + 1)
                act.activation(rs[:, :], rs[:, :], ACT.Exp, scale=-0.5).then_inc(S("rsqrt"), 1)

            def pad(turn):
                for m in range(HALF):
                    act.wait_ge(S("proj"), turn * 4 + m + 1)
                    act.activation(xp[:, m, :, CONV - 1:], seqs(ps[:, m, :]), ACT.Copy).then_inc(S("x_padded"), 1)

            def mamba(l, g):
                turn = g * 2 + l
                for m in range(HALF):
                    act.wait_ge(S("proj"), turn * 4 + HALF + m + 1)
                    act.activation(sz[:, m, :], ps[:, HALF + m, :], ACT.Silu).then_inc(S("z_silu"), 1)
                for m in range(HALF):
                    act.wait_ge(S("conv"), turn * HALF + m + 1)
                    act.activation(u[:, m, :], cv[:, m, :], ACT.Silu,
                                   bias=W(f"conv_b{l}")[:, m:m + 1]).then_inc(S("u_ready"), 1)
                act.preload_act_table_set(LOG_EXP)
                act.wait_ge(S("xdbl"), turn * 2 + 1)
                act.activation(dtl[:, :], ps[0:RANK, 4, :], ACT.Copy).then_inc(S("dtl"), 1)
                act.wait_ge(S("u_ready"), turn * HALF + HALF)
                for m in range(HALF):
                    ins = act.activation(yacc[:, m, :], u[:, m, :], ACT.Copy, scale=W(f"d{l}")[:, m:m + 1])
                ins.then_inc(S("seeded"), 1)
                for m in range(HALF):
                    act.wait_ge(S("dt_mm"), turn * HALF + m + 1)
                    ins = act.activation(ab[:, m, :], ps[:, 6 + m, :], ACT.Abs, bias=W(f"dt_b{l}")[:, m:m + 1])
                ins.then_inc(S("abs_z"), 1)
                act.wait_ge(S("abs_z"), turn + 1)
                act.activation(ab, ab, ACT.Exp, scale=-1.0).then_inc(S("exp_z"), 1)
                act.preload_act_table_set("natural_log")
                act.wait_ge(S("one_plus"), turn + 1)
                act.activation(lb, u1, ACT.Ln).then_inc(S("ln_z"), 1)
                act.preload_act_table_set(LOG_EXP)
                act.wait_ge(S("delta"), turn + 1)
                def copy_b(n):
                    act.wait_ge(S("b_row"), turn * NS + n + 1)
                    if n >= 2:
                        act.wait_ge(S("dbu"), turn * NS + n - 1)
                    act.activation(b_sb[n % 2][:, :], ps[:, B_BANK[n % 2], :], ACT.Copy).then_inc(S("b_copied"), 1)

                copy_b(0)
                for n in range(NS):
                    if n + 1 < NS:
                        copy_b(n + 1)
                    if n >= 2:
                        act.wait_ge(S("scan"), turn * NS + n - 1)
                    for m in range(HALF):
                        ins = act.activation(dA[:, n % 2, m, :, 1:], seqs(dl[:, m, :])[:, :, 1:], ACT.Exp,
                                             scale=a_neg[:, l, m, n:n + 1])
                    ins.then_inc(S("decay"), 1)

            def experts(l, g, last=None):
                def copy_gates(e):
                    act.wait_ge(S(f"gate_spread{l}"), g * EXPERTS + e + 1)
                    if e >= 2 or last is not None:
                        act.wait_ge(S(f"weighted{l}"), g * EXPERTS + e - 1)
                    act.activation(gate_sb[:, e % 2, :], ps[:, 4 + e % 2, :],
                                   ACT.Copy).then_inc(S(f"gate_copied{l}"), 1)

                for i in range(EXPERTS * SLICES):
                    e, f = divmod(i, SLICES)
                    act.wait_ge(S(f"up{l}"), g * 32 + i + 1)
                    if i >= 4 or last is not None:
                        act.wait_ge(S(f"down{l}"), g * 32 + i - 3)
                    act.activation(gelu[:, i % 4, :], ps[:, i % 2, :], ACT.Gelu).then_inc(S(f"gelu{l}"), 1)
                    if i > 1 and f == 1:
                        copy_gates(e - 1)
                    if last is not None and i == 8:
                        act.wait_ge(S("centred"), centred_before(7, last) + 1)
                        act.activation(sq[:, :], ps[:, CENTRE[7], :], ACT.Square).then_inc(S("squared"), 1)
                    if last is not None and i == 12:
                        root(7, last)
                copy_gates(EXPERTS - 1)
                act.preload_act_table_set(LOG_EXP)

            def attend(a, g, keys, halves, scale):
                steps = SEQ * halves
                per = 4 // halves
                parts = {"x": (L, CTX), "f": (L,), "r": (CTX,)}[a]
                blocks = [(k, rows) for k in range(steps) for q in range(per) for rows in parts]
                per_step = per * len(parts)
                base = g * steps * per_step

                def exps(k, part):
                    act.wait_ge(S(f"shifted{a}"), (g * steps + k) * 2 + part + 1)
                    s = pr[:, k % 2, part * 2 * per * keys:(part + 1) * 2 * per * keys]
                    act.activation(s, s, ACT.Exp, scale=scale).then_inc(S(f"probs{a}"), 1)

                exps(0, 0)
                exps(0, 1)
                for b in range(len(blocks) + 2):
                    if b < len(blocks):
                        rows = blocks[b][1]
                        act.wait_ge(S(f"turn{a}"), base + b + 1)
                        if b >= 3:
                            act.wait_ge(S(f"product{a}"), base + b - 2)
                        act.activation(pt[0:rows, b % 3, :, :],
                                       ps[0:rows, 4 + b % 3, :].rearrange("p (a b) -> p a b", a=4),
                                       ACT.Copy).then_inc(S(f"turned{a}"), 1)
                    k, w = divmod(b, per_step)
                    if w == 1 and k % halves == 0 and k:
                        j = k // halves - 1
                        act.wait_ge(S(f"product{a}"), base + k * per_step)
                        if j >= 2:
                            act.wait_ge(S("head_done"), (g * 3 + PHASE[a]) * SEQ + j - 1)
                        act.activation(heads[:, j % 2, :], ps[:, 7, 0:2 * L], ACT.Copy).then_inc(S("heads"), 1)
                    if w == (3 if k < steps else 1) and k % halves == 0 and k:
                        j = k // halves - 1
                        nth = (g * 3 + PHASE[a]) * SEQ + j
                        act.wait_ge(S("heads"), nth + 1)
                        if j:
                            act.wait_ge(S("sums_inverse"), nth)
                        for quad in range(4):
                            top, bottom, cols = held(quad)
                            ins = act.activation(den[32 * quad:32 * quad + 32, :], heads[bottom, j % 2, cols], ACT.Copy)
                        ins.then_inc(S("sums"), 1)
                    if w in (1, 2) and k + 1 < steps:
                        exps(k + 1, w - 1)
                    if a == "r" and b == len(blocks) - 3:
                        norm(0, g + 1, x_in[:, :], lambda: act.wait_ge(S("x_in"), g * 16 + 32))

            act.preload_act_table_set(LOG_EXP)
            act.wait_ge(S("params_in"), 16)
            for l in range(2):
                act.activation(a_neg[:, l, :, :].rearrange("p h n -> p (h n)"), W(f"a_log{l}"), ACT.Exp).then_inc(S("a_exp"), 1)
            act.activation(tmp[:, 0:1], W("temp"), ACT.Abs).then_inc(S("temp"), 1)
            act.wait_ge(S("temp"), 1)
            act.activation(tmp[:, 1:2], tmp[:, 0:1], ACT.Exp, scale=-1.0).then_inc(S("temp"), 1)
            act.wait_ge(S("temp"), 2)
            act.activation(tmp[:, 2:3], tmp[:, 1:2], ACT.Ln, bias=W("ones")[:, 0:1]).then_inc(S("temp"), 1)
            act.wait_ge(S("vector_setup"), 1)
            norm(0, FIRST, x_in[:, :], lambda: act.wait_ge(S("x_in"), 16))
            root(0, FIRST)
            pad(0)
            with act.Fori(0, GROUPS) as g:
                mamba(0, g)
                norm(1, g, res[:, :], lambda: act.wait_ge(S("res1"), g + 1))
                act.wait_ge(S("gate_shift"), g + 1)
                act.activation(rl[:, 0:SEQ, 0:8], rl[:, 0:SEQ, 0:8], ACT.Exp).then_inc(S("gate_exp"), 1)
                experts(0, g)
                norm(2, g, None, None)
                act.wait_ge(S("q_mm_x"), g + 1)
                for i in range(4):
                    act.activation(qm[:, i, :], ps[:, 0, :], ACT.Identity, bias=bqm[:, i:i + 1],
                                   scale=W("head_mask")[:, i:i + 1]).then_inc(S("q_masked_x"), 1)
                attend("x", g, L + CTX, 2, DH ** -0.5)
                norm(3, g, None, None)
                act.wait_ge(S("q_mm_f"), g + 1)
                act.activation(qf[:, :], ps[:, 0, :], ACT.Identity, bias=W("fbq")).then_inc(S("q_biased"), 1)
                act.activation(sq[:, :], ps[:, 0, :], ACT.Square, bias=W("fbq")).then_inc(S("q_squared"), 1)
                act.wait_ge(S("q_norm"), g + 1)
                act.activation(rs[:, :], ps[:, 2, :], ACT.Ln).then_inc(S("q_log"), 1)
                act.wait_ge(S("q_log"), g + 1)
                act.activation(rs[:, :], rs[:, :], ACT.Exp, scale=-0.5).then_inc(S("q_rsqrt"), 1)
                attend("f", g, L, 1, DH ** -0.5)
                act.wait_ge(S("f_shift"), g + 1)
                act.activation(rl[:, 0:SEQ, :], rl[:, 0:SEQ, :], ACT.Exp).then_inc(S("f_exp"), 1)
                norm(4, g, None, None)
                pad(g * 2 + 1)
                mamba(1, g)
                norm(5, g, None, None)
                attend("r", g, CTX, 1, 1.0)
                root(0, g + 1)
                pad(g * 2 + 2)
                norm(6, g, None, None)
                act.wait_ge(S("n6"), g + 1)
            act.wait_ge(S("pick_shift"), 1)
            act.activation(r1[:, :], r1[:, :], ACT.Exp).then_inc(S("pick_exp"), 1)
            experts(1, 0)
            with act.Fori(1, GROUPS) as g:
                experts(1, g, last=g - 1)
            norm(7, GROUPS - 1, None, None)

        @block.vector
        def _(dve):
            def guard(i, g):
                dve.wait_ge(S("var"), norms_before(i, g) + 1)
                dve.tensor_scalar(rs[:, :], ps[:, MEAN[i], :], 1e-24 / D, None, ALU.max).then_inc(S("guarded"), 1)

            def norm(i, g, src, dst, ready):
                nth = norms_before(i, g)
                if i == 1:
                    guard(i, g)
                if i >= 2:
                    src = ps[:, CENTRE[i], :]
                dve.wait_ge(S("rsqrt"), nth + 1)
                dve.tensor_tensor(dst, src, rs[:, :], ALU.mult).then_inc(S(ready), 1)

            def split(rows, bank, c):
                src, hi, r = ps[0:rows, bank, :], bc_hi[0:rows, :], bc_r[0:rows, :]
                first = c.mark(dve.tensor_copy(hi, src))
                dve.tensor_copy(bcs[0:rows, :], src)
                c.wait(first)
                c.link(dve.tensor_tensor(r, src, hi, ALU.subtract))
                second = c.mark(dve.tensor_copy(hi, r))
                dve.tensor_copy(bcs[32:32 + rows, :], r)
                c.wait(second)
                return dve.tensor_tensor(bcs[64:64 + rows, :], r, hi, ALU.subtract)

            def convolve(l, turn, c):
                w = W(f"conv_w{l}")
                last = [None, None]
                for tap in range(CONV):
                    for m in range(HALF):
                        src = xp[:, m, :, tap:tap + L]
                        dst = seqs(cv[:, m, :])
                        coef = w[:, m * CONV + tap:m * CONV + tap + 1]
                        if tap == 0:
                            dve.wait_ge(S("x_padded"), turn * HALF + m + 1)
                            last[m] = c.mark(dve.tensor_scalar(dst, src, coef, None, ALU.mult))
                            continue
                        c.wait(last[m])
                        ins = dve.scalar_tensor_tensor(dst, src, coef, dst, ALU.mult, ALU.add)
                        if tap < CONV - 1:
                            last[m] = c.mark(ins)
                        else:
                            ins.then_inc(S("conv"), 1)

            def mamba(l, g, c):
                turn = g * 2 + l
                dve.wait_ge(S("xdbl"), turn * 2 + 2)
                split(2 * NS, 5, c).then_inc(S("bc_split"), 1)
                dve.wait_ge(S("abs_z"), turn + 1)
                for m in range(HALF):
                    c.mark(dve.tensor_scalar(rb[:, m, :], ps[:, 6 + m, :], W(f"dt_b{l}")[:, m:m + 1], 0.0,
                                                         ALU.add, ALU.max))
                dve.wait_ge(S("exp_z"), turn + 1)
                dve.tensor_scalar(u1, ab, 1.0, None, ALU.add).then_inc(S("one_plus"), 1)
                dve.wait_ge(S("one_plus"), turn + 1)
                c.link(dve.scalar_tensor_tensor(ab, u1, -1.0, ab, ALU.add, ALU.subtract))
                c.link(dve.tensor_tensor(rb, rb, ab, ALU.subtract))
                dve.wait_ge(S("ln_z"), turn + 1)
                dve.tensor_tensor(dl[:, :, :], rb, lb, ALU.add).then_inc(S("delta"), 1)
                dve.wait_ge(S("delta"), turn + 1)
                dve.wait_ge(S("u_ready"), turn * HALF + HALF)
                dve.tensor_tensor(dtu[:, :, :], dl[:, :, :], u[:, :, :], ALU.mult).then_inc(S("dtu"), 1)

                for n in range(NS):
                    dve.wait_ge(S("dbu"), turn * NS + n + 1)
                    dve.wait_ge(S("decay"), turn * NS + n + 1)
                    states = hs[:, n % 2, :, :].rearrange("p h t -> p (h t)")
                    dve.tensor_tensor_scan(states, dA[:, n % 2, :, :, :].rearrange("p h s t -> p (h s t)"),
                                           states, 0.0, ALU.mult, ALU.add).then_inc(S("scan"), 1)
                    dve.wait_ge(S("scan"), turn * NS + n + 1)
                    dve.wait_ge(S("c_row"), turn * NS + n + 1)
                    if n >= 2:
                        dve.wait_ge(S("summed"), turn * (NS + 1) + n)
                    b = C_BANK[n % 2]
                    dve.tensor_tensor(hc[:, n % 2, :, :], hs[:, n % 2, :, :],
                                      ps[:, b:b + 1, :].broadcast_to([128, HALF, TOK]), ALU.mult).then_inc(S("hc"), 1)
                dve.wait_ge(S("summed"), (turn + 1) * (NS + 1))
                dve.wait_ge(S("z_silu"), turn * HALF + HALF)
                dve.tensor_tensor(yacc[:, :, :], ps[:, 4:6, :], sz[:, :, :], ALU.mult).then_inc(S("gated"), 1)

            def experts(l, g, c, first, last=None):
                dve.wait_ge(S("gates_turned"), l * GROUPS + g + 1)
                split(EXPERTS, 6, c).then_inc(S("gates_split"), 1)
                for e in range(EXPERTS):
                    if last is not None and e == 0:
                        dve.wait_ge(S("centred"), centred_before(7, last) + 1)
                    if last is not None and e == 3:
                        last_norm(last)
                    dve.wait_ge(S(f"down{l}"), g * 32 + e * SLICES + SLICES)
                    dve.wait_ge(S(f"gate_copied{l}"), g * EXPERTS + e + 1)
                    dve.tensor_tensor(weighted, ps[:, 2 + e % 2, :], gate_sb[:, e % 2, :],
                                      ALU.mult).then_inc(S(f"weighted{l}"), 1)
                    dve.wait_ge(S(f"weighted{l}"), g * EXPERTS + e + 1)
                    ins = dve.tensor_tensor(res[:, :], weighted, first if e == 0 else res[:, :], ALU.add)
                    if e < EXPERTS - 1:
                        c.link(ins)
                    else:
                        ins.then_inc(S("res2" if l == 0 else "res7"), 1)

            def attend(a, g, keys, halves, c):
                steps = SEQ * halves
                per = 4 // halves
                width = 512 // per
                per_step = 4

                def shift(k, part):
                    nth = (g * steps + k) * 2 + part
                    n = 2 * per * keys
                    at = part * n
                    s = pr[:, k % 2, at:at + n].rearrange("p (q i t) -> p q i t", q=2, i=per)
                    s3 = pr[:, k % 2, at:at + n].rearrange("p (h t) -> p h t", t=keys)
                    src = ps[:, 2 * part:2 * part + 2, :].rearrange("p q (i t) -> p q i t", i=per)[:, :, :, 0:keys]
                    top = mx[:, part * 2 * per:(part + 1) * 2 * per]
                    dve.wait_ge(S(f"scores{a}"), nth + 1)
                    if k >= 2:
                        dve.wait_ge(S(f"turn{a}"), (g * steps + k - 2) * per_step + (part + 1) * per_step // 2)
                    if a == "r":
                        dve.tensor_tensor(s, src, mneg[:, :].unsqueeze(1).unsqueeze(1).broadcast_to([128, 2, per, keys]),
                                          ALU.add).then_inc(S(f"scores_read{a}"), 1)
                        dve.wait_ge(S(f"scores_read{a}"), nth + 1)
                        c.link(dve.tensor_reduce(top, s3, AX.X, ALU.max))
                        dve.tensor_tensor(s3, s3, top.unsqueeze(2).broadcast_to([128, 2 * per, keys]),
                                          ALU.subtract).then_inc(S(f"shifted{a}"), 1)
                    else:
                        c.link(dve.tensor_reduce(top.rearrange("p (q i) -> p q i", q=2), src, AX.X, ALU.max))
                        dve.tensor_tensor(s, src, top.rearrange("p (q i) -> p q i", q=2).unsqueeze(3)
                                          .broadcast_to([128, 2, per, keys]),
                                          ALU.subtract).then_inc(S(f"shifted{a}"), 1)

                for k in range(steps):
                    shift(k, 0)
                    shift(k, 1)
                    if k > halves and (k - 1) % halves == 0:
                        inverse(a, g, (k - 1) // halves - 1, c)
                for j in range((steps - 2) // halves, SEQ):
                    if a == "r" and j == SEQ - 1:
                        guard(0, g + 1)
                    inverse(a, g, j, c)

            def inverse(a, g, j, c):
                nth = (g * 3 + PHASE[a]) * SEQ + j
                dve.wait_ge(S("sums"), nth + 1)
                if j:
                    dve.wait_ge(S("head_done"), nth)
                dve.reciprocal(rec[:, :], den[:, :]).then_inc(S("sums_inverse"), 1)
                if j < POOL_HEADS:
                    return
                dve.wait_ge(S("sums_inverse"), nth + 1)
                now = slice(j * L, (j + 1) * L)
                if a == "r":
                    c.link(dve.tensor_tensor(rec[:, :], rec[:, :], keep_row[:, :], ALU.mult))
                for quad in range(4):
                    top, bottom, cols = held(quad)
                    rows = slice(32 * quad, 32 * quad + 32)
                    ins = dve.tensor_tensor(hT[rows, now], heads[top, j % 2, cols], rec[rows, :], ALU.mult)
                if a == "x":
                    c.link(ins)
                    ins = dve.tensor_tensor(res[:, now], hT[:, now], x1[:, now], ALU.add)
                ins.then_inc(S("head_done"), 1)
                dve.wait_ge(S("head_done"), nth + 1)

            def top_two(tiles, c, values):
                dve.memset(idle[:, :], 0.0)
                for t in range(tiles):
                    m = c.mark(dve.max(v8[:, t, :], values[:, t, :]))
                c.wait(m)
                dve.memset(idle[:, :], 0.0)
                for t in range(tiles):
                    m = c.mark(dve.max_index(i8[:, t, :], v8[:, t, :], values[:, t, :]))
                c.wait(m)
                c.link(dve.tensor_copy(f8[:, 0:tiles, :], i8[:, 0:tiles, :]))

            c = Chain(dve, S("dve_setup"))
            dve.memset(LN_EPS[:, :], 1e-5)
            dve.memset(xp[:, :, :, 0:CONV - 1], 0.0)
            dve.memset(dA[:, :, :, :, 0:1], 0.0)
            c.link(dve.memset(vp[:, :], 0.0))
            dve.memset(vp[:, VALUES_AT - 8:VALUES_AT], 1.0)
            dve.memset(vp_heads[:, :, :, :, 56:64].rearrange("p n s h c -> p (n s h) c"), 1.0)
            dve.wait_ge(S("params_in"), 16)
            dve.wait_ge(S("a_exp"), 2)
            dve.tensor_scalar(a_neg[:, :, :, :], a_neg[:, :, :, :], -1.0, None, ALU.mult)
            dve.tensor_scalar(bqm[:, :], W("head_mask"), W("xbq"), None, ALU.mult)
            dve.wait_ge(S("temp"), 3)
            c.link(dve.tensor_scalar(tmp[:, 3:4], W("temp"), 0.0, tmp[:, 2:3], ALU.max, ALU.add))
            dve.tensor_scalar(spm[:, :], W("head_mask"), tmp[:, 3:4], None, ALU.mult)
            dve.wait_ge(S("mask_in"), 16)
            c.link(dve.tensor_copy(mneg[:, :], mask8[:, :]))
            c.link(dve.tensor_reduce(keep[:, :], mneg[:, :], AX.X, ALU.min))
            dve.tensor_scalar(keep[:, :], keep[:, :], -1.0, 1.0, ALU.mult, ALU.add).then_inc(S("keep"), 1)
            dve.wait_ge(S("keep_spread"), 1)
            dve.tensor_copy(keep_row[:, :], ps[:, 7, 0:L])
            dve.tensor_scalar(mneg[:, :], mneg[:, :], NEG, None, ALU.mult).then_inc(S("vector_setup"), 1)
            dve.wait_ge(S("vector_setup"), 1)

            guard(0, FIRST)
            norm(0, FIRST, x_in[:, :], xn[:, :], "n0")
            convolve(0, 0, c)
            with dve.Fori(0, GROUPS) as g:
                c = Chain(dve, S("dve_order"), g * DVE_LINKS)
                mamba(0, g, c)
                dve.wait_ge(S("mamba_out"), g * 2 + 1)
                dve.tensor_tensor(res[:, :], ps[:, 4, :], xn[:, :], ALU.add).then_inc(S("res1"), 1)
                norm(1, g, res[:, :], xm[:, :], "n1")
                dve.wait_ge(S("logits0"), g + 1)
                lg = rl[:, 0:SEQ, 0:EXPERTS]
                src = ps[:, 6, 0:SEQ * EXPERTS].rearrange("p (s e) -> p s e", s=SEQ)
                c.link(dve.tensor_reduce(r1[:, 0:SEQ], src, AX.X, ALU.max))
                dve.tensor_tensor(lg, src, r1[:, 0:SEQ].unsqueeze(2).broadcast_to([128, SEQ, EXPERTS]),
                                  ALU.subtract).then_inc(S("gate_shift"), 1)
                dve.wait_ge(S("gate_exp"), g + 1)
                c.link(dve.tensor_reduce(r1[:, 0:SEQ], lg, AX.X, ALU.add))
                c.link(dve.reciprocal(r2[:, 0:SEQ], r1[:, 0:SEQ]))
                c.link(dve.tensor_tensor(t8[:, 0:SEQ, :], lg, r2[:, 0:SEQ].unsqueeze(2).broadcast_to([128, SEQ, EXPERTS]),
                                         ALU.mult))
                top_two(SEQ, c, t8)
                c.link(dve.tensor_tensor(r1[:, 0:SEQ], v8[:, 0:SEQ, 0], v8[:, 0:SEQ, 1], ALU.add))
                c.link(dve.reciprocal(r2[:, 0:SEQ], r1[:, 0:SEQ]))
                c.link(dve.tensor_tensor(v8[:, 0:SEQ, 0:2], v8[:, 0:SEQ, 0:2],
                                         r2[:, 0:SEQ].unsqueeze(2).broadcast_to([128, SEQ, 2]), ALU.mult))
                iota = W("iota").unsqueeze(1).broadcast_to([128, SEQ, EXPERTS])
                for k, dst in ((0, gt[:, :, :]), (1, t8[:, 0:SEQ, :])):
                    c.link(dve.tensor_tensor(dst, f8[:, 0:SEQ, k:k + 1].broadcast_to([128, SEQ, EXPERTS]), iota,
                                             ALU.is_equal))
                    c.link(dve.tensor_tensor(dst, dst, v8[:, 0:SEQ, k:k + 1].broadcast_to([128, SEQ, EXPERTS]),
                                             ALU.mult))
                dve.tensor_tensor(gt[:, :, :], gt[:, :, :], t8[:, 0:SEQ, :], ALU.add).then_inc(S("gates0"), 1)
                dve.tensor_scalar(qf[:, :], x_in[:, :], 2.0, None, ALU.mult).then_inc(S("x_used"), 1)
                dve.wait_ge(S("x_used"), g + 1)
                experts(0, g, c, qf[:, :])
                norm(2, g, None, x1[:, :], "n2")
                dve.wait_ge(S("rest_in"), 16)
                dve.wait_ge(S("k_mm_x"), g * 2 + 1)
                dve.tensor_scalar(kt[:, :, 0:L], seqs(ps[:, 1, :]), W("xbk"), None, ALU.add)
                dve.wait_ge(S("k_mm_x"), g * 2 + 2)
                dve.tensor_scalar(kt[:, :, L:L + CTX], ps[:, 2, 0:SEQ * CTX].rearrange("p (s t) -> p s t", s=SEQ),
                                  W("xbk"), None, ALU.add)

                def value(bank, rows, n, bias):
                    b = W(bias)[0:rows, :].rearrange("p (h d) -> p h d", d=DH)
                    for j in range(SEQ):
                        ins = dve.tensor_tensor(head_values(n, j, rows),
                                                ps[0:rows, bank, j * D:(j + 1) * D].rearrange("p (h d) -> p h d", d=DH),
                                                b, ALU.add)
                    return ins

                dve.wait_ge(S("v_mm_x"), g * 2 + 1)
                value(3, L, 0, "xbv")
                dve.wait_ge(S("v_mm_x"), g * 2 + 2)
                value(4, CTX, 1, "xbv").then_inc(S("qkv_x"), 1)

                attend("x", g, L + CTX, 2, c)
                norm(3, g, None, x2[:, :], "n3")

                dve.wait_ge(S("k_mm_f"), g + 1)
                dve.tensor_scalar(kt[:, :, 0:L], seqs(ps[:, 1, :]), W("fbk"), None, ALU.add)
                dve.wait_ge(S("v_mm_f"), g + 1)
                value(3, L, 0, "fbv")
                dve.wait_ge(S("q_rsqrt"), g + 1)
                c.link(dve.tensor_tensor(qt[:, :], qf[:, :], rs[:, :], ALU.mult))
                for i in range(4):
                    ins = dve.tensor_scalar(qm[:, i, :], qt[:, :], W("qe"), spm[:, i:i + 1], ALU.add, ALU.mult)
                ins.then_inc(S("qkv_f"), 1)

                attend("f", g, L, 1, c)
                dve.wait_ge(S("logits_f"), g + 1)
                lg = rl[:, 0:SEQ, :]
                c.link(dve.tensor_tensor(lg, ps[:, 6, 0:SEQ * 17].rearrange("p (s e) -> p s e", s=SEQ),
                                         W("fbrs").unsqueeze(1).broadcast_to([128, SEQ, 17]), ALU.add))
                c.mark(dve.tensor_reduce(r1[:, 0:SEQ], rl[:, 0:SEQ, 0:ROUTED], AX.X, ALU.max))
                c.link(dve.tensor_reduce(r2[:, 0:SEQ], rl[:, 0:SEQ, ROUTED:], AX.X, ALU.max))
                c.mark(dve.tensor_tensor(rl[:, 0:SEQ, 0:ROUTED], rl[:, 0:SEQ, 0:ROUTED],
                                         r1[:, 0:SEQ].unsqueeze(2).broadcast_to([128, SEQ, ROUTED]), ALU.subtract))
                dve.tensor_tensor(rl[:, 0:SEQ, ROUTED:], rl[:, 0:SEQ, ROUTED:],
                                  r2[:, 0:SEQ].unsqueeze(2).broadcast_to([128, SEQ, SHARED]),
                                  ALU.subtract).then_inc(S("f_shift"), 1)
                dve.wait_ge(S("f_exp"), g + 1)
                dve.memset(idle[:, :], 0.0)
                for j in range(SEQ):
                    c.mark(dve.max(v8[:, j, :], rl[:, j, 0:ROUTED]))
                c.mark(dve.tensor_reduce(r1[:, 0:SEQ], rl[:, 0:SEQ, 0:ROUTED], AX.X, ALU.add))
                c.link(dve.tensor_reduce(r2[:, 0:SEQ], rl[:, 0:SEQ, ROUTED:], AX.X, ALU.add))
                c.mark(dve.reciprocal(r1[:, SEQ:2 * SEQ], r1[:, 0:SEQ]))
                c.mark(dve.reciprocal(r2[:, SEQ:2 * SEQ], r2[:, 0:SEQ]))
                c.link(dve.tensor_reduce(r1[:, 2 * SEQ:3 * SEQ], v8[:, 0:SEQ, 0:3], AX.X, ALU.add))
                c.mark(dve.tensor_tensor(r1[:, 0:SEQ], r1[:, 2 * SEQ:3 * SEQ], r1[:, SEQ:2 * SEQ], ALU.mult))
                c.link(dve.tensor_tensor(rl[:, 0:SEQ, ROUTED:], rl[:, 0:SEQ, ROUTED:],
                                         r2[:, SEQ:2 * SEQ].unsqueeze(2).broadcast_to([128, SEQ, SHARED]), ALU.mult))
                w0, w1 = rl[:, 0:SEQ, ROUTED], rl[:, 0:SEQ, ROUTED + 1]
                c.mark(dve.tensor_tensor(r2[:, 0:SEQ], w0, w1, ALU.add))
                c.link(dve.scalar_tensor_tensor(r1[:, 0:SEQ], r1[:, 0:SEQ], 6.0, w1, ALU.mult, ALU.mult))
                c.link(dve.scalar_tensor_tensor(r2[:, 0:SEQ], r2[:, 0:SEQ], 2.0, w0, ALU.mult, ALU.mult))
                dve.tensor_tensor(r1[:, 0:SEQ], r1[:, 0:SEQ], r2[:, 0:SEQ], ALU.add).then_inc(S("gates_f"), 1)
                dve.wait_ge(S("gates_f_spread"), g + 1)
                dve.tensor_tensor(qt[:, :], hT[:, :], ps[:, 5, :], ALU.mult).then_inc(S("gated_f"), 1)
                dve.wait_ge(S("proj_f"), g + 1)
                dve.scalar_tensor_tensor(res[:, :], ps[:, 4, :], W("fbp"), x2[:, :], ALU.add,
                                         ALU.add).then_inc(S("res4"), 1)
                norm(4, g, None, x3[:, :], "n4")

                convolve(1, g * 2 + 1, c)
                mamba(1, g, c)
                dve.wait_ge(S("mamba_out"), g * 2 + 2)
                dve.tensor_tensor(res[:, :], ps[:, 4, :], x3[:, :], ALU.add).then_inc(S("res5"), 1)
                norm(5, g, None, x4[:, :], "n5")

                def rope(bank, n, bias, biass, a, b, dst):
                    src = ps[:, bank, 0:SEQ * n].rearrange("p (s t) -> p s t", s=SEQ)
                    swapped = ps[:, bank + 1, 0:SEQ * n].rearrange("p (s t) -> p s t", s=SEQ)
                    sin = W("rope_sin")[:, 0:n].unsqueeze(1).broadcast_to([128, SEQ, n])
                    cos = W("rope_cos")[:, 0:n].unsqueeze(1).broadcast_to([128, SEQ, n])
                    c.mark(dve.scalar_tensor_tensor(a, src, W(bias), sin, ALU.add, ALU.mult))
                    c.link(dve.scalar_tensor_tensor(b, swapped, W(biass), cos, ALU.add, ALU.mult))
                    c.link(dve.tensor_tensor(dst, a, b, ALU.subtract))

                dve.wait_ge(S("q_mm_r"), g + 1)
                rope(0, L, "rbq", "rbqs", seqs(qf[:, :]), seqs(qt[:, :]), seqs(qf[:, :]))
                for i in range(4):
                    dve.tensor_scalar(qm[:, i, :], qf[:, :], W("head_mask")[:, i:i + 1], None, ALU.mult)
                dve.wait_ge(S("k_mm_r"), g + 1)
                ka = qt[:, 0:SEQ * CTX].rearrange("p (s t) -> p s t", s=SEQ)
                kb = sq[:, 0:SEQ * CTX].rearrange("p (s t) -> p s t", s=SEQ)
                rope(2, CTX, "rbk", "rbks", ka, kb, kt[:, :, 0:CTX])
                dve.wait_ge(S("ctx_used"), g + 1)
                value(4, CTX, 1, "rbv").then_inc(S("qkv_r"), 1)
                attend("r", g, CTX, 1, c)
                norm(0, g + 1, x_in[:, :], xn[:, :], "n0")
                dve.wait_ge(S("proj_r"), g + 1)
                dve.scalar_tensor_tensor(res[:, :], ps[:, 4, :], W("rbo"), x4[:, :], ALU.add,
                                         ALU.add).then_inc(S("res6"), 1)
                convolve(0, g * 2 + 2, c)
                norm(6, g, None, x5[:, bass.ts(g, TOK)], "n6")
                dve.wait_ge(S("n6"), g + 1)
                assert c.n == DVE_LINKS, c.n

            c = Chain(dve, S("dve_rank"))
            dve.wait_ge(S("logits1"), 1)
            c.link(dve.tensor_copy(t8[:, :, :], ps[:, 6, 0:TILES * EXPERTS].rearrange("p (t e) -> p t e", e=EXPERTS)))
            top_two(TILES, c, t8)
            dve.tensor_tensor(r1[:, :], v8[:, :, 1], v8[:, :, 0], ALU.subtract).then_inc(S("pick_shift"), 1)
            iota = W("iota").unsqueeze(1).broadcast_to([128, TILES, EXPERTS])
            for k in range(2):
                ins = dve.tensor_tensor(oh[:, :, k, :].rearrange("p e t -> p t e"),
                                        f8[:, :, k:k + 1].broadcast_to([128, TILES, EXPERTS]), iota, ALU.is_equal)
            ins.then_inc(S("picked"), 1)
            dve.wait_ge(S("pick_exp"), 1)
            c.link(dve.tensor_scalar(r2[:, :], r1[:, :], 1.0, None, ALU.add))
            c.link(dve.reciprocal(v8[:, :, 0], r2[:, :]))
            c.link(dve.tensor_tensor(v8[:, :, 1], v8[:, :, 0], r1[:, :], ALU.mult))
            dve.wait_ge(S("counted"), 1)
            flat = lambda t: t[:, :, :, :].rearrange("p e k t -> p (e k t)")
            c.link(dve.tensor_tensor_scan(flat(tot), W("scan_keep"), ps[:, 5, 0:256], 0.0, ALU.mult, ALU.add))
            c.link(dve.tensor_tensor(flat(rank), flat(tot), ps[:, 5, 0:256], ALU.subtract))
            c.link(dve.tensor_tensor(flat(rank), flat(rank), ps[:, 4, 0:256], ALU.add))
            c.link(dve.scalar_tensor_tensor(flat(rank), flat(rank), float(CAPACITY), flat(oh), ALU.is_le, ALU.mult))
            for k, dst in ((0, gt_all), (1, t8)):
                done = c.mark(dve.tensor_tensor(dst[:, :, :], rank[:, :, k, :].rearrange("p e t -> p t e"),
                                                v8[:, :, k:k + 1].broadcast_to([128, TILES, EXPERTS]), ALU.mult))
            c.wait(done)
            dve.tensor_tensor(gt_all[:, :, :], gt_all[:, :, :], t8[:, :, :], ALU.add).then_inc(S("ranked"), 1)
            dve.wait_ge(S("ranked"), 1)

            def last_norm(g):
                dve.wait_ge(S("out_free"), g + 1)
                norm(7, g, None, yout[:, :], "out_ready")

            c = Chain(dve, S("dve_order2"))
            dve.tensor_copy(gt[:, :, :], gt_all[:, 0:SEQ, :]).then_inc(S("gates1"), 1)
            experts(1, 0, c, x5[:, 0:TOK])
            assert c.n == DVE_LINKS_2, c.n
            dve.wait_ge(S("res7"), 1)
            with dve.Fori(1, GROUPS) as g:
                c = Chain(dve, S("dve_order2"), g * DVE_LINKS_2)
                dve.tensor_copy(gt[:, :, :], gt_all[:, bass.ts(g, SEQ), :]).then_inc(S("gates1"), 1)
                experts(1, g, c, x5[:, bass.ts(g, TOK)], last=g - 1)
                dve.wait_ge(S("res7"), g + 1)
                assert c.n == DVE_LINKS_2, c.n
            last_norm(GROUPS - 1)


_ORDER = ["x_t", "ctx_t", "params", "selectors", "w_in", "w_out", "mask"]


def _shape_constants():
    p = np.arange(128)
    f = np.float32
    c = {}
    c["ident"] = np.eye(128, dtype=f)
    c["mean"] = np.full((128, 128), 1.0 / D, f)
    c["center"] = (np.eye(128) - 1.0 / D).astype(f)
    c["head_ones"] = (p[:, None] // DH == p[None, :] // DH).astype(f)
    c["before"] = (p[:, None] <= p[None, :]).astype(f)
    c["ones"] = np.ones((128, 128), f)
    c["head_mask"] = ((p[:, None] // DH) % 4 == np.arange(4)[None, :]).astype(f)
    c["iota"] = np.broadcast_to(np.arange(EXPERTS, dtype=f), (128, EXPERTS))
    inv = np.exp(np.arange(0, DH, 2, dtype=f) * f(-(4.0 * np.log(f(10.0))) / DH)).astype(f)
    angle = (np.arange(L, dtype=f)[None, :] * inv[(p % DH) // 2][:, None]).astype(f)
    sign = np.where(p % 2 == 0, 1.0, -1.0).astype(f)[:, None]
    c["rope_sin"] = np.sin(angle).astype(f) * sign
    c["rope_cos"] = np.cos(angle).astype(f)
    c["scan_keep"] = np.broadcast_to((np.arange(EXPERTS * 2 * TILES) % (2 * TILES) != 0).astype(f),
                                     (128, EXPERTS * 2 * TILES))
    sel = np.zeros((96, 2 * NS, 128), f)
    for j in range(2 * NS):
        sel[[j, 32 + j, 64 + j], j, :] = 1.0
    return c, sel


def kernel(**inputs):
    import ml_dtypes
    import concourse.bacc as _bacc
    from concourse import mybir as _mybir
    from concourse.bass_utils import run_bass_kernel_spmd as _run

    a = {k: np.asarray(v) for k, v in inputs.items()}
    v, sel = _shape_constants()

    def halves(m):
        m = m.reshape(HALF, 128, -1)
        return np.concatenate([m[0], m[1]], axis=1)

    def col(m):
        return m.reshape(128, 1)

    def rows(m):
        return np.broadcast_to(m.reshape(1, -1), (128, m.size))

    def low(m):
        return np.concatenate([m, np.zeros((128 - m.shape[0], m.shape[1]), m.dtype)])

    swap = np.arange(D) ^ 1
    v["in_w0"], v["in_w1"] = a["L0_attn_in_proj_w"].T, a["L1_attn_W_in"]
    v["x_w0"], v["x_w1"] = halves(a["L0_attn_x_proj_w"].T), halves(a["L1_attn_W_x"])
    v["dt_w0"], v["dt_w1"] = low(a["L0_attn_dt_proj_w"].T), low(a["L1_attn_W_dt"])
    v["out_w0"], v["out_w1"] = halves(a["L0_attn_out_proj_w"].T), halves(a["L1_attn_W_out"])
    v["conv_w0"], v["conv_w1"] = halves(a["L0_attn_conv_w"].reshape(DI, CONV)), halves(a["L1_attn_conv_w"].T)
    for n, k0, k1 in (("conv_b", "conv_b", "conv_b"), ("dt_b", "dt_proj_b", "b_dt"), ("a_log", "A_log", "A_log"),
                      ("d", "D", "D")):
        v[n + "0"] = halves(a["L0_attn_" + k0].reshape(DI, -1))
        v[n + "1"] = halves(a["L1_attn_" + k1].reshape(DI, -1))
    v["gate0"], v["gate1"] = a["L0_attn_gate_w"].T, a["L1_ffn_w_g"]
    for n, p in (("x", "L0_xattn_"), ("f", "L0_ffn_"), ("r", "L1_xattn_")):
        for m in "qkv":
            v[n + m] = a[p + "W" + m].T
        v[n + "bq"], v[n + "bk"], v[n + "bv"] = col(a[p + "bq"]), col(a[p + "bk"]), rows(a[p + "bv"])
    for m in "qk":
        v["r" + m + "s"] = a["L1_xattn_W" + m][swap].T
        v["rb" + m + "s"] = col(a["L1_xattn_b" + m][swap])
    v["fp"], v["fbp"] = a["L0_ffn_Wp"].T, col(a["L0_ffn_bp"])
    v["ro"], v["rbo"] = a["L1_xattn_Wo"].T, col(a["L1_xattn_bo"])
    v["frs"] = np.concatenate([a["L0_ffn_Wr"], a["L0_ffn_Ws"]]).T
    v["fbrs"] = rows(np.concatenate([a["L0_ffn_br"], a["L0_ffn_bs"]]))
    v["temp"] = col(np.repeat(a["L0_ffn_temperature"].reshape(HEADS), DH))
    v["qe"] = col(a["L0_ffn_query_embedding"])
    w_in = np.stack([a["L0_attn_w1"].transpose(2, 0, 1), a["L1_ffn_c_fc"].transpose(1, 0, 2)], axis=1)
    w_out = np.stack([a["L0_attn_w2"].transpose(2, 0, 1).reshape(SLICES, 128, EXPERTS, D).transpose(1, 2, 0, 3),
                      a["L1_ffn_c_proj"].reshape(EXPERTS, SLICES, 128, D).transpose(2, 0, 1, 3)], axis=1)
    arrays = {
        "x_t": a["x"].reshape(B * L, D).T,
        "ctx_t": a["ctx_1024"].reshape(B * CTX, D).T,
        "params": np.concatenate([v[n] for n, _ in PARAMS], axis=1),
        "selectors": sel.astype(ml_dtypes.bfloat16),
        "w_in": w_in,
        "w_out": w_out,
        "mask": a["mask_1x1xSxS2_bk1"].reshape(L, CTX),
    }
    arrays = {k: np.ascontiguousarray(m) for k, m in arrays.items()}
    nc = _bacc.Bacc("TRN2", target_bir_lowering=False, num_devices=1)
    args = [nc.dram_tensor(n, arrays[n].shape, _mybir.dt.from_np(arrays[n].dtype), kind="ExternalInput").ap()
            for n in _ORDER]
    args.append(nc.dram_tensor("out", (D, B * L), F32, kind="ExternalOutput").ap())
    decoder_kernel(nc, *args)
    r = _run(nc, [arrays], core_ids=[0])
    return np.ascontiguousarray(r.results[0]["out"].T).reshape(B, L, D)
```
